# Optimizing a Trainium2 kernel written in Bass

```python
import numpy as np
import jax
import jax.numpy as jnp

def _softmax(x, axis=-1):
    return jax.nn.softmax(x, axis=axis)

def _gelu(x):
    return jax.nn.gelu(x, approximate=True)

def _silu(x):
    return jax.nn.silu(x)

def _sigmoid(x):
    return jax.nn.sigmoid(x)

def _layernorm(x, axis=-1, eps=1e-05):
    m = jnp.mean(x, axis=axis, keepdims=True)
    v = jnp.var(x, axis=axis, keepdims=True)
    return (x - m) / jnp.sqrt(v + eps)

def _scatter_add(tgt, idx, src, axis=0):
    return tgt.at[idx].add(src)

def _segment_sum(src, seg, n):
    return jax.ops.segment_sum(src, seg, n)
kernel_name = 'mk_gnn_preln_d2_gnn_r32_4d8591'

def setup_inputs(seed: int=0):
    np.random.seed(seed)
    _w = jnp.asarray

    def _rec_inputs():
        import jax
        import jax.numpy as jnp
        _gk = jax.random.key(seed)
        x = -0.000202 + 1 * jax.random.normal(jax.random.fold_in(_gk, 1), (50000, 128), jnp.float32)
        src = jax.random.randint(jax.random.fold_in(_gk, 2), (50000,), 0, 50000, jnp.int32)
        dst = jnp.minimum((50000 * jax.random.uniform(jax.random.fold_in(_gk, 3), (50000,)) ** 2.0).astype(jnp.int32), 49999)
        _o = jnp.argsort(dst, stable=True)
        src = src[_o]
        dst = dst[_o]
        edge_type_130 = jax.random.randint(jax.random.fold_in(_gk, 13), (50000,), 0, 130, jnp.int32)
        edge_weight = jax.random.uniform(jax.random.fold_in(_gk, 14), (50000,), jnp.float32, 0.0, 0.999998)
        return (x, src, dst, edge_type_130, edge_weight)
    x, src, dst, edge_type_130, edge_weight = _rec_inputs()

    def _L0_gnn_setup():
        import jax, jax.numpy as jnp
        import numpy as np
        N = 50000
        E = 25000
        C = 128
        H = 4
        D = C // H
        HOPS = 3
        ODE_STEPS = 4

        def _spectral_norm(W, iters=5):
            u = jnp.ones((W.shape[0],), W.dtype) / jnp.sqrt(jnp.asarray(W.shape[0], W.dtype))
            for _ in range(iters):
                v = W.T @ u
                v = v / (jnp.linalg.norm(v) + 1e-12)
                u = W @ v
                u = u / (jnp.linalg.norm(u) + 1e-12)
            u = jax.lax.stop_gradient(u)
            v = jax.lax.stop_gradient(v)
            return W / (u @ W @ v)

        def _layer_norm(x, g, b, eps=1e-05):
            m = x.mean(-1, keepdims=True)
            var = ((x - m) ** 2).mean(-1, keepdims=True)
            return (x - m) * jax.lax.rsqrt(var + eps) * g + b

        def _gat(h, src, dst, W, a_src, a_dst, bias):
            g = (h @ W).reshape(N, H, D)
            es = jnp.einsum('nhd,hd->nh', g, a_src)
            ed = jnp.einsum('nhd,hd->nh', g, a_dst)
            e = jax.nn.leaky_relu(es[src] + ed[dst], 0.2)
            emax = jax.ops.segment_max(e, dst, num_segments=N)
            emax = jnp.where(jnp.isfinite(emax), emax, 0.0)
            ex = jnp.exp(e - emax[dst])
            den = jax.ops.segment_sum(ex, dst, num_segments=N)
            alpha = ex / (den[dst] + 1e-16)
            out = jax.ops.segment_sum(alpha[:, :, None] * g[src], dst, num_segments=N)
            return out.reshape(N, H * D) + bias
        key = jax.random.key(seed)
        k = jax.random.split(key, 16)
        rn = lambda kk, sh, s=0.05: jax.random.normal(kk, sh, jnp.float32) * s
        return {'x': jax.random.normal(k[0], (N, C), jnp.float32), 'edge_index': jax.random.randint(k[1], (2, E), 0, N), 'timestamps': jax.random.uniform(k[2], (E,), dtype=jnp.float32), 'W_in': rn(k[3], (C, C)), 'b_in': jnp.zeros((C,), jnp.float32), 'W1': rn(k[4], (C, H * D)), 'att1_src': rn(k[5], (H, D)), 'att1_dst': rn(k[6], (H, D)), 'bias1': jnp.zeros((H * D,), jnp.float32), 'W2': rn(k[7], (C, H * D)), 'att2_src': rn(k[8], (H, D)), 'att2_dst': rn(k[9], (H, D)), 'bias2': jnp.zeros((H * D,), jnp.float32), 'g1': jnp.ones((C,), jnp.float32), 'be1': jnp.zeros((C,), jnp.float32), 'g2': jnp.ones((C,), jnp.float32), 'be2': jnp.zeros((C,), jnp.float32), 'Wo1': rn(k[10], (C, C)), 'bo1': jnp.zeros((C,), jnp.float32), 'Wo2': rn(k[11], (C, C)), 'bo2': jnp.zeros((C,), jnp.float32), 'w_hop': rn(k[12], (C,)), 'W_out': rn(k[13], (C, C)), 'b_out': jnp.zeros((C,), jnp.float32)}
    _L0_gnn_all = _L0_gnn_setup()
    _L0_gnn_in = {k: v for k, v in _L0_gnn_all.items() if k in ('W_in', 'b_in', 'W1', 'att1_src', 'att1_dst', 'bias1', 'W2', 'att2_src', 'att2_dst', 'bias2', 'g1', 'be1', 'g2', 'be2', 'Wo1', 'bo1', 'Wo2', 'bo2', 'w_hop', 'W_out', 'b_out')}
    del _L0_gnn_all

    def _L1_gnn_setup():
        import jax, jax.numpy as jnp
        import numpy as np
        N_NODES = 50000
        N_EDGES = 25000
        H_DIM = 128
        N_REL2 = 130
        BN_EPS = 1e-05
        key = jax.random.key(seed)
        k1, k2, k3, k4, k5, k6 = jax.random.split(key, 6)
        xavier = float(np.sqrt(2.0 / (H_DIM + H_DIM)))
        return {'ent_emb': jax.random.normal(k1, (N_NODES, H_DIM), dtype=jnp.float32), 'rel_emb': jax.random.normal(k2, (N_REL2, H_DIM), dtype=jnp.float32), 'neigh_w': jax.random.normal(k3, (H_DIM, H_DIM), dtype=jnp.float32) * xavier, 'gamma': jnp.ones((H_DIM,), dtype=jnp.float32), 'beta': jnp.zeros((H_DIM,), dtype=jnp.float32), 'src': jax.random.randint(k4, (N_EDGES,), 0, N_NODES, dtype=jnp.int32), 'dst': jax.random.randint(k5, (N_EDGES,), 0, N_NODES, dtype=jnp.int32), 'rel_id': jax.random.randint(k6, (N_EDGES,), 0, N_REL2, dtype=jnp.int32)}
    _L1_gnn_all = _L1_gnn_setup()
    _L1_gnn_in = {k: v for k, v in _L1_gnn_all.items() if k in ('rel_emb', 'neigh_w', 'gamma', 'beta')}
    del _L1_gnn_all
    return {'x': x, 'src': src, 'dst': dst, 'edge_type_130': edge_type_130, 'edge_weight': edge_weight, 'L0_gnn_W_in': _L0_gnn_in['W_in'], 'L0_gnn_b_in': _L0_gnn_in['b_in'], 'L0_gnn_W1': _L0_gnn_in['W1'], 'L0_gnn_att1_src': _L0_gnn_in['att1_src'], 'L0_gnn_att1_dst': _L0_gnn_in['att1_dst'], 'L0_gnn_bias1': _L0_gnn_in['bias1'], 'L0_gnn_W2': _L0_gnn_in['W2'], 'L0_gnn_att2_src': _L0_gnn_in['att2_src'], 'L0_gnn_att2_dst': _L0_gnn_in['att2_dst'], 'L0_gnn_bias2': _L0_gnn_in['bias2'], 'L0_gnn_g1': _L0_gnn_in['g1'], 'L0_gnn_be1': _L0_gnn_in['be1'], 'L0_gnn_g2': _L0_gnn_in['g2'], 'L0_gnn_be2': _L0_gnn_in['be2'], 'L0_gnn_Wo1': _L0_gnn_in['Wo1'], 'L0_gnn_bo1': _L0_gnn_in['bo1'], 'L0_gnn_Wo2': _L0_gnn_in['Wo2'], 'L0_gnn_bo2': _L0_gnn_in['bo2'], 'L0_gnn_w_hop': _L0_gnn_in['w_hop'], 'L0_gnn_W_out': _L0_gnn_in['W_out'], 'L0_gnn_b_out': _L0_gnn_in['b_out'], 'L1_gnn_rel_emb': _L1_gnn_in['rel_emb'], 'L1_gnn_neigh_w': _L1_gnn_in['neigh_w'], 'L1_gnn_gamma': _L1_gnn_in['gamma'], 'L1_gnn_beta': _L1_gnn_in['beta']}

def reference(x, src, dst, edge_type_130, edge_weight, L0_gnn_W_in, L0_gnn_b_in, L0_gnn_W1, L0_gnn_att1_src, L0_gnn_att1_dst, L0_gnn_bias1, L0_gnn_W2, L0_gnn_att2_src, L0_gnn_att2_dst, L0_gnn_bias2, L0_gnn_g1, L0_gnn_be1, L0_gnn_g2, L0_gnn_be2, L0_gnn_Wo1, L0_gnn_bo1, L0_gnn_Wo2, L0_gnn_bo2, L0_gnn_w_hop, L0_gnn_W_out, L0_gnn_b_out, L1_gnn_rel_emb, L1_gnn_neigh_w, L1_gnn_gamma, L1_gnn_beta):
    import jax
    import jax.numpy as jnp

    def _L0_gnn_ref(x, edge_index, timestamps, W_in, b_in, W1, att1_src, att1_dst, bias1, W2, att2_src, att2_dst, bias2, g1, be1, g2, be2, Wo1, bo1, Wo2, bo2, w_hop, W_out, b_out):
        import jax, jax.numpy as jnp
        import numpy as np
        N = 50000
        E = 25000
        C = 128
        H = 4
        D = C // H
        HOPS = 3
        ODE_STEPS = 4

        def _spectral_norm(W, iters=5):
            u = jnp.ones((W.shape[0],), W.dtype) / jnp.sqrt(jnp.asarray(W.shape[0], W.dtype))
            for _ in range(iters):
                v = W.T @ u
                v = v / (jnp.linalg.norm(v) + 1e-12)
                u = W @ v
                u = u / (jnp.linalg.norm(u) + 1e-12)
            u = jax.lax.stop_gradient(u)
            v = jax.lax.stop_gradient(v)
            return W / (u @ W @ v)

        def _layer_norm(x, g, b, eps=1e-05):
            m = x.mean(-1, keepdims=True)
            var = ((x - m) ** 2).mean(-1, keepdims=True)
            return (x - m) * jax.lax.rsqrt(var + eps) * g + b

        def _gat(h, src, dst, W, a_src, a_dst, bias):
            g = (h @ W).reshape(N, H, D)
            es = jnp.einsum('nhd,hd->nh', g, a_src)
            ed = jnp.einsum('nhd,hd->nh', g, a_dst)
            e = jax.nn.leaky_relu(es[src] + ed[dst], 0.2)
            emax = jax.ops.segment_max(e, dst, num_segments=N)
            emax = jnp.where(jnp.isfinite(emax), emax, 0.0)
            ex = jnp.exp(e - emax[dst])
            den = jax.ops.segment_sum(ex, dst, num_segments=N)
            alpha = ex / (den[dst] + 1e-16)
            out = jax.ops.segment_sum(alpha[:, :, None] * g[src], dst, num_segments=N)
            return out.reshape(N, H * D) + bias
        src, dst = (edge_index[0], edge_index[1])
        loop = jnp.arange(N)
        src_sl = jnp.concatenate([src, loop])
        dst_sl = jnp.concatenate([dst, loop])
        h = jax.nn.gelu(x @ _spectral_norm(W_in) + b_in)
        h = _layer_norm(jax.nn.gelu(_gat(h, src_sl, dst_sl, W1, att1_src, att1_dst, bias1)), g1, be1)
        h = _layer_norm(jax.nn.gelu(_gat(h, src_sl, dst_sl, W2, att2_src, att2_dst, bias2)), g2, be2)
        Wa = _spectral_norm(Wo1)
        Wb = _spectral_norm(Wo2)
        f = lambda y: jnp.tanh(y @ Wa + bo1) @ Wb + bo2
        dt = 1.0 / ODE_STEPS

        def rk4_step(y, _):
            k1 = f(y)
            k2 = f(y + 0.5 * dt * k1)
            k3 = f(y + 0.5 * dt * k2)
            k4 = f(y + dt * k3)
            return (y + dt / 6.0 * (k1 + 2.0 * k2 + 2.0 * k3 + k4), None)
        h, _ = jax.lax.scan(rk4_step, h, None, length=ODE_STEPS)
        deg = jnp.maximum(jax.ops.segment_sum(jnp.ones_like(src, dtype=h.dtype), dst, num_segments=N), 1.0)
        hops = [h]
        cur = h
        for _ in range(HOPS):
            cur = jax.ops.segment_sum(cur[src], dst, num_segments=N) / deg[:, None]
            hops.append(cur)
        stack = jnp.stack(hops, axis=1)
        attn = jax.nn.softmax(stack @ w_hop, axis=1)
        agg = jnp.einsum('nkc,nk->nc', stack, attn)
        return agg @ _spectral_norm(W_out) + b_out

    def _L1_gnn_ref(ent_emb, rel_emb, neigh_w, gamma, beta, src, dst, rel_id):
        import jax, jax.numpy as jnp
        import numpy as np
        N_NODES = 50000
        N_EDGES = 25000
        H_DIM = 128
        N_REL2 = 130
        BN_EPS = 1e-05
        N = ent_emb.shape[0]
        comp = ent_emb[src] * rel_emb[rel_id]
        score = jnp.sum(comp * ent_emb[dst], axis=-1)
        seg_max = jax.ops.segment_max(score, dst, num_segments=N)
        ex = jnp.exp(score - seg_max[dst])
        denom = jax.ops.segment_sum(ex, dst, num_segments=N)
        alpha = ex / denom[dst]
        neigh = jax.ops.segment_sum(comp * alpha[:, None], dst, num_segments=N)
        h = neigh @ neigh_w
        mu = jnp.mean(h, axis=0)
        var = jnp.mean((h - mu) ** 2, axis=0)
        h = (h - mu) / jnp.sqrt(var + BN_EPS) * gamma + beta
        return jnp.tanh(h)
    edge_index = jnp.stack([src, dst])
    h = jnp.maximum(_layernorm(x, axis=-1), 0.0)
    x = x + _L0_gnn_ref(h, edge_index, edge_weight, L0_gnn_W_in, L0_gnn_b_in, L0_gnn_W1, L0_gnn_att1_src, L0_gnn_att1_dst, L0_gnn_bias1, L0_gnn_W2, L0_gnn_att2_src, L0_gnn_att2_dst, L0_gnn_bias2, L0_gnn_g1, L0_gnn_be1, L0_gnn_g2, L0_gnn_be2, L0_gnn_Wo1, L0_gnn_bo1, L0_gnn_Wo2, L0_gnn_bo2, L0_gnn_w_hop, L0_gnn_W_out, L0_gnn_b_out)
    h = jnp.maximum(_layernorm(x, axis=-1), 0.0)
    x = x + _L1_gnn_ref(h, L1_gnn_rel_emb, L1_gnn_neigh_w, L1_gnn_gamma, L1_gnn_beta, src, dst, edge_type_130)
    return x

_drawn_inputs = setup_inputs


def setup_inputs(seed=0):
    import zlib

    import numpy as np

    out = dict(_drawn_inputs(seed))
    spreads = {'L0_gnn_b_in': (0.0, 0.1),
     'L0_gnn_bias1': (0.0, 0.1),
     'L0_gnn_bias2': (0.0, 0.1),
     'L0_gnn_g1': (1.0, 0.2),
     'L0_gnn_be1': (0.0, 0.1),
     'L0_gnn_g2': (1.0, 0.2),
     'L0_gnn_be2': (0.0, 0.1),
     'L0_gnn_bo1': (0.0, 0.413),
     'L0_gnn_bo2': (0.0, 0.1),
     'L0_gnn_b_out': (0.0, 0.1),
     'L1_gnn_gamma': (1.0, 0.2),
     'L1_gnn_beta': (0.0, 0.1)}
    factors = {'L0_gnn_att1_src': 39.204,
     'L0_gnn_att1_dst': 64.0,
     'L0_gnn_att2_src': 40.745,
     'L0_gnn_att2_dst': 64.0}
    for name, (base, spread) in spreads.items():
        noise = np.random.default_rng([zlib.crc32(name.encode()), seed]).standard_normal(out[name].shape)
        drawn = base * np.exp(spread * noise) if base else spread * noise
        out[name] = jnp.asarray(drawn.astype(out[name].dtype))
    for name, factor in factors.items():
        out[name] = (out[name] * factor).astype(out[name].dtype)
    return out
```

```python
from contextlib import ExitStack

import numpy as np

import concourse.bass as bass
from concourse import mybir

F32 = mybir.dt.float32
I32 = mybir.dt.int32
ALU = mybir.AluOpType
ACT = mybir.ActivationFunctionType
AX = mybir.AxisListType

N = 50000
C = 128
H = 4
D = C // H
A = 4
POOL_SETUP = 14
SL = 3
G = 512
IT = 33
NP = IT * SL * G
EC = IT * SL * A
EP = 128 * EC
NULL = EP
GW = C + 2 * H
PW = C + 2 * H
HW = C + 1
CW = 3 * HW + 1
LW = C + 2
NR = 130
BIG = 1.0e30
EPS = 1.0e-5
ODE_STEPS = 4
DT = 1.0 / ODE_STEPS


class Steps:

    def __init__(self, eng, sem, i=None, per_iteration=0, base=0):
        self.eng, self.sem, self.i, self.per, self.base, self.n = eng, sem, i, per_iteration, base, 0

    def value(self):
        own = self.base + self.n
        return own if self.i is None or isinstance(self.i, int) and self.i == 0 else self.i * self.per + own

    def done(self, ins):
        ins.then_inc(self.sem, 1)
        self.n += 1

    def wait(self):
        self.eng.wait_ge(self.sem, self.value())

    def link(self, ins):
        self.done(ins)
        self.wait()


class Phase:

    def __init__(self, nc, tag):
        self.nc, self.tag, self.stack, self.used = nc, tag, ExitStack(), []

    def __enter__(self):
        return self

    def __exit__(self, *a):
        return self.stack.__exit__(*a)

    def sem(self, name):
        self.used.append(self.nc.alloc_semaphore(f"{self.tag}_{name}"))
        return self.used[-1]

    def clear(self):
        self.nc.clear_and_free_semaphores(self.used)
        self.nc.all_engine_barrier()

    def sems(self, name, n=SL):
        return [self.sem(f"{name}{s}") for s in range(n)]

    def sb(self, name, shape, dt=F32):
        return self.stack.enter_context(self.nc.sbuf_tensor(f"{self.tag}_{name}", shape, dt))

    def sbs(self, name, shape, dt=F32, n=SL):
        return [self.sb(f"{name}{s}", shape, dt) for s in range(n)]

    def ps(self, name):
        return self.stack.enter_context(self.nc.psum_tensor(f"{self.tag}_{name}", [128, 512], F32))

    def pss(self, name, n=SL):
        return [self.ps(f"{name}{s}") for s in range(n)]

    def block(self):
        self.stack.callback(self.clear)
        return self.stack.enter_context(self.nc.Block())


class Pace:

    def __init__(self, eng, sem):
        self.eng, self.sem = eng, sem

    def tick(self):
        self.eng.sem_inc(self.sem, 1)


def rounds(eng, body):
    body(0)
    with eng.Fori(1, IT) as i:
        body(i)


def col(v):
    return v.rearrange("(p a) -> p a", a=1)


def row(v):
    return v.rearrange("(a n) -> a n", a=1)



VECTORS = ("b_in", "g1", "be1", "g2", "be2", "bo1", "bo2", "gamma", "beta", "w_hop")
WEIGHTS = ("W_in", "Wo1", "Wo2", "W_out", "W1", "W2")


def setup(nc, t, d, r):
    with Phase(nc, "su") as ph:
        loaded = ph.sem("loaded")
        dst_in = ph.sem("dst_in")
        next_in = ph.sem("next_in")
        nd_set = ph.sem("nd_set")
        zeroed = ph.sem("zeroed")
        pool_step = ph.sem("pool_step")
        dve_step = ph.sem("dve_step")
        flags_ready = ph.sem("flags_ready")
        ends_ready = ph.sem("ends_ready")
        rows_done = ph.sem("rows_done")
        turned = ph.sem("turned")
        wt_ready = ph.sem("wt_ready")
        att_done = ph.sem("att_done")
        uv_ready = ph.sem("uv_ready")
        mv_done = ph.sem("mv_done")
        sq_ready = ph.sem("sq_ready")
        ss_done = ph.sem("ss_done")
        ss_ready = ph.sem("ss_ready")
        nrm_ready = ph.sem("nrm_ready")
        scaled = ph.sem("scaled")
        m_done = ph.sem("m_done")
        stored = ph.sem("stored")

        dsti = ph.sb("dsti", [128, EC], I32)
        dstf = ph.sb("dstf", [128, EC + 1])
        nd = ph.sb("nd", [128, 1], I32)
        isl = ph.sb("isl", [128, EC])
        ones_e = ph.sb("ones_e", [128, EC])
        real = ph.sb("real", [128, EC])
        sidf = ph.sb("sidf", [128, EC])
        sidx = ph.sb("sidx", [128, EC], I32)
        eidx = ph.sb("eidx", [128, EC], I32)
        nulli = ph.sb("nulli", [128, EC], I32)
        nrow = ph.sb("nrow", [1, PW + CW + LW])
        ut = ph.sb("ut", [128, 128])
        lt = ph.sb("lt", [128, 128])
        ones = ph.sb("ones", [128, 128])
        half = ph.sb("half", [128, 4])
        asd = [ph.sb(f"asd{l}", [128, 2 * H]) for l in range(2)]
        raw = ph.sb("raw", [128, 6, 128])
        wt = ph.sb("wt", [128, 6, 128])
        u = ph.sb("u", [128, 4])
        x = ph.sb("x", [128, 4])
        sq = ph.sb("sq", [128, 4])
        nrm = ph.sb("nrm", [128, 4])
        rn = ph.sb("rn", [128, 4])
        wbt = ph.sb("wbt", [128, 128])
        vec = ph.sb("vec", [128, 1])
        dfb = ph.sb("dfb", [128, 2, 128])
        pa = ph.ps("pa")
        pb = ph.ps("pb")
        pc = ph.ps("pc")
        block = ph.block()

        loads = [(raw[:, k, :], d[w]) for k, w in enumerate(WEIGHTS)]
        loads += [(r[k][:, :], col(d[k])) for k in VECTORS]
        loads += [(r[k + "_all"][:, :], row(d[k]).broadcast_to([128, C])) for k in ("bias1", "bias2")]
        loads += [(r["b_out_row"][:, :], row(d["b_out"])), (r["neigh_w"][:, :], d["neigh_w"]),
                  (r["rel_a"][:, :], d["rel_emb"][0:128, :]), (r["rel_b"][:, :], d["rel_emb"][128:NR, :])]
        for l in range(2):
            for k, base in ((f"att{l + 1}_src", 0), (f"att{l + 1}_dst", H)):
                for h in range(H):
                    loads.append((asd[l][h * D:(h + 1) * D, base + h:base + h + 1],
                                  d[k][h:h + 1, :].rearrange("a n -> n a")))

        @block.sync
        def _(sp):
            sp.dma_start(dsti[:, :], d["dst"]).then_inc(dst_in, 16)
            sp.wait_ge(nd_set, 1)
            sp.dma_start(nd[0:127, :], d["dst"][1:128, 0:1]).then_inc(next_in, 16)
            sp.wait_ge(zeroed, 5)
            for o, i_ in loads:
                sp.dma_start(o, i_).then_inc(loaded, 16)
            sp.dma_start(t["last_edge"][0:NP, :].rearrange("(p e) a -> p (e a)", p=128), nulli[:, :]).then_inc(stored, 16)
            for name, lo, w in (("pg", 0, PW), ("pc", PW, CW), ("p1", PW, HW + 1), ("p2", PW, HW + 1), ("pl", PW + CW, LW)):
                sp.dma_start(t[name][NULL:NULL + 1, :], nrow[:, lo:lo + w]).then_inc(stored, 16)
            sp.wait_ge(flags_ready, 1)
            sp.dma_start(t["sidx"], sidx[:, :]).then_inc(stored, 16)
            sp.dma_start(t["eidx"], eidx[:, :]).then_inc(stored, 16)
            sp.wait_ge(stored, 16 * 8)

        @block.gpsimd
        def _(pool):
            st = Steps(pool, pool_step)
            nc.gpsimd.memset(nd[:, :], -1).then_inc(nd_set, 1)
            nc.gpsimd.memset(asd[0][:, :], 0.0).then_inc(zeroed, 1)
            nc.gpsimd.memset(asd[1][:, :], 0.0).then_inc(zeroed, 1)
            nc.gpsimd.memset(nulli[:, :], NULL).then_inc(zeroed, 1)
            st.link(nc.gpsimd.memset(nrow[:, :], 0.0))
            nc.gpsimd.memset(nrow[:, C + H:PW], -BIG).then_inc(zeroed, 1)
            nc.gpsimd.memset(nrow[:, PW + CW + C:PW + CW + C + 1], 1.0).then_inc(zeroed, 1)
            st.link(nc.gpsimd.memset(r["ident"][:, :], 0.0))
            st.link(nc.gpsimd.affine_select(out=r["ident"][:, :], in_=r["ident"][:, :], compare_op=ALU.not_equal,
                                            fill=1.0, base=0, pattern=[[-1, 128]], channel_multiplier=1))
            st.done(nc.gpsimd.memset(ones[:, :], 1.0))
            st.done(nc.gpsimd.memset(half[:, :], 0.5))
            st.done(nc.gpsimd.memset(ones_e[:, :], 1.0))
            st.done(nc.gpsimd.memset(r["mhalf"][:, :], -0.5))
            st.done(nc.gpsimd.iota(eidx[:, :], pattern=[[1, EC]], base=0, channel_multiplier=EC))
            st.done(nc.gpsimd.iota(r["pid"][:, :], pattern=[[1, 1]], base=0, channel_multiplier=1))
            st.done(nc.gpsimd.iota(r["low"][:, :], pattern=[[1, 1]], base=0, channel_multiplier=EC))
            st.done(nc.gpsimd.iota(r["spare"][:, :], pattern=[[1, 1]], base=EP + 1, channel_multiplier=1))
            st.link(nc.gpsimd.memset(r["ones_row"][:, :], 1.0))
            st.link(nc.gpsimd.affine_select(out=ut[:, :], in_=ones[:, :], compare_op=ALU.is_gt, fill=0.0,
                                            base=0, pattern=[[1, 128]], channel_multiplier=-1))
            st.link(nc.gpsimd.affine_select(out=lt[:, :], in_=ones[:, :], compare_op=ALU.is_gt, fill=0.0,
                                            base=0, pattern=[[-1, 128]], channel_multiplier=1))
            assert st.n == POOL_SETUP
            for k in range(10):
                pool.wait_ge(ss_ready, k + 1)
                nc.gpsimd.tensor_tensor(out=nrm[:, :], in0=sq[:, :], in1=half[:, :], op=ALU.pow).then_inc(nrm_ready, 1)

        @block.tensor
        def _(pe):
            ident = r["ident"]
            pe.wait_ge(pool_step, POOL_SETUP)
            pe.wait_ge(loaded, 16 * len(loads))
            for k in range(6):
                o = pa[:, k * 128:(k + 1) * 128] if k < 4 else pb[:, (k - 4) * 128:(k - 3) * 128]
                last = nc.tensor.transpose(o, raw[:, k, :], ident[:, :])
            last.then_inc(turned, 1)
            pe.wait_ge(wt_ready, 2)
            for l in range(2):
                last = nc.tensor.matmul(pb[:, 8 * l:8 * l + 8], wt[:, 4 + l, :], asd[l][:, :], start=True, stop=True)
            last.then_inc(att_done, 1)
            pe.wait_ge(ends_ready, 2)
            for k in range(2):
                last = nc.tensor.matmul(pc[:, k * 128:(k + 1) * 128], dfb[:, k, :], ident[:, :], start=True, stop=True)
            last.then_inc(rows_done, 1)
            for h in range(10):
                pe.wait_ge(uv_ready, h + 1)
                for m in range(4):
                    w = raw if h % 2 == 0 else wt
                    last = nc.tensor.matmul(pa[:, m:m + 1], w[:, m, :], u[:, m:m + 1], start=True, stop=True)
                last.then_inc(mv_done, 1)
                pe.wait_ge(sq_ready, h + 1)
                nc.tensor.matmul(pa[:, 8:12], ones[:, :], sq[:, :], start=True, stop=True).then_inc(ss_done, 1)
            pe.wait_ge(sq_ready, 11)
            nc.tensor.matmul(pa[:, 8:12], ones[:, :], sq[:, :], start=True, stop=True).then_inc(ss_done, 1)
            pe.wait_ge(scaled, 5)
            nc.tensor.matmul(pa[:, 0:128], wbt[:, :], r["Wa"][:, :], start=True, stop=True)
            nc.tensor.matmul(pa[:, 128:129], r["Wa"][:, :], r["bo2"][:, :], start=True, stop=True).then_inc(m_done, 1)

        @block.vector
        def _(dve):
            st = Steps(dve, dve_step)
            v_ = nc.vector
            dve.wait_ge(dst_in, 16)
            dve.wait_ge(next_in, 16)
            dve.wait_ge(pool_step, POOL_SETUP)
            st.link(v_.tensor_copy(dstf[:, 0:EC], dsti[:, :]))
            st.link(v_.tensor_copy(dstf[:, EC:EC + 1], nd[:, :]))
            st.link(v_.tensor_tensor(isl[:, :], dstf[:, 0:EC], dstf[:, 1:EC + 1], ALU.not_equal))
            st.link(v_.tensor_scalar(real[:, :], dstf[:, 0:EC], float(N), None, ALU.is_lt))
            st.link(v_.tensor_tensor(isl[:, :], isl[:, :], real[:, :], ALU.mult))
            st.link(v_.tensor_copy(sidf[:, :], eidx[:, :]))
            st.link(v_.tensor_scalar(sidf[:, :], sidf[:, :], float(NP), None, ALU.add))
            st.link(v_.tensor_tensor(real[:, :], dstf[:, 0:EC], sidf[:, :], ALU.subtract))
            st.link(v_.tensor_tensor(real[:, :], real[:, :], isl[:, :], ALU.mult))
            st.link(v_.tensor_tensor(sidf[:, :], sidf[:, :], real[:, :], ALU.add))
            v_.tensor_copy(sidx[:, :], sidf[:, :]).then_inc(flags_ready, 1)
            same, fresh = r["same"], r["fresh"]
            st.link(v_.tensor_tensor(same[:, 1:EC], dstf[:, 1:EC], dstf[:, 0:EC - 1], ALU.is_equal))
            st.link(v_.memset(same[:, 0:1], 0.0))
            st.link(v_.tensor_scalar(fresh[:, :], same[:, :], -1.0, BIG, ALU.add, ALU.mult))
            st.link(v_.tensor_tensor_scan(r["cnt"][:, :], same[:, :], ones_e[:, :], 0.0, ALU.mult, ALU.add))
            st.link(v_.tensor_copy(r["dfirst"][:, :], dsti[:, 0:1]))
            v_.tensor_copy(dfb[:, 0, :], dstf[:, 0:1].broadcast_to([128, 128])).then_inc(ends_ready, 1)
            v_.tensor_copy(dfb[:, 1, :], dstf[:, EC - 1:EC].broadcast_to([128, 128])).then_inc(ends_ready, 1)

            dve.wait_ge(turned, 1)
            v_.tensor_copy(wt[:, 0:4, :], pa[:, :].rearrange("p (k n) -> p k n", k=4)).then_inc(wt_ready, 1)
            v_.tensor_copy(wt[:, 4:6, :], pb[:, 0:256].rearrange("p (k n) -> p k n", k=2)).then_inc(wt_ready, 1)
            dve.wait_ge(att_done, 1)
            for l in range(2):
                st.link(v_.tensor_copy(r[f"W{l + 1}e"][:, 0:C], raw[:, 4 + l, :]))
                st.link(v_.tensor_copy(r[f"W{l + 1}e"][:, C:GW], pb[:, 8 * l:8 * l + 8]))
            st.link(v_.tensor_copy(r["pidf"][:, 0:1], r["pid"][:, :]))
            st.link(v_.tensor_scalar(r["pidf"][:, 1:2], r["pidf"][:, 0:1], 128.0, None, ALU.add))
            dve.wait_ge(rows_done, 1)
            st.link(v_.scalar_tensor_tensor(r["carry"][:, :], pc[:, 0:128], dstf[:, EC - 1:EC], ut[:, :],
                                            ALU.is_equal, ALU.mult))
            st.link(v_.scalar_tensor_tensor(r["carry_mask"][:, :], pc[:, 128:256], dstf[:, 0:1], lt[:, :],
                                            ALU.is_equal, ALU.mult))
            st.link(v_.reduce_max(r["chained"][:, :], r["carry_mask"][:, :], AX.X))
            st.link(v_.tensor_scalar(r["carry_mask"][:, :], r["carry_mask"][:, :], -1.0, BIG, ALU.add, ALU.mult))
            v_.memset(u[:, :], float(1.0 / np.sqrt(np.float32(C)))).then_inc(uv_ready, 1)
            for h in range(10):
                dve.wait_ge(mv_done, h + 1)
                st.link(v_.tensor_copy(x[:, :], pa[:, 0:4]))
                v_.tensor_tensor(sq[:, :], x[:, :], x[:, :], ALU.mult).then_inc(sq_ready, 1)
                dve.wait_ge(ss_done, h + 1)
                v_.tensor_copy(sq[:, :], pa[:, 8:12]).then_inc(ss_ready, 1)
                dve.wait_ge(nrm_ready, h + 1)
                st.link(v_.tensor_scalar(nrm[:, :], nrm[:, :], 1e-12, None, ALU.add))
                st.link(v_.reciprocal(rn[:, :], nrm[:, :]))
                v_.tensor_tensor(u[:, :], x[:, :], rn[:, :], ALU.mult).then_inc(uv_ready, 1)
            dve.wait_ge(uv_ready, 11)
            v_.tensor_tensor(sq[:, :], u[:, :], x[:, :], ALU.mult).then_inc(sq_ready, 1)
            dve.wait_ge(ss_done, 11)
            st.link(v_.reciprocal(rn[:, :], pa[:, 8:12]))
            for o, src, m in ((r["W_in"], raw[:, 0, :], 0), (r["Wa"], raw[:, 1, :], 1), (r["Wb"], raw[:, 2, :], 2),
                              (wbt, wt[:, 2, :], 2), (r["W_out"], raw[:, 3, :], 3)):
                v_.tensor_scalar(o[:, :], src, rn[:, m:m + 1], None, ALU.mult).then_inc(scaled, 1)
            dve.wait_ge(m_done, 1)
            st.link(v_.tensor_copy(r["WbWa"][:, :], pa[:, 0:128]))
            st.link(v_.tensor_copy(vec[:, :], pa[:, 128:129]))
            for k in range(2 * ODE_STEPS + 1):
                st.link(v_.scalar_tensor_tensor(r["tanh_bias"][:, k:k + 1], vec[:, :], k * DT / 2, r["bo1"][:, :],
                                                ALU.mult, ALU.add))
            st.link(v_.tensor_tensor(r["be2_bo2"][:, :], r["be2"][:, :], r["bo2"][:, :], ALU.add))



def value(eng, v):
    return v if isinstance(v, int) else eng.snap(v)


def node_rows(ap, i, s):
    v = ap.rearrange("(g p a) c -> g p (a c)", p=128, a=A)
    g = i * SL + s
    return v[g] if isinstance(g, int) else v[bass.ds(g, 1)].rearrange("o p f -> (o p) f")


def edge_columns(ap, i, s):
    j = (i * SL + s) * A
    return ap[:, j:j + A] if isinstance(j, int) else ap[:, bass.ds(j, A)]


def edge_rows(ap, i, s, lo=0, hi=None):
    v = ap[0:EP, :].rearrange("(p j) c -> p j c", p=128)
    hi = ap.shape[1] if hi is None else hi
    j = (i * SL + s) * A
    return v[:, j:j + A, lo:hi] if isinstance(j, int) else v[:, bass.ds(j, A), lo:hi]


def at(ap):
    return bass.IndirectOffsetOnAxis(ap=ap, axis=0)


def over(v, n):
    return v.unsqueeze(3).broadcast_to(list(v.shape) + [n])


def layer_norm_stats(nc, st, pace, rows, stats, mv, var, var_ready):
    for a in range(A):
        last = nc.vector.bn_stats(stats[:, a, :], rows[:, a, :])
    st.link(last)
    pace.tick()
    for a in range(A):
        last = nc.vector.bn_aggr(mv[:, a, :], stats[:, a, :])
    st.link(last)
    nc.vector.tensor_scalar(var[:, :], mv[:, :, 1], EPS, None, ALU.add).then_inc(var_ready, 1)


def normalize(nc, out, rows, mv, rstd):
    for a in range(A):
        last = nc.vector.tensor_scalar(out[:, a, :], rows[:, a, :], mv[:, a, 0:1], rstd[:, a:a + 1],
                                       ALU.subtract, ALU.mult)
    return last


def node_in(nc, t, d, r):
    with Phase(nc, "ni") as ph:
        x_in = ph.sems("x_in")
        idx_in = ph.sems("idx_in")
        scattered = ph.sems("scattered")
        step = ph.sem("dve_step")
        var_ready = ph.sems("var_ready")
        rstd_ready = ph.sems("rstd_ready")
        xn_ready = ph.sems("xn_ready")
        turned = ph.sems("turned")
        relu_done = ph.sems("relu_done")
        h_done = ph.sems("h_done")
        gelu_done = ph.sems("gelu_done")
        g_done = ph.sems("g_done")
        g_part = ph.sems("g_part")
        g_ready = ph.sems("g_ready")
        stored = ph.sems("stored")

        x = ph.sbs("x", [128, A, C])
        xn = ph.sbs("xn", [128, A, C])
        stats = ph.sbs("stats", [128, A, 6])
        mv = ph.sbs("mv", [128, A, 2])
        var = ph.sbs("var", [128, A])
        rstd = ph.sbs("rstd", [128, A])
        xt = ph.sbs("xt", [128, G])
        ht = ph.sbs("ht", [128, G])
        g = ph.sbs("g", [128, A, GW])
        ed = ph.sbs("ed", [128, A, H])
        sidx = ph.sbs("sidx", [128, A], I32)
        eidx = ph.sbs("eidx", [128, A], I32)
        pt = ph.pss("pt")
        pg = ph.pss("pg")
        block = ph.block()
        K = 3 * SL

        @block.sync
        def _(sp):
            def loads(i, first=False):
                seen = None if first else value(sp, i)
                seen_s = None if first else value(sp, i * 64)
                src = [node_rows(d["x"], i, s) for s in range(SL)]
                for s in range(SL):
                    if not first:
                        sp.wait_ge(xn_ready[s], seen)
                    sp.dma_start(x[s][:, :, :].rearrange("p a c -> p (a c)"), src[s]).then_inc(x_in[s], 16)
                    if not first:
                        sp.wait_ge(scattered[s], seen_s)
                    sp.dma_start(sidx[s][:, :], edge_columns(t["sidx"], i, s)).then_inc(idx_in[s], 16)
                    sp.dma_start(eidx[s][:, :], edge_columns(t["eidx"], i, s)).then_inc(idx_in[s], 16)

            loads(0, True)
            with sp.Fori(1, IT) as i:
                loads(i)

        @block.gpsimd
        def _(pool):
            pace = Pace(pool, ph.sem("pool_pace"))

            def body(i):
                for s in range(SL):
                    pool.wait_ge(var_ready[s], i + 1)
                    nc.gpsimd.tensor_tensor(out=rstd[s][:, :], in0=var[s][:, :], in1=r["mhalf"][:, :],
                                            op=ALU.pow).then_inc(rstd_ready[s], 1)
                    pool.wait_ge(idx_in[s], i * 32 + 32)
                    pace.tick()
                    for a in range(A):
                        nc.gpsimd.indirect_dma_start(out=t["last_edge"], out_offset=at(sidx[s][:, a:a + 1]),
                                                     in_=eidx[s][:, a:a + 1], in_offset=None).then_inc(scattered[s], 16)

            rounds(pool, body)
            for s in range(SL):
                pool.wait_ge(scattered[s], IT * 64)

        @block.vector
        def _(dve):
            pace = Pace(dve, ph.sem("dve_pace"))

            def body(i):
                st = Steps(dve, step, i, K)
                for s in range(SL):
                    dve.wait_ge(x_in[s], i * 16 + 16)
                    layer_norm_stats(nc, st, pace, x[s], stats[s], mv[s], var[s], var_ready[s])
                for s in range(SL):
                    dve.wait_ge(rstd_ready[s], i + 1)
                    normalize(nc, xn[s], x[s], mv[s], rstd[s]).then_inc(xn_ready[s], 1)
                for s in range(SL):
                    dve.wait_ge(g_done[s], i + 1)
                    if not isinstance(i, int):
                        dve.wait_ge(stored[s], i * 32)
                    st.done(nc.vector.tensor_copy(g[s][:, 0:3, :], pg[s][:, 0:3 * GW].rearrange("p (a c) -> p a c", a=3)))
                    dve.wait_ge(g_part[s], i + 1)
                    st.wait()
                    nc.vector.tensor_copy(ed[s][:, :, :], g[s][:, :, C + H:GW]).then_inc(g_ready[s], 1)
                assert st.n == K, st.n

            rounds(dve, body)

        @block.tensor
        def _(pe):
            def body(i):
                for s in range(SL):
                    pe.wait_ge(xn_ready[s], i + 1)
                    if not isinstance(i, int):
                        pe.wait_ge(g_part[s], i)
                    for a in range(A):
                        last = nc.tensor.transpose(pt[s][:, a * 128:(a + 1) * 128], xn[s][:, a, :], r["ident"][:, :])
                    last.then_inc(turned[s], 1)
                for s in range(SL):
                    pe.wait_ge(relu_done[s], i + 1)
                    nc.tensor.matmul(pt[s][:, :], r["W_in"][:, :], xt[s][:, :], start=True, stop=True).then_inc(h_done[s], 1)
                for s in range(SL):
                    pe.wait_ge(gelu_done[s], i + 1)
                    if not isinstance(i, int):
                        pe.wait_ge(g_ready[s], i)
                    for a in range(A):
                        o = pg[s][:, a * GW:(a + 1) * GW] if a < 3 else pt[s][:, 0:GW]
                        last = nc.tensor.matmul(o, ht[s][:, a * 128:(a + 1) * 128], r["W1e"][:, :], start=True, stop=True)
                    last.then_inc(g_done[s], 1)

            rounds(pe, body)

        @block.scalar
        def _(act):
            def body(i):
                for s in range(SL):
                    act.wait_ge(turned[s], i + 1)
                    nc.scalar.activation(xt[s][:, :], pt[s][:, :], ACT.Relu).then_inc(relu_done[s], 1)
                for s in range(SL):
                    act.wait_ge(h_done[s], i + 1)
                    nc.scalar.activation(ht[s][:, :], pt[s][:, :], ACT.Gelu_apprx_tanh,
                                         bias=r["b_in"][:, 0:1]).then_inc(gelu_done[s], 1)
                for s in range(SL):
                    act.wait_ge(g_done[s], i + 1)
                    if not isinstance(i, int):
                        act.wait_ge(stored[s], i * 32)
                    nc.scalar.activation(g[s][:, 3, :], pt[s][:, 0:GW], ACT.Copy).then_inc(g_part[s], 1)
                for s in range(SL):
                    act.wait_ge(g_ready[s], i + 1)
                    act.dma_start(node_rows(t["g"], i, s), g[s][:, :, :].rearrange("p a c -> p (a c)")).then_inc(stored[s], 16)
                    act.dma_start(node_rows(t["ed"], i, s), ed[s][:, :, :].rearrange("p a c -> p (a c)")).then_inc(stored[s], 16)

            rounds(act, body)
            for s in range(SL):
                act.wait_ge(stored[s], IT * 32)


def fix_index(nc, t, d, r):
    with Phase(nc, "fi") as ph:
        got = ph.sem("got")
        step = ph.sem("dve_step")
        lasti = ph.sb("lasti", [128, 1], I32)
        f = [ph.sb(f"f{k}", [128, 1]) for k in range(6)]
        block = ph.block()

        @block.gpsimd
        def _(pool):
            nc.gpsimd.indirect_dma_start(out=lasti[:, :], out_offset=None, in_=t["last_edge"][0:NP, :],
                                         in_offset=at(r["dfirst"][:, :])).then_inc(got, 16)

        @block.vector
        def _(dve):
            st = Steps(dve, step)
            v_ = nc.vector
            dve.wait_ge(got, 16)
            last, low, ok, a, b, c = (x[:, :] for x in f)
            st.link(v_.tensor_copy(last, lasti[:, :]))
            st.link(v_.tensor_copy(low, r["low"][:, :]))
            st.link(v_.tensor_tensor(ok, last, low, ALU.is_ge))
            st.link(v_.tensor_scalar(a, low, float(EC), None, ALU.add))
            st.link(v_.tensor_tensor(a, last, a, ALU.is_lt))
            st.link(v_.tensor_tensor(ok, ok, a, ALU.mult))
            st.link(v_.tensor_tensor(ok, ok, r["chained"][:, :], ALU.mult))
            st.link(v_.tensor_scalar(b, last, -float(NULL), None, ALU.add))
            st.link(v_.tensor_tensor(b, b, ok, ALU.mult))
            st.link(v_.tensor_scalar(b, b, float(NULL), None, ALU.add))
            st.link(v_.tensor_copy(r["fix_get"][:, :], b))
            st.link(v_.tensor_copy(c, r["spare"][:, :]))
            st.link(v_.tensor_tensor(b, last, c, ALU.subtract))
            st.link(v_.tensor_tensor(b, b, ok, ALU.mult))
            st.link(v_.tensor_tensor(b, b, c, ALU.add))
            st.link(v_.tensor_copy(r["fix_put"][:, :], b))


def gat_edges(nc, t, d, r, tag, g_name, ed_name):
    with Phase(nc, tag) as ph:
        idx_in = ph.sems("idx_in")
        rows_in = ph.sems("rows_in")
        step = ph.sem("dve_step")
        start = ph.sem("start")
        arg_ready = ph.sems("arg_ready")
        exp_done = ph.sems("exp_done")
        row_ready = ph.sems("row_ready")
        stored = ph.sems("stored")

        srci = ph.sbs("srci", [128, A], I32)
        dsti = ph.sbs("dsti", [128, A], I32)
        rows = ph.sbs("rows", [128, A, GW])
        edst = ph.sbs("edst", [128, A, H])
        e = ph.sbs("e", [128, A, H])
        base = ph.sbs("base", [128, A, H])
        arg = ph.sbs("arg", [128, 2, A, H])
        wts = ph.sbs("wts", [128, 2, A, H])
        gw = ph.sbs("gw", [128, A, C])
        tmp = ph.sb("tmp", [128, C])
        out = ph.sbs("out", [128, A, PW])
        block = ph.block()
        K = SL * 18

        @block.sync
        def _(sp):
            def load(i, s, js=None):
                sp.dma_start(srci[s][:, :], edge_columns(d["src"], i, s)).then_inc(idx_in[s], 16)
                sp.dma_start(dsti[s][:, :], edge_columns(d["dst"], i, s)).then_inc(idx_in[s], 16)

            def store(i, s):
                sp.dma_start(edge_rows(t["pg"], i, s), out[s][:, :, :]).then_inc(stored[s], 16)

            for s in range(SL):
                load(0, s)
            with sp.Fori(0, IT - 1) as i:
                ready = sp.snap(i + 1)
                for s in range(SL):
                    sp.wait_ge(row_ready[s], ready)
                    load(i + 1, s)
                    store(i, s)
            for s in range(SL):
                sp.wait_ge(row_ready[s], IT)
                store(IT - 1, s)
            for s in range(SL):
                sp.wait_ge(stored[s], IT * 16)

        @block.gpsimd
        def _(pool):
            pace = Pace(pool, ph.sem("pool_pace"))

            def body(i):
                for s in range(SL):
                    if not isinstance(i, int):
                        pool.wait_ge(row_ready[s], i)
                    pool.wait_ge(idx_in[s], i * 32 + 32)
                    pace.tick()
                    for a in range(A):
                        nc.gpsimd.indirect_dma_start(out=rows[s][:, a, :], out_offset=None, in_=t[g_name],
                                                     in_offset=at(srci[s][:, a:a + 1])).then_inc(rows_in[s], 16)
                    for a in range(A):
                        nc.gpsimd.indirect_dma_start(out=edst[s][:, a, :], out_offset=None, in_=t[ed_name],
                                                     in_offset=at(dsti[s][:, a:a + 1])).then_inc(rows_in[s], 16)

            rounds(pool, body)

        @block.scalar
        def _(act):
            def body(i):
                for s in range(SL):
                    act.wait_ge(arg_ready[s], i + 1)
                    nc.scalar.activation(wts[s][:, :, :, :], arg[s][:, :, :, :], ACT.Exp).then_inc(exp_done[s], 1)

            rounds(act, body)

        @block.vector
        def _(dve):
            v_ = nc.vector
            before = out[SL - 1]
            v_.memset(before[:, A - 1, 0:C + H], 0.0).then_inc(start, 1)
            v_.memset(before[:, A - 1, C + H:PW], -BIG).then_inc(start, 1)
            dve.wait_ge(start, 2)

            def body(i):
                st = Steps(dve, step, i, K)
                for s in range(SL):
                    o, prev = out[s], out[(s - 1) % SL][:, A - 1, :]
                    m = o[:, :, C + H:PW]
                    fresh = edge_columns(r["fresh"], i, s)
                    dve.wait_ge(rows_in[s], i * 128 + 128)
                    if not isinstance(i, int):
                        dve.wait_ge(stored[s], i * 16)
                    st.link(v_.tensor_tensor(e[s][:, :, :], rows[s][:, :, C:C + H], edst[s][:, :, :], ALU.add))
                    st.link(v_.scalar_tensor_tensor(e[s][:, :, :], e[s][:, :, :], 0.2, e[s][:, :, :], ALU.mult, ALU.max))
                    for h in range(H):
                        last = v_.tensor_tensor_scan(m[:, :, h], fresh, e[s][:, :, h], prev[:, C + H + h:C + H + h + 1],
                                                     ALU.add, ALU.max)
                    st.link(last)
                    st.done(v_.tensor_tensor(base[s][:, 0:1, :], prev[:, C + H:PW].unsqueeze(1),
                                             fresh[:, 0:1].unsqueeze(2).broadcast_to([128, 1, H]), ALU.add))
                    st.link(v_.tensor_tensor(base[s][:, 1:A, :], m[:, 0:A - 1, :],
                                             fresh[:, 1:A].unsqueeze(2).broadcast_to([128, A - 1, H]), ALU.add))
                    st.done(v_.tensor_tensor(arg[s][:, 0, :, :], base[s][:, :, :], m, ALU.subtract))
                    v_.tensor_tensor(arg[s][:, 1, :, :], e[s][:, :, :], m, ALU.subtract).then_inc(arg_ready[s], 1)
                    dve.wait_ge(exp_done[s], i + 1)
                    keep, w = wts[s][:, 0, :, :], wts[s][:, 1, :, :]
                    for h in range(H):
                        st.done(v_.tensor_tensor_scan(o[:, :, C + h], keep[:, :, h], w[:, :, h], prev[:, C + h:C + h + 1],
                                                      ALU.mult, ALU.add))
                    st.link(v_.tensor_tensor(gw[s][:, :, :].rearrange("p a (h d) -> p a h d", h=H),
                                             rows[s][:, :, 0:C].rearrange("p a (h d) -> p a h d", h=H),
                                             over(w, D), ALU.mult))
                    for a in range(A):
                        was = prev[:, 0:C] if a == 0 else o[:, a - 1, 0:C]
                        st.link(v_.tensor_tensor(tmp[:, :].rearrange("p (h d) -> p h d", h=H),
                                                 was.rearrange("p (h d) -> p h d", h=H),
                                                 keep[:, a, :].unsqueeze(2).broadcast_to([128, H, D]), ALU.mult))
                        ins = v_.tensor_tensor(o[:, a, 0:C], tmp[:, :], gw[s][:, a, :], ALU.add)
                        if a < A - 1:
                            st.link(ins)
                        else:
                            ins.then_inc(row_ready[s], 1)
                            dve.wait_ge(row_ready[s], i + 1)
                assert st.n == K, st.n

            rounds(dve, body)
            st = Steps(dve, start, base=2)
            st.link(v_.tensor_copy(r["tail"][:, 0:PW], out[SL - 1][:, A - 1, :]))


def softmax_fix(nc, t, d, r, tag, name, heads, width):
    per = C // heads
    sums, tops = C, C + heads
    with Phase(nc, tag) as ph:
        step = ph.sem("dve_step")
        spread = ph.sem("spread")
        tops_done = ph.sem("tops_done")
        arg_ready = ph.sem("arg_ready")
        exp_done = ph.sem("exp_done")
        w_ready = ph.sem("w_ready")
        cin_done = ph.sem("cin_done")
        got = ph.sem("got")
        fixed = ph.sem("fixed")
        put = ph.sem("put")
        mb = ph.sb("mb", [128, heads, 128])
        masked = ph.sb("masked", [128, 128])
        mc = ph.sb("mc", [128, heads])
        arg = ph.sb("arg", [128, heads, 128])
        w = ph.sb("w", [128, heads, 128])
        old = ph.sb("old", [128, width])
        arg2 = ph.sb("arg2", [128, 2, heads])
        f = ph.sb("f", [128, 2, heads])
        t1 = ph.sb("t1", [128, C])
        t2 = ph.sb("t2", [128, C])
        pm = ph.ps("pm")
        pq = ph.ps("pq")
        pc = ph.ps("pc")
        block = ph.block()
        tail = r["tail"]

        @block.gpsimd
        def _(pool):
            nc.gpsimd.indirect_dma_start(out=old[:, :], out_offset=None, in_=t[name][0:EP + 1, :],
                                         in_offset=at(r["fix_get"][:, :])).then_inc(got, 16)
            pool.wait_ge(fixed, 1)
            nc.gpsimd.indirect_dma_start(out=t[name], out_offset=at(r["fix_put"][:, :]), in_=old[:, :],
                                         in_offset=None).then_inc(put, 16)
            pool.wait_ge(put, 16)

        @block.tensor
        def _(pe):
            for k, p in ((0, pm), (1, pq)):
                pe.wait_ge(spread, heads * (k + 1))
                for h in range(heads):
                    last = nc.tensor.matmul(p[:, h * 128:(h + 1) * 128], mb[:, h, :], r["ident"][:, :], start=True, stop=True)
                last.then_inc(tops_done, 1)
            pe.wait_ge(w_ready, heads)
            for h in range(heads):
                nc.tensor.matmul(pc[:, h * per:(h + 1) * per], w[:, h, :], tail[:, h * per:(h + 1) * per], start=True, stop=True)
                last = nc.tensor.matmul(pc[:, C + h:C + h + 1], w[:, h, :], tail[:, sums + h:sums + h + 1], start=True, stop=True)
            last.then_inc(cin_done, 1)

        @block.scalar
        def _(act):
            act.wait_ge(arg_ready, heads)
            nc.scalar.activation(w[:, :, :], arg[:, :, :], ACT.Exp).then_inc(exp_done, 1)
            act.wait_ge(arg_ready, heads + 2)
            nc.scalar.activation(f[:, :, :], arg2[:, :, :], ACT.Exp).then_inc(exp_done, 1)

        @block.vector
        def _(dve):
            st = Steps(dve, step)
            v_ = nc.vector
            for h in range(heads):
                v_.tensor_copy(mb[:, h, :], tail[:, tops + h:tops + h + 1].broadcast_to([128, 128])).then_inc(spread, 1)
            dve.wait_ge(tops_done, 1)
            for h in range(heads):
                st.link(v_.tensor_tensor(masked[:, :], pm[:, h * 128:(h + 1) * 128], r["carry_mask"][:, :], ALU.add))
                st.link(v_.reduce_max(mc[:, h:h + 1], masked[:, :], AX.X))
            for h in range(heads):
                v_.tensor_copy(mb[:, h, :], mc[:, h:h + 1].broadcast_to([128, 128])).then_inc(spread, 1)
            dve.wait_ge(tops_done, 2)
            for h in range(heads):
                st.link(v_.tensor_scalar(arg[:, h, :], pq[:, h * 128:(h + 1) * 128], tail[:, tops + h:tops + h + 1], -1.0,
                                         ALU.subtract, ALU.mult))
                v_.tensor_scalar(arg[:, h, :], arg[:, h, :], 0.0, None, ALU.min).then_inc(arg_ready, 1)
            dve.wait_ge(exp_done, 1)
            for h in range(heads):
                v_.tensor_tensor(w[:, h, :], w[:, h, :], r["carry"][:, :], ALU.mult).then_inc(w_ready, 1)
            dve.wait_ge(got, 16)
            om = old[:, tops:tops + heads]
            st.link(v_.tensor_tensor(t1[:, 0:heads], om, mc[:, :], ALU.max))
            v_.tensor_tensor(arg2[:, 0, :], om, t1[:, 0:heads], ALU.subtract).then_inc(arg_ready, 1)
            v_.tensor_tensor(arg2[:, 1, :], mc[:, :], t1[:, 0:heads], ALU.subtract).then_inc(arg_ready, 1)
            dve.wait_ge(arg_ready, heads + 2)
            st.link(v_.tensor_copy(om, t1[:, 0:heads]))
            dve.wait_ge(exp_done, 2)
            dve.wait_ge(cin_done, 1)
            for lo, n in ((0, C), (sums, heads)):
                k = n // heads
                f0, f1 = (f[:, q, :].unsqueeze(2).broadcast_to([128, heads, k]) for q in (0, 1))

                def cut(v):
                    return v.rearrange("p (h k) -> p h k", h=heads)

                st.link(v_.tensor_tensor(cut(t1[:, 0:n]), cut(old[:, lo:lo + n]), f0, ALU.mult))
                st.link(v_.tensor_tensor(cut(t2[:, 0:n]), cut(pc[:, lo:lo + n]), f1, ALU.mult))
                ins = v_.tensor_tensor(old[:, lo:lo + n], t1[:, 0:n], t2[:, 0:n], ALU.add)
                if lo == 0:
                    st.link(ins)
                else:
                    ins.then_inc(fixed, 1)


def gat_args(nc, st, near, own, sc, arg, arg_ready):
    v_ = nc.vector
    top = near[:, :, C + H:PW]
    st.link(v_.tensor_tensor(sc[:, 0, :, :], own[:, :, C:C + H], own[:, :, C + H:GW], ALU.add))
    st.link(v_.scalar_tensor_tensor(sc[:, 0, :, :], sc[:, 0, :, :], 0.2, sc[:, 0, :, :], ALU.mult, ALU.max))
    st.link(v_.tensor_tensor(sc[:, 1, :, :], top, sc[:, 0, :, :], ALU.max))
    st.done(v_.tensor_tensor(arg[:, 0, :, :], top, sc[:, 1, :, :], ALU.subtract))
    v_.tensor_tensor(arg[:, 1, :, :], sc[:, 0, :, :], sc[:, 1, :, :], ALU.subtract).then_inc(arg_ready, 1)


def gat_mix(nc, st, near, own, sc, f, bias, mixed):
    v_ = nc.vector
    st.link(v_.tensor_tensor(sc[:, 2, :, :], near[:, :, C:C + H], f[:, 0, :, :], ALU.mult))
    st.link(v_.tensor_tensor(sc[:, 2, :, :], sc[:, 2, :, :], f[:, 1, :, :], ALU.add))
    st.link(v_.tensor_scalar(sc[:, 2, :, :], sc[:, 2, :, :], 1e-16, None, ALU.add))
    st.link(v_.reciprocal(sc[:, 3, :, :], sc[:, 2, :, :]))
    st.done(v_.tensor_tensor(sc[:, 4, :, :], f[:, 0, :, :], sc[:, 3, :, :], ALU.mult))
    st.link(v_.tensor_tensor(sc[:, 5, :, :], f[:, 1, :, :], sc[:, 3, :, :], ALU.mult))

    def heads(v):
        return v[:, :, 0:C].rearrange("p a (h d) -> p a h d", h=H)

    st.done(v_.tensor_tensor(heads(near), heads(near), over(sc[:, 4, :, :], D), ALU.mult))
    st.link(v_.tensor_tensor(heads(own), heads(own), over(sc[:, 5, :, :], D), ALU.mult))
    st.link(v_.tensor_tensor(near[:, :, 0:C], near[:, :, 0:C], own[:, :, 0:C], ALU.add))
    v_.tensor_tensor(near[:, :, 0:C], near[:, :, 0:C], bias[:, :].unsqueeze(1).broadcast_to([128, A, C]),
                     ALU.add).then_inc(mixed, 1)


def gather_rows(nc, out, src, idx, arrived):
    for a in range(A):
        nc.gpsimd.indirect_dma_start(out=out[:, a, :], out_offset=None, in_=src, in_offset=at(idx[:, a:a + 1])).then_inc(arrived, 16)


def gat_nodes(nc, t, d, r):
    with Phase(nc, "gn") as ph:
        own_in = ph.sems("own_in")
        idx_in = ph.sems("idx_in")
        near_in = ph.sems("near_in")
        step = ph.sem("dve_step")
        arg_ready = ph.sems("arg_ready")
        exp_done = ph.sems("exp_done")
        mixed = ph.sems("mixed")
        gelu_done = ph.sems("gelu_done")
        var_ready = ph.sems("var_ready")
        rstd_ready = ph.sems("rstd_ready")
        xn_ready = ph.sems("xn_ready")
        turned = ph.sems("turned")
        ht_ready = ph.sems("ht_ready")
        g_done = ph.sems("g_done")
        g_part = ph.sems("g_part")
        g_ready = ph.sems("g_ready")
        stored = ph.sems("stored")

        own = ph.sbs("own", [128, A, GW])
        near = ph.sbs("near", [128, A, PW])
        idx = ph.sbs("idx", [128, A], I32)
        sc = ph.sbs("sc", [128, 6, A, H])
        arg = ph.sbs("arg", [128, 2, A, H])
        f = ph.sbs("f", [128, 2, A, H])
        y = ph.sbs("y", [128, A, C])
        stats = ph.sbs("stats", [128, A, 6])
        mv = ph.sbs("mv", [128, A, 2])
        var = ph.sbs("var", [128, A])
        rstd = ph.sbs("rstd", [128, A])
        ht = ph.sbs("ht", [128, G])
        g = ph.sbs("g", [128, A, GW])
        ed = ph.sbs("ed", [128, A, H])
        pt = ph.pss("pt")
        pg = ph.pss("pg")
        dve_pace = ph.sem("dve_pace")
        pool_pace = ph.sem("pool_pace")
        block = ph.block()
        K = 16 * SL

        @block.sync
        def _(sp):
            def load(i, s):
                sp.dma_start(idx[s][:, :], node_rows(t["last_edge"][0:NP, :], i, s)).then_inc(idx_in[s], 16)
                sp.dma_start(own[s][:, :, :].rearrange("p a c -> p (a c)"), node_rows(t["g"], i, s)).then_inc(own_in[s], 16)

            for s in range(SL):
                load(0, s)
            with sp.Fori(0, IT - 1) as i:
                done = sp.snap(i + 1)
                for s in range(SL):
                    sp.wait_ge(mixed[s], done)
                    load(i + 1, s)

        @block.gpsimd
        def _(pool):
            pace = Pace(pool, pool_pace)

            def root(i, s):
                pool.wait_ge(var_ready[s], i + 1)
                nc.gpsimd.tensor_tensor(out=rstd[s][:, :], in0=var[s][:, :], in1=r["mhalf"][:, :],
                                        op=ALU.pow).then_inc(rstd_ready[s], 1)

            for s in range(SL):
                pool.wait_ge(idx_in[s], 16)
                gather_rows(nc, near[s], t["pg"][0:EP + 1, :], idx[s], near_in[s])
            with pool.Fori(0, IT - 1) as i:
                for s in range(SL):
                    root(i, s)
                    pool.wait_ge(idx_in[s], i * 16 + 32)
                    pool.wait_ge(gelu_done[s], i + 1)
                    pace.tick()
                    gather_rows(nc, near[s], t["pg"][0:EP + 1, :], idx[s], near_in[s])
            for s in range(SL):
                root(IT - 1, s)

        @block.vector
        def _(dve):
            pace = Pace(dve, dve_pace)

            def body(i):
                st = Steps(dve, step, i, K)
                for s in range(SL):
                    dve.wait_ge(own_in[s], i * 16 + 16)
                    dve.wait_ge(near_in[s], i * 64 + 64)
                    gat_args(nc, st, near[s], own[s], sc[s], arg[s], arg_ready[s])
                for s in range(SL):
                    dve.wait_ge(exp_done[s], i + 1)
                    gat_mix(nc, st, near[s], own[s], sc[s], f[s], r["bias1_all"], mixed[s])
                for s in range(SL):
                    dve.wait_ge(gelu_done[s], i + 1)
                    layer_norm_stats(nc, st, pace, y[s], stats[s], mv[s], var[s], var_ready[s])
                for s in range(SL):
                    dve.wait_ge(rstd_ready[s], i + 1)
                    normalize(nc, y[s], y[s], mv[s], rstd[s]).then_inc(xn_ready[s], 1)
                for s in range(SL):
                    dve.wait_ge(g_done[s], i + 1)
                    if not isinstance(i, int):
                        dve.wait_ge(stored[s], i * 32)
                    st.done(nc.vector.tensor_copy(g[s][:, 0:3, :], pg[s][:, 0:3 * GW].rearrange("p (a c) -> p a c", a=3)))
                    dve.wait_ge(g_part[s], i + 1)
                    st.wait()
                    nc.vector.tensor_copy(ed[s][:, :, :], g[s][:, :, C + H:GW]).then_inc(g_ready[s], 1)
                assert st.n == K, st.n

            rounds(dve, body)

        @block.tensor
        def _(pe):
            def body(i):
                for s in range(SL):
                    pe.wait_ge(xn_ready[s], i + 1)
                    if not isinstance(i, int):
                        pe.wait_ge(g_part[s], i)
                    for a in range(A):
                        last = nc.tensor.transpose(pt[s][:, a * 128:(a + 1) * 128], y[s][:, a, :], r["ident"][:, :])
                    last.then_inc(turned[s], 1)
                for s in range(SL):
                    pe.wait_ge(ht_ready[s], i + 1)
                    if not isinstance(i, int):
                        pe.wait_ge(g_ready[s], i)
                    for a in range(A):
                        o = pg[s][:, a * GW:(a + 1) * GW] if a < 3 else pt[s][:, 0:GW]
                        last = nc.tensor.matmul(o, ht[s][:, a * 128:(a + 1) * 128], r["W2e"][:, :], start=True, stop=True)
                    last.then_inc(g_done[s], 1)

            rounds(pe, body)

        @block.scalar
        def _(act):
            def body(i):
                for s in range(SL):
                    act.wait_ge(arg_ready[s], i + 1)
                    nc.scalar.activation(f[s][:, :, :, :], arg[s][:, :, :, :], ACT.Exp).then_inc(exp_done[s], 1)
                for s in range(SL):
                    act.wait_ge(mixed[s], i + 1)
                    if not isinstance(i, int):
                        act.wait_ge(turned[s], i)
                    nc.scalar.activation(y[s][:, :, :], near[s][:, :, 0:C], ACT.Gelu_apprx_tanh).then_inc(gelu_done[s], 1)
                for s in range(SL):
                    act.wait_ge(turned[s], i + 1)
                    nc.scalar.activation(ht[s][:, :], pt[s][:, :], ACT.Identity, bias=r["be1"][:, 0:1],
                                         scale=r["g1"][:, 0:1]).then_inc(ht_ready[s], 1)
                for s in range(SL):
                    act.wait_ge(g_done[s], i + 1)
                    if not isinstance(i, int):
                        act.wait_ge(stored[s], i * 32)
                    nc.scalar.activation(g[s][:, 3, :], pt[s][:, 0:GW], ACT.Copy).then_inc(g_part[s], 1)
                for s in range(SL):
                    act.wait_ge(g_ready[s], i + 1)
                    act.dma_start(node_rows(t["g2"], i, s), g[s][:, :, :].rearrange("p a c -> p (a c)")).then_inc(stored[s], 16)
                    act.dma_start(node_rows(t["ed2"], i, s), ed[s][:, :, :].rearrange("p a c -> p (a c)")).then_inc(stored[s], 16)

            rounds(act, body)
            for s in range(SL):
                act.wait_ge(stored[s], IT * 32)


def ode_nodes(nc, t, d, r):
    with Phase(nc, "od") as ph:
        own_in = ph.sems("own_in")
        idx_in = ph.sems("idx_in")
        near_in = ph.sems("near_in")
        srci_in = ph.sems("srci_in")
        look_in = ph.sems("look_in")
        look_out = ph.sems("look_out")
        step = ph.sem("dve_step")
        arg_ready = ph.sems("arg_ready")
        exp_done = ph.sems("exp_done")
        mixed = ph.sems("mixed")
        gelu_done = ph.sems("gelu_done")
        var_ready = ph.sems("var_ready")
        rstd_ready = ph.sems("rstd_ready")
        xn_ready = ph.sems("xn_ready")
        turned = ph.sems("turned")
        y0_ready = ph.sems("y0_ready")
        mm_done = ph.sems("mm_done")
        z0_ready = ph.sems("z0_ready")
        t_ready = ph.sems("t_ready")
        z_ready = ph.sems("z_ready")
        u_ready = ph.sems("u_ready")
        y_ready = ph.sems("y_ready")
        back = ph.sems("back")
        h_part = ph.sems("h_part")
        h_ready = ph.sems("h_ready")
        stored = ph.sems("stored")
        dve_pace = ph.sem("dve_pace")
        pool_pace = ph.sem("pool_pace")

        own = ph.sbs("own", [128, A, GW])
        near = ph.sbs("near", [128, A, PW])
        idx = ph.sbs("idx", [128, A], I32)
        srci = ph.sbs("srci", [128, A], I32)
        look = ph.sbs("look", [128, A], I32)
        sc = ph.sbs("sc", [128, 6, A, H])
        arg = ph.sbs("arg", [128, 2, A, H])
        f = ph.sbs("f", [128, 2, A, H])
        y = ph.sbs("y", [128, A, C])
        stats = ph.sbs("stats", [128, A, 6])
        mv = ph.sbs("mv", [128, A, 2])
        var = ph.sbs("var", [128, A])
        rstd = ph.sbs("rstd", [128, A])
        y0 = ph.sbs("y0", [128, G])
        y0b = ph.sbs("y0b", [128, G])
        z0 = ph.sbs("z0", [128, G])
        zs = ph.sbs("zs", [128, G])
        z = ph.sbs("z", [128, G])
        ta = [ph.sbs(f"t{k}_", [128, G]) for k in range(2)]
        u = ph.sbs("u", [128, G])
        yt = ph.sbs("yt", [128, G])
        h = ph.sbs("h", [128, A, HW])
        pt = ph.pss("pt")
        pz = ph.pss("pz")
        block = ph.block()
        K = 15 * SL
        MM = 4 * ODE_STEPS + 1
        TT = 4 * ODE_STEPS
        ZZ = 4 * ODE_STEPS - 1
        STAGES = [(n, k) for n in range(ODE_STEPS) for k in range(4)]

        @block.sync
        def _(sp):
            def load(i, s):
                sp.dma_start(idx[s][:, :], node_rows(t["last_edge"][0:NP, :], i, s)).then_inc(idx_in[s], 16)
                sp.dma_start(own[s][:, :, :].rearrange("p a c -> p (a c)"), node_rows(t["g2"], i, s)).then_inc(own_in[s], 16)
                sp.dma_start(srci[s][:, :], edge_columns(d["src"], i, s)).then_inc(srci_in[s], 16)

            def store_look(i, s):
                sp.dma_start(edge_columns(t["src_edge"], i, s), look[s][:, :]).then_inc(look_out[s], 16)

            for s in range(SL):
                load(0, s)
            with sp.Fori(0, IT - 1) as i:
                done, looked = sp.snap(i + 1), sp.snap(i * 64 + 64)
                for s in range(SL):
                    sp.wait_ge(look_in[s], looked)
                    store_look(i, s)
                    sp.wait_ge(mixed[s], done)
                    load(i + 1, s)
            for s in range(SL):
                sp.wait_ge(look_in[s], IT * 64)
                store_look(IT - 1, s)
            for s in range(SL):
                sp.wait_ge(look_out[s], IT * 16)

        @block.gpsimd
        def _(pool):
            pace = Pace(pool, pool_pace)

            def root(i, s):
                pool.wait_ge(var_ready[s], i + 1)
                nc.gpsimd.tensor_tensor(out=rstd[s][:, :], in0=var[s][:, :], in1=r["mhalf"][:, :],
                                        op=ALU.pow).then_inc(rstd_ready[s], 1)

            def look_up(s):
                for a in range(A):
                    nc.gpsimd.indirect_dma_start(out=look[s][:, a:a + 1], out_offset=None, in_=t["last_edge"][0:NP, :],
                                                 in_offset=at(srci[s][:, a:a + 1])).then_inc(look_in[s], 16)

            for s in range(SL):
                pool.wait_ge(idx_in[s], 16)
                gather_rows(nc, near[s], t["pg"][0:EP + 1, :], idx[s], near_in[s])
            for s in range(SL):
                pool.wait_ge(srci_in[s], 16)
                look_up(s)
            with pool.Fori(0, IT - 1) as i:
                for s in range(SL):
                    root(i, s)
                for s in range(SL):
                    pool.wait_ge(idx_in[s], i * 16 + 32)
                    pool.wait_ge(gelu_done[s], i + 1)
                    pace.tick()
                    gather_rows(nc, near[s], t["pg"][0:EP + 1, :], idx[s], near_in[s])
                for s in range(SL):
                    pool.wait_ge(srci_in[s], i * 16 + 32)
                    pool.wait_ge(look_out[s], i * 16 + 16)
                    pace.tick()
                    look_up(s)
            for s in range(SL):
                root(IT - 1, s)

        @block.vector
        def _(dve):
            pace = Pace(dve, dve_pace)
            v_ = nc.vector

            def body(i):
                st = Steps(dve, step, i, K)
                for s in range(SL):
                    dve.wait_ge(own_in[s], i * 16 + 16)
                    dve.wait_ge(near_in[s], i * 64 + 64)
                    gat_args(nc, st, near[s], own[s], sc[s], arg[s], arg_ready[s])
                for s in range(SL):
                    dve.wait_ge(exp_done[s], i + 1)
                    gat_mix(nc, st, near[s], own[s], sc[s], f[s], r["bias2_all"], mixed[s])
                for s in range(SL):
                    dve.wait_ge(gelu_done[s], i + 1)
                    layer_norm_stats(nc, st, pace, y[s], stats[s], mv[s], var[s], var_ready[s])
                for s in range(SL):
                    dve.wait_ge(rstd_ready[s], i + 1)
                    normalize(nc, y[s], y[s], mv[s], rstd[s]).then_inc(xn_ready[s], 1)
                zn, un = 0, 0
                for q, (n, k) in enumerate(STAGES):
                    for s in range(SL):
                        if q > 0:
                            dve.wait_ge(t_ready[s], i * TT + q)
                            if q > 1:
                                weight = 2.0 if STAGES[q - 1][1] in (1, 2) else 1.0
                                if q > 2:
                                    dve.wait_ge(u_ready[s], i * ZZ + un)
                                v_.scalar_tensor_tensor(u[s][:, :], ta[(q - 1) % 2][s][:, :], weight, u[s][:, :],
                                                        ALU.mult, ALU.add).then_inc(u_ready[s], 1)
                            dve.wait_ge(mm_done[s], i * MM + q + 1)
                            first = z0[s] if k == 0 or n == 0 else zs[s]
                            scale = (DT / 6, DT / 2, DT / 2, DT)[k]
                            if q == 1:
                                dve.wait_ge(z0_ready[s], i + 1)
                            elif k > 0 and n > 0:
                                dve.wait_ge(z_ready[s], i * ZZ + q - 1)
                            v_.scalar_tensor_tensor((zs if k == 0 else z)[s][:, :], pz[s][:, :], scale, first[:, :],
                                                    ALU.mult, ALU.add).then_inc(z_ready[s], 1)
                    if q > 1:
                        un += 1
                for s in range(SL):
                    dve.wait_ge(t_ready[s], i * TT + TT)
                    dve.wait_ge(u_ready[s], i * ZZ + un)
                    v_.scalar_tensor_tensor(u[s][:, :], ta[(TT - 1) % 2][s][:, :], 1.0, u[s][:, :],
                                            ALU.mult, ALU.add).then_inc(u_ready[s], 1)
                for s in range(SL):
                    dve.wait_ge(mm_done[s], i * MM + MM)
                    v_.scalar_tensor_tensor(yt[s][:, :], pz[s][:, :], DT / 6, y0b[s][:, :],
                                            ALU.mult, ALU.add).then_inc(y_ready[s], 1)
                assert st.n == K and un + 1 == ZZ, (st.n, un)

            rounds(dve, body)

        @block.tensor
        def _(pe):
            def body(i):
                for s in range(SL):
                    pe.wait_ge(xn_ready[s], i + 1)
                    if not isinstance(i, int):
                        pe.wait_ge(h_ready[s], i)
                    for a in range(A):
                        last = nc.tensor.transpose(pt[s][:, a * 128:(a + 1) * 128], y[s][:, a, :], r["ident"][:, :])
                    last.then_inc(turned[s], 1)
                for s in range(SL):
                    pe.wait_ge(y0_ready[s], i + 1)
                    nc.tensor.matmul(pz[s][:, :], r["Wa"][:, :], y0[s][:, :], start=True, stop=True).then_inc(mm_done[s], 1)
                for q, (n, k) in enumerate(STAGES):
                    if q == 0:
                        continue
                    for s in range(SL):
                        if k == 0:
                            pe.wait_ge(u_ready[s], i * ZZ + q - 1)
                            src = u[s]
                        else:
                            pe.wait_ge(t_ready[s], i * TT + q)
                            src = u[s] if q == 1 else ta[(q - 1) % 2][s]
                        if q == 1:
                            pe.wait_ge(z0_ready[s], i + 1)
                        else:
                            pe.wait_ge(z_ready[s], i * ZZ + q - 1)
                        nc.tensor.matmul(pz[s][:, :], r["WbWa"][:, :], src[:, :], start=True, stop=True).then_inc(mm_done[s], 1)
                for s in range(SL):
                    pe.wait_ge(u_ready[s], i * ZZ + ZZ)
                    pe.wait_ge(z_ready[s], i * ZZ + ZZ)
                    nc.tensor.matmul(pz[s][:, :], r["Wb"][:, :], u[s][:, :], start=True, stop=True).then_inc(mm_done[s], 1)
                for s in range(SL):
                    pe.wait_ge(y_ready[s], i + 1)
                    for a in range(A):
                        nc.tensor.matmul(pz[s][:, a:a + 1], yt[s][:, a * 128:(a + 1) * 128], r["w_hop"][:, :], start=True, stop=True)
                    for a in range(A):
                        last = nc.tensor.transpose(pt[s][:, a * 128:(a + 1) * 128], yt[s][:, a * 128:(a + 1) * 128], r["ident"][:, :])
                    last.then_inc(back[s], 1)

            rounds(pe, body)

        @block.scalar
        def _(act):
            def body(i):
                for s in range(SL):
                    act.wait_ge(arg_ready[s], i + 1)
                    nc.scalar.activation(f[s][:, :, :, :], arg[s][:, :, :, :], ACT.Exp).then_inc(exp_done[s], 1)
                for s in range(SL):
                    act.wait_ge(mixed[s], i + 1)
                    nc.scalar.activation(y[s][:, :, :], near[s][:, :, 0:C], ACT.Gelu_apprx_tanh).then_inc(gelu_done[s], 1)
                for s in range(SL):
                    act.wait_ge(turned[s], i + 1)
                    nc.scalar.activation(y0[s][:, :], pt[s][:, :], ACT.Identity, bias=r["be2"][:, 0:1],
                                         scale=r["g2"][:, 0:1]).then_inc(y0_ready[s], 1)
                    nc.scalar.activation(y0b[s][:, :], pt[s][:, :], ACT.Identity, bias=r["be2_bo2"][:, 0:1],
                                         scale=r["g2"][:, 0:1])
                for s in range(SL):
                    act.wait_ge(mm_done[s], i * MM + 1)
                    nc.scalar.activation(u[s][:, :], pz[s][:, :], ACT.Tanh, bias=r["tanh_bias"][:, 0:1]).then_inc(t_ready[s], 1)
                    nc.scalar.activation(z0[s][:, :], pz[s][:, :], ACT.Copy).then_inc(z0_ready[s], 1)
                for q, (n, k) in enumerate(STAGES):
                    if q == 0:
                        continue
                    for s in range(SL):
                        act.wait_ge(z_ready[s], i * ZZ + q)
                        b = 2 * n + (0, 1, 1, 2)[k]
                        nc.scalar.activation(ta[q % 2][s][:, :], (zs if k == 0 else z)[s][:, :], ACT.Tanh,
                                             bias=r["tanh_bias"][:, b:b + 1]).then_inc(t_ready[s], 1)
                for s in range(SL):
                    act.wait_ge(back[s], i + 1)
                    if not isinstance(i, int):
                        act.wait_ge(stored[s], i * 16)
                    nc.scalar.activation(h[s][:, :, 0:C], pt[s][:, :].rearrange("p (a c) -> p a c", a=A),
                                         ACT.Copy).then_inc(h_part[s], 1)
                    nc.scalar.activation(h[s][:, :, C], pz[s][:, 0:A], ACT.Copy).then_inc(h_ready[s], 1)
                for s in range(SL):
                    act.wait_ge(h_part[s], i + 1)
                    act.wait_ge(h_ready[s], i + 1)
                    act.dma_start(node_rows(t["h"], i, s), h[s][:, :, :].rearrange("p a c -> p (a c)")).then_inc(stored[s], 16)

            rounds(act, body)
            for s in range(SL):
                act.wait_ge(stored[s], IT * 16)


def hop_edges(nc, t, d, r, k):
    source, index, width = ((t["h"], d["src"], HW), (t["p1"][0:EP + 1, :], t["src_edge"], HW + 1),
                            (t["p2"][0:EP + 1, :], t["src_edge"], HW + 1))[k - 1]
    stores = 1 if k == 3 else 2
    with Phase(nc, f"h{k}") as ph:
        idx_in = ph.sems("idx_in")
        rows_in = ph.sems("rows_in")
        step = ph.sem("dve_step")
        start = ph.sem("start")
        row_ready = ph.sems("row_ready")
        stored = ph.sems("stored")
        pool_pace = ph.sem("pool_pace")
        idx = ph.sbs("idx", [128, A], I32)
        rows = ph.sbs("rows", [128, A, width])
        rc = ph.sbs("rc", [128, A])
        mean = ph.sbs("mean", [128, A, HW])
        out = ph.sbs("out", [128, A, HW + 1])
        block = ph.block()
        K = SL * (4 + 3 * (k > 1))

        @block.sync
        def _(sp):
            def load(i, s):
                sp.dma_start(idx[s][:, :], edge_columns(index, i, s)).then_inc(idx_in[s], 16)

            def store(i, s):
                lo = (k - 1) * HW
                if k < 3:
                    sp.dma_start(edge_rows(t[f"p{k}"], i, s), out[s][:, :, :]).then_inc(stored[s], 16)
                    sp.dma_start(edge_rows(t["pc"], i, s, lo, lo + HW), out[s][:, :, 0:HW]).then_inc(stored[s], 16)
                else:
                    sp.dma_start(edge_rows(t["pc"], i, s, lo, CW), out[s][:, :, :]).then_inc(stored[s], 16)

            for s in range(SL):
                load(0, s)
            with sp.Fori(0, IT - 1) as i:
                ready = sp.snap(i + 1)
                for s in range(SL):
                    sp.wait_ge(row_ready[s], ready)
                    load(i + 1, s)
                    store(i, s)
            for s in range(SL):
                sp.wait_ge(row_ready[s], IT)
                store(IT - 1, s)
            for s in range(SL):
                sp.wait_ge(stored[s], IT * 16 * stores)

        @block.gpsimd
        def _(pool):
            pace = Pace(pool, pool_pace)

            def body(i):
                for s in range(SL):
                    if not isinstance(i, int):
                        pool.wait_ge(row_ready[s], i)
                    pool.wait_ge(idx_in[s], i * 16 + 16)
                    pace.tick()
                    gather_rows(nc, rows[s], source, idx[s], rows_in[s])

            rounds(pool, body)

        @block.vector
        def _(dve):
            v_ = nc.vector
            v_.memset(out[SL - 1][:, A - 1, :], 0.0).then_inc(start, 1)
            dve.wait_ge(start, 1)

            def body(i):
                st = Steps(dve, step, i, K)
                for s in range(SL):
                    o, prev = out[s], out[(s - 1) % SL][:, A - 1, :]
                    same = edge_columns(r["same"], i, s)
                    dve.wait_ge(rows_in[s], i * 64 + 64)
                    if not isinstance(i, int):
                        dve.wait_ge(stored[s], i * 16 * stores)
                    st.done(v_.tensor_copy(o[:, :, HW], edge_columns(r["cnt"], i, s)))
                    v = rows[s]
                    if k > 1:
                        v = mean[s]
                        st.link(v_.tensor_scalar(rc[s][:, :], rows[s][:, :, HW], 1.0, None, ALU.max))
                        st.link(v_.reciprocal(rc[s][:, :], rc[s][:, :]))
                        st.link(v_.tensor_tensor(v[:, :, :], rows[s][:, :, 0:HW],
                                                 rc[s][:, :].unsqueeze(2).broadcast_to([128, A, HW]), ALU.mult))
                    for a in range(A):
                        was = prev[:, 0:HW] if a == 0 else o[:, a - 1, 0:HW]
                        ins = v_.scalar_tensor_tensor(o[:, a, 0:HW], was, same[:, a:a + 1], v[:, a, 0:HW], ALU.mult, ALU.add)
                        if a < A - 1:
                            st.link(ins)
                        else:
                            ins.then_inc(row_ready[s], 1)
                            dve.wait_ge(row_ready[s], i + 1)
                assert st.n == K, st.n

            rounds(dve, body)
            Steps(dve, start, base=1).link(v_.tensor_copy(r["tail"][:, 0:HW + 1], out[SL - 1][:, A - 1, :]))


def hop_fix(nc, t, d, r, k):
    name, width = (("p1", HW + 1), ("p2", HW + 1), ("pc", CW))[k - 1]
    with Phase(nc, f"hf{k}") as ph:
        got = ph.sem("got")
        summed = ph.sem("summed")
        step = ph.sem("dve_step")
        fixed = ph.sem("fixed")
        put = ph.sem("put")
        old = ph.sb("old", [128, width])
        pc = ph.ps("pc")
        block = ph.block()

        @block.tensor
        def _(pe):
            nc.tensor.matmul(pc[:, 0:HW + 1], r["carry"][:, :], r["tail"][:, 0:HW + 1], start=True, stop=True).then_inc(summed, 1)

        @block.gpsimd
        def _(pool):
            nc.gpsimd.indirect_dma_start(out=old[:, :], out_offset=None, in_=t[name][0:EP + 1, :],
                                         in_offset=at(r["fix_get"][:, :])).then_inc(got, 16)
            pool.wait_ge(fixed, 1)
            nc.gpsimd.indirect_dma_start(out=t[name], out_offset=at(r["fix_put"][:, :]), in_=old[:, :],
                                         in_offset=None).then_inc(put, 16)
            pool.wait_ge(put, 16)

        @block.vector
        def _(dve):
            st = Steps(dve, step)
            v_ = nc.vector
            carried = r["carried"]
            dve.wait_ge(summed, 1)
            lo = (k - 1) * HW
            st.link(v_.tensor_copy(carried[:, lo:lo + HW + 1], pc[:, 0:HW + 1]))
            dve.wait_ge(got, 16)
            part = carried[:, lo:lo + HW + 1] if k < 3 else carried[:, :]
            v_.tensor_tensor(old[:, :], old[:, :], part, ALU.add).then_inc(fixed, 1)


def hop_nodes(nc, t, d, r):
    with Phase(nc, "hn") as ph:
        own_in = ph.sems("own_in")
        x_in = ph.sems("x_in")
        idx_in = ph.sems("idx_in")
        near_in = ph.sems("near_in")
        step = ph.sem("dve_step")
        arg_ready = ph.sems("arg_ready")
        exp_done = ph.sems("exp_done")
        weighted = ph.sems("weighted")
        agg_done = ph.sems("agg_done")
        agg_ready = ph.sems("agg_ready")
        o_done = ph.sems("o_done")
        x1_ready = ph.sems("x1_ready")
        var_ready = ph.sems("var_ready")
        rstd_ready = ph.sems("rstd_ready")
        shift_ready = ph.sems("shift_ready")
        h2_part = ph.sem("h2_part")
        h2_ready = ph.sems("h2_ready")
        stored = ph.sems("stored")
        dve_pace = ph.sem("dve_pace")
        pool_pace = ph.sem("pool_pace")
        own = ph.sbs("own", [128, A, HW])
        x = ph.sbs("x", [128, A, C])
        near = ph.sbs("near", [128, A, CW])
        idx = ph.sbs("idx", [128, A], I32)
        rc = ph.sbs("rc", [128, A])
        sc = ph.sbs("sc", [128, A, 4])
        top = ph.sbs("top", [128, A])
        arg = ph.sbs("arg", [128, A, 4])
        w = ph.sbs("w", [128, A, 4])
        agt = ph.sbs("agt", [128, G])
        x1 = ph.sbs("x1", [128, A, C])
        stats = ph.sbs("stats", [128, A, 6])
        mv = ph.sbs("mv", [128, A, 2])
        var = ph.sbs("var", [128, A])
        rstd = ph.sbs("rstd", [128, A])
        shift = ph.sbs("shift", [128, A])
        h2 = ph.sbs("h2", [128, A, C])
        pt = ph.pss("pt")
        po = ph.pss("po")
        block = ph.block()
        K = 26 * SL

        @block.sync
        def _(sp):
            def load(i, s):
                sp.dma_start(idx[s][:, :], node_rows(t["last_edge"][0:NP, :], i, s)).then_inc(idx_in[s], 16)
                sp.dma_start(own[s][:, :, :].rearrange("p a c -> p (a c)"), node_rows(t["h"], i, s)).then_inc(own_in[s], 16)

            def load_x(i, s):
                sp.dma_start(x[s][:, :, :].rearrange("p a c -> p (a c)"), node_rows(d["x"], i, s)).then_inc(x_in[s], 16)

            for s in range(SL):
                load(0, s)
                load_x(0, s)
            with sp.Fori(0, IT - 1) as i:
                done = sp.snap(i + 1)
                for s in range(SL):
                    sp.wait_ge(agg_done[s], done)
                    load(i + 1, s)
                for s in range(SL):
                    sp.wait_ge(x1_ready[s], done)
                    load_x(i + 1, s)

        @block.gpsimd
        def _(pool):
            pace = Pace(pool, pool_pace)

            def root(i, s):
                pool.wait_ge(var_ready[s], i + 1)
                nc.gpsimd.tensor_tensor(out=rstd[s][:, :], in0=var[s][:, :], in1=r["mhalf"][:, :],
                                        op=ALU.pow).then_inc(rstd_ready[s], 1)

            for s in range(SL):
                pool.wait_ge(idx_in[s], 16)
                gather_rows(nc, near[s], t["pc"][0:EP + 1, :], idx[s], near_in[s])
            with pool.Fori(0, IT - 1) as i:
                for s in range(SL):
                    root(i, s)
                    pool.wait_ge(idx_in[s], i * 16 + 32)
                    pace.tick()
                    gather_rows(nc, near[s], t["pc"][0:EP + 1, :], idx[s], near_in[s])
            for s in range(SL):
                root(IT - 1, s)

        @block.vector
        def _(dve):
            pace = Pace(dve, dve_pace)
            v_ = nc.vector

            def body(i):
                st = Steps(dve, step, i, K)
                for s in range(SL):
                    dve.wait_ge(own_in[s], i * 16 + 16)
                    dve.wait_ge(near_in[s], i * 64 + 64)
                    st.done(v_.tensor_copy(sc[s][:, :, 0], own[s][:, :, C]))
                    st.link(v_.tensor_scalar(rc[s][:, :], near[s][:, :, 3 * HW], 1.0, None, ALU.max))
                    st.link(v_.reciprocal(rc[s][:, :], rc[s][:, :]))
                    dots = near[s][:, :, 0:3 * HW].rearrange("p a (k c) -> p a k c", k=3)[:, :, :, C]
                    rc3 = rc[s][:, :].unsqueeze(2).broadcast_to([128, A, 3])
                    st.link(v_.tensor_tensor(sc[s][:, :, 1:4], dots, rc3, ALU.mult))
                    st.link(v_.tensor_reduce(top[s][:, :], sc[s][:, :, :], AX.X, ALU.max))
                    v_.tensor_tensor(arg[s][:, :, :], sc[s][:, :, :], top[s][:, :].unsqueeze(2).broadcast_to([128, A, 4]),
                                     ALU.subtract).then_inc(arg_ready[s], 1)
                for s in range(SL):
                    dve.wait_ge(exp_done[s], i + 1)
                    st.link(v_.tensor_reduce(top[s][:, :], w[s][:, :, :], AX.X, ALU.add))
                    st.link(v_.reciprocal(top[s][:, :], top[s][:, :]))
                    st.link(v_.tensor_tensor(w[s][:, :, :], w[s][:, :, :], top[s][:, :].unsqueeze(2).broadcast_to([128, A, 4]), ALU.mult))
                    st.link(v_.tensor_tensor(w[s][:, :, 1:4], w[s][:, :, 1:4],
                                             rc[s][:, :].unsqueeze(2).broadcast_to([128, A, 3]), ALU.mult))
                    for a in range(A):
                        for k in range(4):
                            v = own[s][:, a, 0:C] if k == 0 else near[s][:, a, (k - 1) * HW:(k - 1) * HW + C]
                            ins = v_.tensor_scalar(v, v, w[s][:, a, k:k + 1], None, ALU.mult)
                            if a < A - 1 or k < 3:
                                st.done(ins)
                            else:
                                ins.then_inc(weighted[s], 1)
                for s in range(SL):
                    dve.wait_ge(o_done[s], i + 1)
                    dve.wait_ge(x_in[s], i * 16 + 16)
                    if not isinstance(i, int):
                        dve.wait_ge(stored[s], i * 32)
                    v_.tensor_tensor(x1[s][:, :, :], po[s][:, :].rearrange("p (a c) -> p a c", a=A), x[s][:, :, :],
                                     ALU.add).then_inc(x1_ready[s], 1)
                    dve.wait_ge(x1_ready[s], i + 1)
                    layer_norm_stats(nc, st, pace, x1[s], stats[s], mv[s], var[s], var_ready[s])
                for s in range(SL):
                    dve.wait_ge(rstd_ready[s], i + 1)
                    v_.scalar_tensor_tensor(shift[s][:, :], mv[s][:, :, 0], -1.0, rstd[s][:, :],
                                            ALU.mult, ALU.mult).then_inc(shift_ready[s], 1)
                assert st.n == K, st.n

            rounds(dve, body)

        @block.tensor
        def _(pe):
            def body(i):
                for s in range(SL):
                    pe.wait_ge(weighted[s], i + 1)
                    if not isinstance(i, int):
                        pe.wait_ge(agg_ready[s], i)
                    for a in range(A):
                        for k in range(4):
                            v = own[s][:, a, 0:C] if k == 0 else near[s][:, a, (k - 1) * HW:(k - 1) * HW + C]
                            last = nc.tensor.matmul(pt[s][:, a * 128:(a + 1) * 128], v, r["ident"][:, :],
                                                    start=(k == 0), stop=(k == 3))
                    last.then_inc(agg_done[s], 1)
                for s in range(SL):
                    pe.wait_ge(agg_ready[s], i + 1)
                    if not isinstance(i, int):
                        pe.wait_ge(x1_ready[s], i)
                    for a in range(A):
                        o = po[s][:, a * 128:(a + 1) * 128]
                        nc.tensor.matmul(o, agt[s][:, a * 128:(a + 1) * 128], r["W_out"][:, :], start=True, stop=False)
                        last = nc.tensor.matmul(o, r["ones_row"][:, :], r["b_out_row"][:, :], start=False, stop=True)
                    last.then_inc(o_done[s], 1)

            rounds(pe, body)

        @block.scalar
        def _(act):
            def body(i):
                for s in range(SL):
                    act.wait_ge(arg_ready[s], i + 1)
                    nc.scalar.activation(w[s][:, :, :], arg[s][:, :, :], ACT.Exp).then_inc(exp_done[s], 1)
                for s in range(SL):
                    act.wait_ge(agg_done[s], i + 1)
                    nc.scalar.activation(agt[s][:, :], pt[s][:, :], ACT.Copy).then_inc(agg_ready[s], 1)
                for s in range(SL):
                    act.wait_ge(shift_ready[s], i + 1)
                    act.dma_start(node_rows(t["x1"], i, s), x1[s][:, :, :].rearrange("p a c -> p (a c)")).then_inc(stored[s], 16)
                    if not isinstance(i, int):
                        act.wait_ge(stored[s], i * 32)
                    for a in range(A):
                        ins = nc.scalar.activation(h2[s][:, a, :], x1[s][:, a, :], ACT.Relu, bias=shift[s][:, a:a + 1],
                                                   scale=rstd[s][:, a:a + 1])
                        ins.then_inc(h2_ready[s] if a == A - 1 else h2_part, 1)
                for s in range(SL):
                    act.wait_ge(h2_ready[s], i + 1)
                    act.dma_start(node_rows(t["h2"], i, s), h2[s][:, :, :].rearrange("p a c -> p (a c)")).then_inc(stored[s], 16)

            rounds(act, body)
            for s in range(SL):
                act.wait_ge(stored[s], IT * 32)


def relation_edges(nc, t, d, r):
    with Phase(nc, "re") as ph:
        idx_in = ph.sems("idx_in")
        rel_in = ph.sems("rel_in")
        rows_in = ph.sems("rows_in")
        step = ph.sem("dve_step")
        start = ph.sem("start")
        hot_ready = ph.sems("hot_ready")
        rel_done = ph.sems("rel_done")
        arg_ready = ph.sems("arg_ready")
        exp_done = ph.sems("exp_done")
        row_ready = ph.sems("row_ready")
        stored = ph.sems("stored")
        pool_pace = ph.sem("pool_pace")
        srci = ph.sbs("srci", [128, A], I32)
        dsti = ph.sbs("dsti", [128, A], I32)
        rel = ph.sbs("rel", [128, G], I32)
        hot_a = ph.sbs("hot_a", [128, G])
        hot_b = ph.sbs("hot_b", [NR - 128, G])
        hs = ph.sbs("hs", [128, A, C])
        hd = ph.sbs("hd", [128, A, C])
        comp = ph.sbs("comp", [128, A, C])
        score = ph.sbs("score", [128, A])
        base = ph.sbs("base", [128, A])
        arg = ph.sbs("arg", [128, 2, A])
        wts = ph.sbs("wts", [128, 2, A])
        out = ph.sbs("out", [128, A, LW])
        pr = ph.pss("pr")
        block = ph.block()
        K = SL * 12

        @block.sync
        def _(sp):
            def load(i, s):
                sp.dma_start(srci[s][:, :], edge_columns(d["src"], i, s)).then_inc(idx_in[s], 16)
                sp.dma_start(dsti[s][:, :], edge_columns(d["dst"], i, s)).then_inc(idx_in[s], 16)
                j = (i * SL + s) * A
                flat = d["rel_t"].rearrange("(o j) p -> o (j p)", j=A)
                o = i * SL + s
                one = flat[o:o + 1, :] if isinstance(o, int) else flat[bass.ds(o, 1), :]
                sp.dma_start(rel[s][:, :], one.broadcast_to([128, G])).then_inc(rel_in[s], 16)

            def store(i, s):
                sp.dma_start(edge_rows(t["pl"], i, s), out[s][:, :, :]).then_inc(stored[s], 16)

            for s in range(SL):
                load(0, s)
            with sp.Fori(0, IT - 1) as i:
                ready = sp.snap(i + 1)
                for s in range(SL):
                    sp.wait_ge(row_ready[s], ready)
                    load(i + 1, s)
                    store(i, s)
            for s in range(SL):
                sp.wait_ge(row_ready[s], IT)
                store(IT - 1, s)
            for s in range(SL):
                sp.wait_ge(stored[s], IT * 16)

        @block.gpsimd
        def _(pool):
            pace = Pace(pool, pool_pace)

            def body(i):
                for s in range(SL):
                    if not isinstance(i, int):
                        pool.wait_ge(row_ready[s], i)
                    pool.wait_ge(idx_in[s], i * 32 + 32)
                    pace.tick()
                    gather_rows(nc, hs[s], t["h2"], srci[s], rows_in[s])
                    gather_rows(nc, hd[s], t["h2"], dsti[s], rows_in[s])

            rounds(pool, body)

        @block.tensor
        def _(pe):
            def body(i):
                for s in range(SL):
                    pe.wait_ge(hot_ready[s], i * 2 + 2)
                    for a in range(A):
                        o, c = pr[s][:, a * 128:(a + 1) * 128], slice(a * 128, (a + 1) * 128)
                        nc.tensor.matmul(o, hot_a[s][:, c], r["rel_a"][:, :], start=True, stop=False)
                        last = nc.tensor.matmul(o, hot_b[s][:, c], r["rel_b"][:, :], start=False, stop=True)
                    last.then_inc(rel_done[s], 1)

            rounds(pe, body)

        @block.scalar
        def _(act):
            def body(i):
                for s in range(SL):
                    act.wait_ge(arg_ready[s], i + 1)
                    nc.scalar.activation(wts[s][:, :, :], arg[s][:, :, :], ACT.Exp).then_inc(exp_done[s], 1)

            rounds(act, body)

        @block.vector
        def _(dve):
            v_ = nc.vector
            v_.memset(out[SL - 1][:, A - 1, 0:C + 1], 0.0).then_inc(start, 1)
            v_.memset(out[SL - 1][:, A - 1, C + 1:LW], -BIG).then_inc(start, 1)
            dve.wait_ge(start, 2)

            def body(i):
                st = Steps(dve, step, i, K)
                for s in range(SL):
                    dve.wait_ge(rel_in[s], i * 16 + 16)
                    v_.tensor_scalar(hot_a[s][:, :], rel[s][:, :], r["pidf"][:, 0:1], None, ALU.is_equal).then_inc(hot_ready[s], 1)
                    v_.tensor_scalar(hot_b[s][:, :], rel[s][0:NR - 128, :], r["pidf"][0:NR - 128, 1:2], None,
                                     ALU.is_equal).then_inc(hot_ready[s], 1)
                for s in range(SL):
                    o, prev = out[s], out[(s - 1) % SL][:, A - 1, :]
                    m = o[:, :, C + 1]
                    fresh = edge_columns(r["fresh"], i, s)
                    dve.wait_ge(rows_in[s], i * 128 + 128)
                    dve.wait_ge(rel_done[s], i + 1)
                    if not isinstance(i, int):
                        dve.wait_ge(stored[s], i * 16)
                    st.link(v_.tensor_tensor(comp[s][:, :, :], pr[s][:, :].rearrange("p (a c) -> p a c", a=A), hs[s][:, :, :], ALU.mult))
                    st.link(v_.tensor_tensor(hd[s][:, :, :], comp[s][:, :, :], hd[s][:, :, :], ALU.mult))
                    st.link(v_.tensor_reduce(score[s][:, :], hd[s][:, :, :], AX.X, ALU.add))
                    st.link(v_.tensor_tensor_scan(m, fresh, score[s][:, :], prev[:, C + 1:LW], ALU.add, ALU.max))
                    st.done(v_.tensor_tensor(base[s][:, 0:1], prev[:, C + 1:LW], fresh[:, 0:1], ALU.add))
                    st.link(v_.tensor_tensor(base[s][:, 1:A], m[:, 0:A - 1], fresh[:, 1:A], ALU.add))
                    st.done(v_.tensor_tensor(arg[s][:, 0, :], base[s][:, :], m, ALU.subtract))
                    v_.tensor_tensor(arg[s][:, 1, :], score[s][:, :], m, ALU.subtract).then_inc(arg_ready[s], 1)
                    dve.wait_ge(exp_done[s], i + 1)
                    keep, w = wts[s][:, 0, :], wts[s][:, 1, :]
                    st.done(v_.tensor_tensor_scan(o[:, :, C], keep, w, prev[:, C:C + 1], ALU.mult, ALU.add))
                    st.link(v_.tensor_tensor(comp[s][:, :, :], comp[s][:, :, :], w.unsqueeze(2).broadcast_to([128, A, C]), ALU.mult))
                    for a in range(A):
                        was = prev[:, 0:C] if a == 0 else o[:, a - 1, 0:C]
                        ins = v_.scalar_tensor_tensor(o[:, a, 0:C], was, keep[:, a:a + 1], comp[s][:, a, :], ALU.mult, ALU.add)
                        if a < A - 1:
                            st.link(ins)
                        else:
                            ins.then_inc(row_ready[s], 1)
                            dve.wait_ge(row_ready[s], i + 1)
                assert st.n == K, st.n

            rounds(dve, body)
            Steps(dve, start, base=2).link(v_.tensor_copy(r["tail"][:, 0:LW], out[SL - 1][:, A - 1, :]))


def norm_nodes(nc, t, d, r):
    with Phase(nc, "nn") as ph:
        idx_in = ph.sems("idx_in")
        near_in = ph.sems("near_in")
        step = ph.sem("dve_step")
        divided = ph.sems("divided")
        turned = ph.sems("turned")
        nt_ready = ph.sems("nt_ready")
        h_done = ph.sems("h_done")
        stats_done = ph.sems("stats_done")
        h_ready = ph.sems("h_ready")
        stored = ph.sems("stored")
        pool_pace = ph.sem("pool_pace")
        dve_pace = ph.sem("dve_pace")
        root_ready = ph.sem("root_ready")
        var_ready = ph.sem("var_ready")
        end = ph.sem("end")
        idx = ph.sbs("idx", [128, A], I32)
        near = ph.sbs("near", [128, A, LW])
        rs = ph.sbs("rs", [128, A])
        nt = ph.sbs("nt", [128, G])
        ht = ph.sbs("ht", [128, G])
        stats = ph.sb("stats", [128, IT * SL, 6])
        mv = ph.sb("mv", [128, 2])
        m2 = ph.sb("m2", [128, 1])
        var = ph.sb("var", [128, 1])
        rstd = ph.sb("rstd", [128, 1])
        pt = ph.pss("pt")
        po = ph.pss("po")
        block = ph.block()
        K = SL

        @block.sync
        def _(sp):
            def load(i, s):
                sp.dma_start(idx[s][:, :], node_rows(t["last_edge"][0:NP, :], i, s)).then_inc(idx_in[s], 16)

            def store(i, s):
                g = i * SL + s
                o = t["ht"][g] if isinstance(g, int) else t["ht"][bass.ds(g, 1)].rearrange("o p f -> (o p) f")
                sp.dma_start(o, ht[s][:, :]).then_inc(stored[s], 16)

            for s in range(SL):
                load(0, s)
            with sp.Fori(0, IT - 1) as i:
                done = sp.snap(i + 1)
                for s in range(SL):
                    sp.wait_ge(divided[s], done)
                    load(i + 1, s)
                for s in range(SL):
                    sp.wait_ge(h_ready[s], done)
                    store(i, s)
            for s in range(SL):
                sp.wait_ge(h_ready[s], IT)
                store(IT - 1, s)
            for s in range(SL):
                sp.wait_ge(stored[s], IT * 16)

        @block.gpsimd
        def _(pool):
            pace = Pace(pool, pool_pace)

            def body(i):
                for s in range(SL):
                    pool.wait_ge(idx_in[s], i * 16 + 16)
                    if not isinstance(i, int):
                        pool.wait_ge(turned[s], i)
                    pace.tick()
                    gather_rows(nc, near[s], t["pl"][0:EP + 1, :], idx[s], near_in[s])

            rounds(pool, body)
            pool.wait_ge(var_ready, 1)
            nc.gpsimd.tensor_tensor(out=rstd[:, :], in0=var[:, :], in1=r["mhalf"][:, 0:1], op=ALU.pow).then_inc(root_ready, 1)

        @block.vector
        def _(dve):
            pace = Pace(dve, dve_pace)
            v_ = nc.vector

            def body(i):
                st = Steps(dve, step, i, K)
                for s in range(SL):
                    dve.wait_ge(near_in[s], i * 64 + 64)
                    st.link(v_.reciprocal(rs[s][:, :], near[s][:, :, C]))
                    v_.tensor_tensor(near[s][:, :, 0:C], near[s][:, :, 0:C], rs[s][:, :].unsqueeze(2).broadcast_to([128, A, C]),
                                     ALU.mult).then_inc(divided[s], 1)
                for s in range(SL):
                    dve.wait_ge(h_ready[s], i + 1)
                    pace.tick()
                    g = i * SL + s
                    o = stats[:, g, :] if isinstance(g, int) else stats[:, bass.ds(g, 1), :].rearrange("p o k -> p (o k)")
                    v_.bn_stats(o, ht[s][:, :]).then_inc(stats_done[s], 1)
                assert st.n == K, st.n

            rounds(dve, body)
            grow = NP / N
            st = Steps(dve, end)
            for s in range(SL):
                dve.wait_ge(stats_done[s], IT)
            st.link(v_.bn_aggr(mv[:, :], stats[:, :, :].rearrange("p g k -> p (g k)")))
            st.link(v_.tensor_tensor(m2[:, :], mv[:, 0:1], mv[:, 0:1], ALU.mult))
            st.link(v_.scalar_tensor_tensor(var[:, :], m2[:, :], 1.0 - grow, mv[:, 1:2], ALU.mult, ALU.add))
            v_.tensor_scalar(var[:, :], var[:, :], grow, EPS, ALU.mult, ALU.add).then_inc(var_ready, 1)
            dve.wait_ge(root_ready, 1)
            st.link(v_.tensor_tensor(r["bn_scale"][:, :], rstd[:, :], r["gamma"][:, :], ALU.mult))
            st.link(v_.scalar_tensor_tensor(m2[:, :], mv[:, 0:1], -grow, r["bn_scale"][:, :], ALU.mult, ALU.mult))
            st.link(v_.tensor_tensor(r["bn_shift"][:, :], m2[:, :], r["beta"][:, :], ALU.add))

        @block.tensor
        def _(pe):
            def body(i):
                for s in range(SL):
                    pe.wait_ge(divided[s], i + 1)
                    if not isinstance(i, int):
                        pe.wait_ge(nt_ready[s], i)
                    for a in range(A):
                        last = nc.tensor.transpose(pt[s][:, a * 128:(a + 1) * 128], near[s][:, a, 0:C], r["ident"][:, :])
                    last.then_inc(turned[s], 1)
                for s in range(SL):
                    pe.wait_ge(nt_ready[s], i + 1)
                    if not isinstance(i, int):
                        pe.wait_ge(h_ready[s], i)
                    nc.tensor.matmul(po[s][:, :], r["neigh_w"][:, :], nt[s][:, :], start=True, stop=True).then_inc(h_done[s], 1)

            rounds(pe, body)

        @block.scalar
        def _(act):
            def body(i):
                for s in range(SL):
                    act.wait_ge(turned[s], i + 1)
                    nc.scalar.activation(nt[s][:, :], pt[s][:, :], ACT.Copy).then_inc(nt_ready[s], 1)
                for s in range(SL):
                    act.wait_ge(h_done[s], i + 1)
                    if not isinstance(i, int):
                        act.wait_ge(stored[s], i * 16)
                        act.wait_ge(stats_done[s], i)
                    nc.scalar.activation(ht[s][:, :], po[s][:, :], ACT.Copy).then_inc(h_ready[s], 1)

            rounds(act, body)


def out_nodes(nc, t, d, r, out):
    with Phase(nc, "on") as ph:
        h_in = ph.sems("h_in")
        x_in = ph.sems("x_in")
        tanh_done = ph.sems("tanh_done")
        turned = ph.sems("turned")
        o_ready = ph.sems("o_ready")
        stored = ph.sems("stored")
        ht = ph.sbs("ht", [128, G])
        x1 = ph.sbs("x1", [128, G])
        th = ph.sbs("th", [128, G])
        o = ph.sbs("o", [128, G])
        pt = ph.pss("pt")
        block = ph.block()

        @block.sync
        def _(sp):
            def load(i, s):
                g = i * SL + s
                h = t["ht"][g] if isinstance(g, int) else t["ht"][bass.ds(g, 1)].rearrange("o p f -> (o p) f")
                sp.dma_start(ht[s][:, :], h).then_inc(h_in[s], 16)

            def load_x(i, s):
                sp.dma_start(x1[s][:, :], node_rows(t["x1"], i, s)).then_inc(x_in[s], 16)

            for s in range(SL):
                load(0, s)
                load_x(0, s)
            with sp.Fori(0, IT - 1) as i:
                done = sp.snap(i + 1)
                for s in range(SL):
                    sp.wait_ge(tanh_done[s], done)
                    load(i + 1, s)
                    sp.wait_ge(o_ready[s], done)
                    load_x(i + 1, s)

        @block.scalar
        def _(act):
            def body(i):
                for s in range(SL):
                    act.wait_ge(h_in[s], i * 16 + 16)
                    if not isinstance(i, int):
                        act.wait_ge(turned[s], i)
                    nc.scalar.activation(th[s][:, :], ht[s][:, :], ACT.Tanh, bias=r["bn_shift"][:, 0:1],
                                         scale=r["bn_scale"][:, 0:1]).then_inc(tanh_done[s], 1)
                for s in range(SL):
                    act.wait_ge(o_ready[s], i + 1)
                    act.dma_start(node_rows(out, i, s), o[s][:, :]).then_inc(stored[s], 16)

            rounds(act, body)
            for s in range(SL):
                act.wait_ge(stored[s], IT * 16)

        @block.tensor
        def _(pe):
            def body(i):
                for s in range(SL):
                    pe.wait_ge(tanh_done[s], i + 1)
                    if not isinstance(i, int):
                        pe.wait_ge(o_ready[s], i)
                    for a in range(A):
                        last = nc.tensor.transpose(pt[s][:, a * 128:(a + 1) * 128], th[s][:, a * 128:(a + 1) * 128], r["ident"][:, :])
                    last.then_inc(turned[s], 1)

            rounds(pe, body)

        @block.vector
        def _(dve):
            def body(i):
                for s in range(SL):
                    dve.wait_ge(turned[s], i + 1)
                    dve.wait_ge(x_in[s], i * 16 + 16)
                    if not isinstance(i, int):
                        dve.wait_ge(stored[s], i * 16)
                    nc.vector.tensor_tensor(o[s][:, :], pt[s][:, :], x1[s][:, :], ALU.add).then_inc(o_ready[s], 1)

            rounds(dve, body)


def build(nc, d, out, upto=99):
    t = {}

    def dram(name, shape, dt=F32):
        t[name] = nc.dram_tensor(f"w_{name}", shape, dt, kind="Internal").ap()

    dram("g", (NP, GW))
    dram("ed", (NP, H))
    dram("g2", (NP, GW))
    dram("ed2", (NP, H))
    dram("pg", (EP + 129, PW))
    dram("p1", (EP + 129, HW + 1))
    dram("p2", (EP + 129, HW + 1))
    dram("pc", (EP + 129, CW))
    dram("pl", (EP + 129, LW))
    dram("h", (NP, HW))
    dram("x1", (NP, C))
    dram("h2", (NP, C))
    dram("ht", (IT * SL, 128, G))
    dram("last_edge", (NP + EP, 1), I32)
    dram("src_edge", (128, EC), I32)
    dram("sidx", (128, EC), I32)
    dram("eidx", (128, EC), I32)
    with ExitStack() as stack, nc.allow_non_contiguous_dma(reason="one word for each partition"):
        r = {}

        def keep(name, shape, dt=F32):
            r[name] = stack.enter_context(nc.sbuf_tensor(f"r_{name}", shape, dt))

        for k in ("ident", "W_in", "Wa", "Wb", "WbWa", "W_out", "neigh_w", "rel_a", "carry", "carry_mask",
                  "bias1_all", "bias2_all"):
            keep(k, [128, 128])
        for k in VECTORS + ("be2_bo2", "chained"):
            keep(k, [128, 1])
        for k in ("pid", "low", "spare", "dfirst", "fix_get", "fix_put"):
            keep(k, [128, 1], I32)
        keep("tail", [128, PW])
        keep("carried", [128, CW])
        keep("pidf", [128, 2])
        keep("bn_scale", [128, 1])
        keep("bn_shift", [128, 1])
        keep("W1e", [128, GW])
        keep("W2e", [128, GW])
        keep("rel_b", [NR - 128, 128])
        keep("b_out_row", [1, 128])
        keep("ones_row", [1, 128])
        keep("mhalf", [128, A])
        keep("tanh_bias", [128, 2 * ODE_STEPS + 1])
        for k in ("same", "fresh", "cnt"):
            keep(k, [128, EC])
        phases(nc, t, d, r, out, upto)


def phases(nc, t, d, r, out, upto):
    setup(nc, t, d, r)
    if upto < 1:
        return
    node_in(nc, t, d, r)
    fix_index(nc, t, d, r)
    if upto < 2:
        return
    gat_edges(nc, t, d, r, "ge1", "g", "ed")
    softmax_fix(nc, t, d, r, "gf1", "pg", H, PW)
    if upto < 3:
        return
    gat_nodes(nc, t, d, r)
    gat_edges(nc, t, d, r, "ge2", "g2", "ed2")
    softmax_fix(nc, t, d, r, "gf2", "pg", H, PW)
    if upto < 4:
        return
    ode_nodes(nc, t, d, r)
    if upto < 5:
        return
    for k in (1, 2, 3):
        hop_edges(nc, t, d, r, k)
        hop_fix(nc, t, d, r, k)
    if upto < 6:
        return
    hop_nodes(nc, t, d, r)
    if upto < 7:
        return
    relation_edges(nc, t, d, r)
    softmax_fix(nc, t, d, r, "rf", "pl", 1, LW)
    if upto < 8:
        return
    norm_nodes(nc, t, d, r)
    out_nodes(nc, t, d, r, out)


NAMES = {"L0_gnn_W_in": "W_in", "L0_gnn_b_in": "b_in", "L0_gnn_W1": "W1", "L0_gnn_att1_src": "att1_src",
         "L0_gnn_att1_dst": "att1_dst", "L0_gnn_bias1": "bias1", "L0_gnn_W2": "W2", "L0_gnn_att2_src": "att2_src",
         "L0_gnn_att2_dst": "att2_dst", "L0_gnn_bias2": "bias2", "L0_gnn_g1": "g1", "L0_gnn_be1": "be1",
         "L0_gnn_g2": "g2", "L0_gnn_be2": "be2", "L0_gnn_Wo1": "Wo1", "L0_gnn_bo1": "bo1", "L0_gnn_Wo2": "Wo2",
         "L0_gnn_bo2": "bo2", "L0_gnn_w_hop": "w_hop", "L0_gnn_W_out": "W_out", "L0_gnn_b_out": "b_out",
         "L1_gnn_rel_emb": "rel_emb", "L1_gnn_neigh_w": "neigh_w", "L1_gnn_gamma": "gamma", "L1_gnn_beta": "beta"}


def lay_out(inputs):
    def edges(name, fill):
        return np.concatenate([np.asarray(inputs[name]), np.full(EP - N, fill, np.int32)]).reshape(128, EC)

    x = np.asarray(inputs["x"])
    arrays = {"x": np.concatenate([x, np.zeros((NP - N, C), x.dtype)]),
              "src": edges("src", N), "dst": edges("dst", N)}
    arrays["rel_t"] = np.ascontiguousarray(edges("edge_type_130", 0).T)
    for name, short in NAMES.items():
        arrays[short] = np.ascontiguousarray(inputs[name])
    return arrays


def kernel(**inputs):
    import concourse.bacc as _bacc
    from concourse.bass_utils import run_bass_kernel_spmd as _run

    nc = _bacc.Bacc("TRN2", target_bir_lowering=False, num_devices=1)
    arrays = {f"in_{k}": a for k, a in lay_out(inputs).items()}
    d = {k[3:]: nc.dram_tensor(k, a.shape, mybir.dt.from_np(a.dtype), kind="ExternalInput").ap()
         for k, a in arrays.items()}
    out = nc.dram_tensor("out_0", (NP, C), F32, kind="ExternalOutput").ap()
    build(nc, d, out)
    r = _run(nc, [arrays], core_ids=[0])
    return r.results[0]["out_0"][:N]
```

```python
from contextlib import ExitStack

import numpy as np

import concourse.bass as bass
from concourse import mybir

F32 = mybir.dt.float32
I32 = mybir.dt.int32
ALU = mybir.AluOpType
ACT = mybir.ActivationFunctionType
AX = mybir.AxisListType

N = 50000
C = 128
H = 4
D = C // H
A = 4
POOL_SETUP = 14
SL = 3
G = 512
IT = 33
NP = IT * SL * G
OSL = 4
OIT = 25
EC = IT * SL * A
EP = 128 * EC
NULL = EP
GW = C + 2 * H
PW = C + 2 * H
HW = C + 1
CW = 3 * HW + 1
LW = C + 2
NR = 130
BIG = 1.0e30
EPS = 1.0e-5
ODE_STEPS = 4
DT = 1.0 / ODE_STEPS


class Steps:

    def __init__(self, eng, sem, i=None, per_iteration=0, base=0):
        self.eng, self.sem, self.i, self.per, self.base, self.n = eng, sem, i, per_iteration, base, 0

    def value(self):
        own = self.base + self.n
        return own if self.i is None or isinstance(self.i, int) and self.i == 0 else self.i * self.per + own

    def done(self, ins):
        ins.then_inc(self.sem, 1)
        self.n += 1

    def wait(self):
        self.eng.wait_ge(self.sem, self.value())

    def link(self, ins):
        self.done(ins)
        self.wait()


class Phase:

    def __init__(self, nc, tag):
        self.nc, self.tag, self.stack, self.used = nc, tag, ExitStack(), []

    def __enter__(self):
        return self

    def __exit__(self, *a):
        return self.stack.__exit__(*a)

    def sem(self, name):
        self.used.append(self.nc.alloc_semaphore(f"{self.tag}_{name}"))
        return self.used[-1]

    def clear(self):
        self.nc.clear_and_free_semaphores(self.used)
        self.nc.all_engine_barrier()

    def sems(self, name, n=SL):
        return [self.sem(f"{name}{s}") for s in range(n)]

    def sb(self, name, shape, dt=F32):
        return self.stack.enter_context(self.nc.sbuf_tensor(f"{self.tag}_{name}", shape, dt))

    def sbs(self, name, shape, dt=F32, n=SL):
        return [self.sb(f"{name}{s}", shape, dt) for s in range(n)]

    def ps(self, name):
        return self.stack.enter_context(self.nc.psum_tensor(f"{self.tag}_{name}", [128, 512], F32))

    def pss(self, name, n=SL):
        return [self.ps(f"{name}{s}") for s in range(n)]

    def block(self):
        self.stack.callback(self.clear)
        return self.stack.enter_context(self.nc.Block())


class Pace:

    def __init__(self, eng, sem):
        self.eng, self.sem = eng, sem

    def tick(self):
        self.eng.sem_inc(self.sem, 1)


def rounds(eng, body, turns=IT):
    body(0)
    with eng.Fori(1, turns) as i:
        body(i)


def landed(i, b, each):
    return (i + 2 - b) * (each // 2)


def double_rounds(eng, body):
    body(0, 0)
    body(1, 1)
    with eng.Fori(0, (IT - 3) // 2) as j:
        body(j * 2 + 2, 0)
        body(j * 2 + 3, 1)
    body(IT - 1, 0)


def late_rounds(eng, body, peeled):
    for i in range(peeled):
        body(i)
    with eng.Fori(peeled, IT) as i:
        body(i)


def later(i, n=1):
    return not isinstance(i, int) or i >= n


def final(i):
    return isinstance(i, int) and i == IT - 1


def col(v):
    return v.rearrange("(p a) -> p a", a=1)


def row(v):
    return v.rearrange("(a n) -> a n", a=1)



VECTORS = ("b_in", "g1", "be1", "g2", "be2", "bo1", "bo2", "gamma", "beta", "w_hop")
WEIGHTS = ("W_in", "Wo1", "Wo2", "W_out", "W1", "W2")


def setup(nc, t, d, r):
    with Phase(nc, "su") as ph:
        loaded = ph.sem("loaded")
        dst_in = ph.sem("dst_in")
        next_in = ph.sem("next_in")
        nd_set = ph.sem("nd_set")
        zeroed = ph.sem("zeroed")
        pool_step = ph.sem("pool_step")
        dve_step = ph.sem("dve_step")
        flags_ready = ph.sem("flags_ready")
        ends_ready = ph.sem("ends_ready")
        rows_done = ph.sem("rows_done")
        turned = ph.sem("turned")
        wt_ready = ph.sem("wt_ready")
        att_done = ph.sem("att_done")
        uv_ready = ph.sem("uv_ready")
        mv_done = ph.sem("mv_done")
        sq_ready = ph.sem("sq_ready")
        ss_done = ph.sem("ss_done")
        ss_ready = ph.sem("ss_ready")
        nrm_ready = ph.sem("nrm_ready")
        scaled = ph.sem("scaled")
        m_done = ph.sem("m_done")
        stored = ph.sem("stored")

        dsti = ph.sb("dsti", [128, EC], I32)
        dstf = ph.sb("dstf", [128, EC + 1])
        nd = ph.sb("nd", [128, 1], I32)
        isl = ph.sb("isl", [128, EC])
        ones_e = ph.sb("ones_e", [128, EC])
        real = ph.sb("real", [128, EC])
        sidf = ph.sb("sidf", [128, EC])
        sidx = ph.sb("sidx", [128, EC], I32)
        eidx = ph.sb("eidx", [128, EC], I32)
        nulli = ph.sb("nulli", [128, EC], I32)
        nrow = ph.sb("nrow", [1, PW + CW + LW])
        zeros = ph.sb("zeros", [128, G])
        ut = ph.sb("ut", [128, 128])
        lt = ph.sb("lt", [128, 128])
        ones = ph.sb("ones", [128, 128])
        half = ph.sb("half", [128, 4])
        asd = [ph.sb(f"asd{l}", [128, 2 * H]) for l in range(2)]
        raw = ph.sb("raw", [128, 6, 128])
        wt = ph.sb("wt", [128, 6, 128])
        u = ph.sb("u", [128, 4])
        x = ph.sb("x", [128, 4])
        sq = ph.sb("sq", [128, 4])
        nrm = ph.sb("nrm", [128, 4])
        rn = ph.sb("rn", [128, 4])
        wbt = ph.sb("wbt", [128, 128])
        vec = ph.sb("vec", [128, 1])
        dfb = ph.sb("dfb", [128, 2, 128])
        pa = ph.ps("pa")
        pb = ph.ps("pb")
        pc = ph.ps("pc")
        block = ph.block()

        loads = [(raw[:, k, :], d[w]) for k, w in enumerate(WEIGHTS)]
        loads += [(r[k][:, :], col(d[k])) for k in VECTORS]
        loads += [(r[k + "_all"][:, 0:C], row(d[k]).broadcast_to([128, C])) for k in ("bias1", "bias2")]
        loads += [(r["b_out_row"][:, :], row(d["b_out"])), (r["neigh_w"][:, :], d["neigh_w"]),
                  (r["rel_a"][:, :], d["rel_emb"][0:128, :]), (r["rel_b"][:, :], d["rel_emb"][128:NR, :])]
        for l in range(2):
            for k, base in ((f"att{l + 1}_src", 0), (f"att{l + 1}_dst", H)):
                for h in range(H):
                    loads.append((asd[l][h * D:(h + 1) * D, base + h:base + h + 1],
                                  d[k][h:h + 1, :].rearrange("a n -> n a")))

        @block.sync
        def _(sp):
            sp.dma_start(dsti[:, :], d["dst"]).then_inc(dst_in, 16)
            sp.wait_ge(nd_set, 1)
            sp.dma_start(nd[0:127, :], d["dst"][1:128, 0:1]).then_inc(next_in, 16)
            sp.wait_ge(zeroed, 8)
            for o, i_ in loads:
                sp.dma_start(o, i_).then_inc(loaded, 16)
            sp.dma_start(t["last_edge"][0:NP, :].rearrange("(p e) a -> p (e a)", p=128), nulli[:, :]).then_inc(stored, 16)
            for name, lo, w in (("pg", 0, PW), ("pc", PW, CW), ("p1", PW, HW + 1), ("p2", PW, HW + 1), ("pl", PW + CW, LW)):
                sp.dma_start(t[name][NULL:NULL + 1, :], nrow[:, lo:lo + w]).then_inc(stored, 16)
            sp.wait_ge(flags_ready, 1)
            sp.dma_start(t["sidx"], sidx[:, :]).then_inc(stored, 16)
            sp.dma_start(t["eidx"], eidx[:, :]).then_inc(stored, 16)
            sp.dma_start(t["y0"][IT * SL], zeros[:, :]).then_inc(stored, 16)
            sp.wait_ge(stored, 16 * 9)

        @block.gpsimd
        def _(pool):
            st = Steps(pool, pool_step)
            nc.gpsimd.memset(nd[:, :], -1).then_inc(nd_set, 1)
            nc.gpsimd.memset(asd[0][:, :], 0.0).then_inc(zeroed, 1)
            nc.gpsimd.memset(asd[1][:, :], 0.0).then_inc(zeroed, 1)
            nc.gpsimd.memset(zeros[:, :], 0.0).then_inc(zeroed, 1)
            nc.gpsimd.memset(r["bias1_all"][:, :], 0.0).then_inc(zeroed, 1)
            nc.gpsimd.memset(r["bias2_all"][:, :], 0.0).then_inc(zeroed, 1)
            nc.gpsimd.memset(nulli[:, :], NULL).then_inc(zeroed, 1)
            st.link(nc.gpsimd.memset(nrow[:, :], 0.0))
            nc.gpsimd.memset(nrow[:, C + H:PW], -BIG).then_inc(zeroed, 1)
            nc.gpsimd.memset(nrow[:, PW + CW + C:PW + CW + C + 1], 1.0).then_inc(zeroed, 1)
            st.link(nc.gpsimd.memset(r["ident"][:, :], 0.0))
            st.link(nc.gpsimd.affine_select(out=r["ident"][:, :], in_=r["ident"][:, :], compare_op=ALU.not_equal,
                                            fill=1.0, base=0, pattern=[[-1, 128]], channel_multiplier=1))
            st.done(nc.gpsimd.memset(ones[:, :], 1.0))
            st.done(nc.gpsimd.memset(half[:, :], 0.5))
            st.done(nc.gpsimd.memset(ones_e[:, :], 1.0))
            st.done(nc.gpsimd.memset(r["mhalf"][:, :], -0.5))
            st.done(nc.gpsimd.iota(eidx[:, :], pattern=[[1, EC]], base=0, channel_multiplier=EC))
            st.done(nc.gpsimd.iota(r["pid"][:, :], pattern=[[1, 1]], base=0, channel_multiplier=1))
            st.done(nc.gpsimd.iota(r["low"][:, :], pattern=[[1, 1]], base=0, channel_multiplier=EC))
            st.done(nc.gpsimd.iota(r["spare"][:, :], pattern=[[1, 1]], base=EP + 1, channel_multiplier=1))
            st.link(nc.gpsimd.memset(r["ones_row"][:, :], 1.0))
            st.link(nc.gpsimd.affine_select(out=ut[:, :], in_=ones[:, :], compare_op=ALU.is_gt, fill=0.0,
                                            base=0, pattern=[[1, 128]], channel_multiplier=-1))
            st.link(nc.gpsimd.affine_select(out=lt[:, :], in_=ones[:, :], compare_op=ALU.is_gt, fill=0.0,
                                            base=0, pattern=[[-1, 128]], channel_multiplier=1))
            assert st.n == POOL_SETUP
            for k in range(10):
                pool.wait_ge(ss_ready, k + 1)
                nc.gpsimd.tensor_tensor(out=nrm[:, :], in0=sq[:, :], in1=half[:, :], op=ALU.pow).then_inc(nrm_ready, 1)

        @block.tensor
        def _(pe):
            ident = r["ident"]
            pe.wait_ge(pool_step, POOL_SETUP)
            pe.wait_ge(loaded, 16 * len(loads))
            for k in range(6):
                o = pa[:, k * 128:(k + 1) * 128] if k < 4 else pb[:, (k - 4) * 128:(k - 3) * 128]
                last = nc.tensor.transpose(o, raw[:, k, :], ident[:, :])
            last.then_inc(turned, 1)
            pe.wait_ge(wt_ready, 2)
            for l in range(2):
                last = nc.tensor.matmul(pb[:, 8 * l:8 * l + 8], wt[:, 4 + l, :], asd[l][:, :], start=True, stop=True)
            last.then_inc(att_done, 1)
            pe.wait_ge(ends_ready, 2)
            for k in range(2):
                last = nc.tensor.matmul(pc[:, k * 128:(k + 1) * 128], dfb[:, k, :], ident[:, :], start=True, stop=True)
            last.then_inc(rows_done, 1)
            for h in range(10):
                pe.wait_ge(uv_ready, h + 1)
                for m in range(4):
                    w = raw if h % 2 == 0 else wt
                    last = nc.tensor.matmul(pa[:, m:m + 1], w[:, m, :], u[:, m:m + 1], start=True, stop=True)
                last.then_inc(mv_done, 1)
                pe.wait_ge(sq_ready, h + 1)
                nc.tensor.matmul(pa[:, 8:12], ones[:, :], sq[:, :], start=True, stop=True).then_inc(ss_done, 1)
            pe.wait_ge(sq_ready, 11)
            nc.tensor.matmul(pa[:, 8:12], ones[:, :], sq[:, :], start=True, stop=True).then_inc(ss_done, 1)
            pe.wait_ge(scaled, 5)
            nc.tensor.matmul(pa[:, 0:128], wbt[:, :], r["Wa"][:, :], start=True, stop=True)
            nc.tensor.matmul(pa[:, 128:129], r["Wa"][:, :], r["bo2"][:, :], start=True, stop=True).then_inc(m_done, 1)

        @block.vector
        def _(dve):
            st = Steps(dve, dve_step)
            v_ = nc.vector
            dve.wait_ge(dst_in, 16)
            dve.wait_ge(next_in, 16)
            dve.wait_ge(pool_step, POOL_SETUP)
            st.link(v_.tensor_copy(dstf[:, 0:EC], dsti[:, :]))
            st.link(v_.tensor_copy(dstf[:, EC:EC + 1], nd[:, :]))
            st.link(v_.tensor_tensor(isl[:, :], dstf[:, 0:EC], dstf[:, 1:EC + 1], ALU.not_equal))
            st.link(v_.tensor_scalar(real[:, :], dstf[:, 0:EC], float(N), None, ALU.is_lt))
            st.link(v_.tensor_tensor(isl[:, :], isl[:, :], real[:, :], ALU.mult))
            st.link(v_.tensor_copy(sidf[:, :], eidx[:, :]))
            st.link(v_.tensor_scalar(sidf[:, :], sidf[:, :], float(NP), None, ALU.add))
            st.link(v_.tensor_tensor(real[:, :], dstf[:, 0:EC], sidf[:, :], ALU.subtract))
            st.link(v_.tensor_tensor(real[:, :], real[:, :], isl[:, :], ALU.mult))
            st.link(v_.tensor_tensor(sidf[:, :], sidf[:, :], real[:, :], ALU.add))
            v_.tensor_copy(sidx[:, :], sidf[:, :]).then_inc(flags_ready, 1)
            same, fresh = r["same"], r["fresh"]
            st.link(v_.tensor_tensor(same[:, 1:EC], dstf[:, 1:EC], dstf[:, 0:EC - 1], ALU.is_equal))
            st.link(v_.memset(same[:, 0:1], 0.0))
            st.link(v_.tensor_scalar(fresh[:, :], same[:, :], -1.0, BIG, ALU.add, ALU.mult))
            st.link(v_.tensor_tensor_scan(r["cnt"][:, :], same[:, :], ones_e[:, :], 0.0, ALU.mult, ALU.add))
            st.link(v_.tensor_copy(r["dfirst"][:, :], dsti[:, 0:1]))
            v_.tensor_copy(dfb[:, 0, :], dstf[:, 0:1].broadcast_to([128, 128])).then_inc(ends_ready, 1)
            v_.tensor_copy(dfb[:, 1, :], dstf[:, EC - 1:EC].broadcast_to([128, 128])).then_inc(ends_ready, 1)

            dve.wait_ge(turned, 1)
            v_.tensor_copy(wt[:, 0:4, :], pa[:, :].rearrange("p (k n) -> p k n", k=4)).then_inc(wt_ready, 1)
            v_.tensor_copy(wt[:, 4:6, :], pb[:, 0:256].rearrange("p (k n) -> p k n", k=2)).then_inc(wt_ready, 1)
            dve.wait_ge(att_done, 1)
            for l in range(2):
                st.link(v_.tensor_copy(r[f"W{l + 1}e"][:, 0:C], raw[:, 4 + l, :]))
                st.link(v_.tensor_copy(r[f"W{l + 1}e"][:, C:GW], pb[:, 8 * l:8 * l + 8]))
            st.link(v_.tensor_copy(r["pidf"][:, 0:1], r["pid"][:, :]))
            st.link(v_.tensor_scalar(r["pidf"][:, 1:2], r["pidf"][:, 0:1], 128.0, None, ALU.add))
            dve.wait_ge(rows_done, 1)
            st.link(v_.scalar_tensor_tensor(r["carry"][:, :], pc[:, 0:128], dstf[:, EC - 1:EC], ut[:, :],
                                            ALU.is_equal, ALU.mult))
            st.link(v_.scalar_tensor_tensor(r["carry_mask"][:, :], pc[:, 128:256], dstf[:, 0:1], lt[:, :],
                                            ALU.is_equal, ALU.mult))
            st.link(v_.reduce_max(r["chained"][:, :], r["carry_mask"][:, :], AX.X))
            st.link(v_.tensor_scalar(r["carry_mask"][:, :], r["carry_mask"][:, :], -1.0, BIG, ALU.add, ALU.mult))
            v_.memset(u[:, :], float(1.0 / np.sqrt(np.float32(C)))).then_inc(uv_ready, 1)
            for h in range(10):
                dve.wait_ge(mv_done, h + 1)
                st.link(v_.tensor_copy(x[:, :], pa[:, 0:4]))
                v_.tensor_tensor(sq[:, :], x[:, :], x[:, :], ALU.mult).then_inc(sq_ready, 1)
                dve.wait_ge(ss_done, h + 1)
                v_.tensor_copy(sq[:, :], pa[:, 8:12]).then_inc(ss_ready, 1)
                dve.wait_ge(nrm_ready, h + 1)
                st.link(v_.tensor_scalar(nrm[:, :], nrm[:, :], 1e-12, None, ALU.add))
                st.link(v_.reciprocal(rn[:, :], nrm[:, :]))
                v_.tensor_tensor(u[:, :], x[:, :], rn[:, :], ALU.mult).then_inc(uv_ready, 1)
            dve.wait_ge(uv_ready, 11)
            v_.tensor_tensor(sq[:, :], u[:, :], x[:, :], ALU.mult).then_inc(sq_ready, 1)
            dve.wait_ge(ss_done, 11)
            st.link(v_.reciprocal(rn[:, :], pa[:, 8:12]))
            for o, src, m in ((r["W_in"], raw[:, 0, :], 0), (r["Wa"], raw[:, 1, :], 1), (r["Wb"], raw[:, 2, :], 2),
                              (wbt, wt[:, 2, :], 2), (r["W_out"], raw[:, 3, :], 3)):
                v_.tensor_scalar(o[:, :], src, rn[:, m:m + 1], None, ALU.mult).then_inc(scaled, 1)
            dve.wait_ge(m_done, 1)
            st.link(v_.tensor_copy(r["WbWa"][:, :], pa[:, 0:128]))
            st.link(v_.tensor_copy(vec[:, :], pa[:, 128:129]))
            for k in range(2 * ODE_STEPS + 1):
                st.link(v_.scalar_tensor_tensor(r["tanh_bias"][:, k:k + 1], vec[:, :], k * DT / 2, r["bo1"][:, :],
                                                ALU.mult, ALU.add))



def value(eng, v):
    return v if isinstance(v, int) else eng.snap(v)


def node_rows(ap, i, s, slots=SL):
    v = ap.rearrange("(g p a) c -> g p (a c)", p=128, a=A)
    g = i * slots + s
    return v[g] if isinstance(g, int) else v[bass.ds(g, 1)].rearrange("o p f -> (o p) f")


def edge_columns(ap, i, s, slots=SL):
    j = (i * slots + s) * A
    return ap[:, j:j + A] if isinstance(j, int) else ap[:, bass.ds(j, A)]


def edge_rows(ap, i, s, lo=0, hi=None):
    v = ap[0:EP, :].rearrange("(p j) c -> p j c", p=128)
    hi = ap.shape[1] if hi is None else hi
    j = (i * SL + s) * A
    return v[:, j:j + A, lo:hi] if isinstance(j, int) else v[:, bass.ds(j, A), lo:hi]


def turned_rows(ap, i, s, slots=SL):
    g = i * slots + s
    return ap[g] if isinstance(g, int) else ap[bass.ds(g, 1)].rearrange("o p f -> (o p) f")


def at(ap):
    return bass.IndirectOffsetOnAxis(ap=ap, axis=0)


def over(v, n):
    return v.unsqueeze(3).broadcast_to(list(v.shape) + [n])


NORM_STEPS = SL + 1 + 12


def norm_tiles(ph):
    tiles = {k: ph.sb(k, [128, SL * A]) for k in ("var", "half", "sq", "rstd", "shift")}
    tiles["stats"] = ph.sb("stats", [128, SL * A, 6])
    tiles["mv"] = ph.sb("mv", [128, SL * A, 2])
    return tiles


def row_stats(nc, st, norms, rows, s):
    for a in range(A):
        last = nc.vector.bn_stats(norms["stats"][:, s * A + a, :], rows[:, a, :])
    st.done(last)


def row_norms(nc, st, pace, norms, shift_ready):
    v_ = nc.vector
    var, half, sq, y = (norms[k][:, :] for k in ("var", "half", "sq", "rstd"))
    st.wait()
    pace.tick()
    for k in range(SL * A):
        last = v_.bn_aggr(norms["mv"][:, k, :], norms["stats"][:, k, :])
    st.link(last)
    st.link(v_.tensor_scalar(var, norms["mv"][:, :, 1], EPS, None, ALU.add))
    st.link(v_.tensor_scalar(half.bitcast(I32), var.bitcast(I32), 1, None, ALU.logical_shift_right))
    st.link(v_.tensor_scalar(y.bitcast(I32), half.bitcast(I32), -1.0, float(0x5F3759DF), ALU.mult, ALU.add))
    for _ in range(3):
        st.link(v_.tensor_tensor(sq, y, y, ALU.mult))
        st.link(v_.scalar_tensor_tensor(half, sq, -0.5, var, ALU.mult, ALU.mult))
        st.link(v_.scalar_tensor_tensor(y, half, 1.5, y, ALU.add, ALU.mult))
    v_.scalar_tensor_tensor(norms["shift"][:, :], norms["mv"][:, :, 0], -1.0, y, ALU.mult, ALU.mult).then_inc(shift_ready, 1)


def normalize(nc, norms, out, rows, s, func, ready):
    for a in range(A):
        k = s * A + a
        last = nc.scalar.activation(out[:, a, :], rows[:, a, :], func, bias=norms["shift"][:, k:k + 1],
                                    scale=norms["rstd"][:, k:k + 1])
    last.then_inc(ready, 1)


def evacuate(nc, st, g, pg, pt, bias, ed, g_ready):
    st.done(nc.vector.tensor_tensor(g[:, 0:3, :], pg[:, 0:3 * GW].rearrange("p (a c) -> p a c", a=3),
                                    bias[:, :].unsqueeze(1).broadcast_to([128, 3, GW]), ALU.add))
    st.link(nc.vector.tensor_tensor(g[:, 3, :], pt[:, 0:GW], bias[:, :], ALU.add))
    nc.vector.tensor_copy(ed[:, :, :], g[:, :, C + H:GW]).then_inc(g_ready, 1)


def project(nc, pg, pt, ht, w, g_done):
    for a in range(A):
        o = pg[:, a * GW:(a + 1) * GW] if a < 3 else pt[:, 0:GW]
        last = nc.tensor.matmul(o, ht[:, a * 128:(a + 1) * 128], w[:, :], start=True, stop=True)
    last.then_inc(g_done, 1)


def node_in(nc, t, d, r):
    with Phase(nc, "ni") as ph:
        x_in = ph.sems("x_in")
        idx_in = ph.sems("idx_in")
        scattered = ph.sems("scattered")
        step = ph.sem("dve_step")
        shift_ready = ph.sem("shift_ready")
        xn_ready = ph.sems("xn_ready")
        turned = ph.sems("turned")
        xt_ready = ph.sems("xt_ready")
        h_done = ph.sems("h_done")
        gelu_done = ph.sems("gelu_done")
        g_done = ph.sems("g_done")
        g_ready = ph.sems("g_ready")
        stored = ph.sems("stored")
        dve_pace = ph.sem("dve_pace")
        pool_pace = ph.sem("pool_pace")

        x = ph.sbs("x", [128, A, C])
        xn = ph.sbs("xn", [128, A, C])
        norms = norm_tiles(ph)
        xt = ph.sbs("xt", [128, G])
        ht = ph.sbs("ht", [128, G])
        g = ph.sbs("g", [128, A, GW])
        ed = ph.sbs("ed", [128, A, H])
        sidx = ph.sbs("sidx", [128, A], I32)
        eidx = ph.sbs("eidx", [128, A], I32)
        pt = ph.pss("pt")
        pg = ph.pss("pg")
        block = ph.block()
        FIRST, K = NORM_STEPS, NORM_STEPS + 2 * SL

        @block.sync
        def _(sp):
            def load_x(i, s):
                sp.dma_start(x[s][:, :, :].rearrange("p a c -> p (a c)"), node_rows(d["x"], i, s)).then_inc(x_in[s], 16)

            def load_idx(i, s):
                sp.dma_start(sidx[s][:, :], edge_columns(t["sidx"], i, s)).then_inc(idx_in[s], 16)
                sp.dma_start(eidx[s][:, :], edge_columns(t["eidx"], i, s)).then_inc(idx_in[s], 16)

            def store(i, s):
                sp.dma_start(node_rows(t["g"], i, s), g[s][:, :, :].rearrange("p a c -> p (a c)")).then_inc(stored[s], 16)
                sp.dma_start(node_rows(t["ed"], i, s), ed[s][:, :, :].rearrange("p a c -> p (a c)")).then_inc(stored[s], 16)

            def body(i):
                seen, used = value(sp, i + 1), value(sp, i * 64 + 64)
                if not isinstance(i, int):
                    before, was = sp.snap(i), sp.snap(i - 1)
                    for s in range(SL):
                        sp.wait_ge(g_ready[s], before)
                        store(was, s)
                for s in range(SL):
                    sp.wait_ge(xn_ready[s], seen)
                    load_x(i + 1, s)
                for s in range(SL):
                    sp.wait_ge(scattered[s], used)
                    load_idx(i + 1, s)

            for s in range(SL):
                load_x(0, s)
                load_idx(0, s)
            body(0)
            with sp.Fori(1, IT - 1) as i:
                body(i)
            for i in (IT - 2, IT - 1):
                for s in range(SL):
                    sp.wait_ge(g_ready[s], i + 1)
                    store(i, s)
            for s in range(SL):
                sp.wait_ge(stored[s], IT * 32)

        @block.gpsimd
        def _(pool):
            pace = Pace(pool, pool_pace)

            def body(i):
                for s in range(SL):
                    pool.wait_ge(idx_in[s], i * 32 + 32)
                    pace.tick()
                    for a in range(A):
                        nc.gpsimd.indirect_dma_start(out=t["last_edge"], out_offset=at(sidx[s][:, a:a + 1]),
                                                     in_=eidx[s][:, a:a + 1], in_offset=None).then_inc(scattered[s], 16)

            rounds(pool, body)
            for s in range(SL):
                pool.wait_ge(scattered[s], IT * 64)

        @block.vector
        def _(dve):
            pace = Pace(dve, dve_pace)

            def body(i):
                st = Steps(dve, step, i, K, 0 if isinstance(i, int) else FIRST - K)
                for s in range(SL):
                    dve.wait_ge(x_in[s], i * 16 + 16)
                    row_stats(nc, st, norms, x[s], s)
                if not isinstance(i, int):
                    for s in range(SL):
                        dve.wait_ge(xn_ready[s], i)
                row_norms(nc, st, pace, norms, shift_ready)
                if not isinstance(i, int):
                    for s in range(SL):
                        dve.wait_ge(g_done[s], i)
                        evacuate(nc, st, g[s], pg[s], pt[s], r["bias1_all"], ed[s], g_ready[s])

            rounds(dve, body)
            st = Steps(dve, step, IT, K, FIRST - K)
            for s in range(SL):
                dve.wait_ge(g_done[s], IT)
                evacuate(nc, st, g[s], pg[s], pt[s], r["bias1_all"], ed[s], g_ready[s])

        @block.tensor
        def _(pe):
            def body(i):
                for s in range(SL):
                    pe.wait_ge(xn_ready[s], i + 1)
                    if not isinstance(i, int):
                        pe.wait_ge(g_ready[s], i)
                    for a in range(A):
                        last = nc.tensor.transpose(pt[s][:, a * 128:(a + 1) * 128], xn[s][:, a, :], r["ident"][:, :])
                    last.then_inc(turned[s], 1)
                for s in range(SL):
                    pe.wait_ge(xt_ready[s], i + 1)
                    nc.tensor.matmul(pt[s][:, :], r["W_in"][:, :], xt[s][:, :], start=True, stop=True).then_inc(h_done[s], 1)
                for s in range(SL):
                    pe.wait_ge(gelu_done[s], i + 1)
                    if not isinstance(i, int):
                        pe.wait_ge(stored[s], i * 32)
                    project(nc, pg[s], pt[s], ht[s], r["W1e"], g_done[s])

            rounds(pe, body)

        @block.scalar
        def _(act):
            def body(i):
                act.wait_ge(shift_ready, i + 1)
                for s in range(SL):
                    if not isinstance(i, int):
                        act.wait_ge(turned[s], i)
                    normalize(nc, norms, xn[s], x[s], s, ACT.Relu, xn_ready[s])
                for s in range(SL):
                    act.wait_ge(turned[s], i + 1)
                    nc.scalar.activation(xt[s][:, :], pt[s][:, :], ACT.Copy).then_inc(xt_ready[s], 1)
                for s in range(SL):
                    act.wait_ge(h_done[s], i + 1)
                    nc.scalar.activation(ht[s][:, :], pt[s][:, :], ACT.Gelu_apprx_tanh,
                                         bias=r["b_in"][:, 0:1]).then_inc(gelu_done[s], 1)

            rounds(act, body)


def fix_index(nc, t, d, r):
    with Phase(nc, "fi") as ph:
        got = ph.sem("got")
        step = ph.sem("dve_step")
        lasti = ph.sb("lasti", [128, 1], I32)
        f = [ph.sb(f"f{k}", [128, 1]) for k in range(6)]
        block = ph.block()

        @block.gpsimd
        def _(pool):
            nc.gpsimd.indirect_dma_start(out=lasti[:, :], out_offset=None, in_=t["last_edge"][0:NP, :],
                                         in_offset=at(r["dfirst"][:, :])).then_inc(got, 16)

        @block.vector
        def _(dve):
            st = Steps(dve, step)
            v_ = nc.vector
            dve.wait_ge(got, 16)
            last, low, ok, a, b, c = (x[:, :] for x in f)
            st.link(v_.tensor_copy(last, lasti[:, :]))
            st.link(v_.tensor_copy(low, r["low"][:, :]))
            st.link(v_.tensor_tensor(ok, last, low, ALU.is_ge))
            st.link(v_.tensor_scalar(a, low, float(EC), None, ALU.add))
            st.link(v_.tensor_tensor(a, last, a, ALU.is_lt))
            st.link(v_.tensor_tensor(ok, ok, a, ALU.mult))
            st.link(v_.tensor_tensor(ok, ok, r["chained"][:, :], ALU.mult))
            st.link(v_.tensor_scalar(b, last, -float(NULL), None, ALU.add))
            st.link(v_.tensor_tensor(b, b, ok, ALU.mult))
            st.link(v_.tensor_scalar(b, b, float(NULL), None, ALU.add))
            st.link(v_.tensor_copy(r["fix_get"][:, :], b))
            st.link(v_.tensor_copy(c, r["spare"][:, :]))
            st.link(v_.tensor_tensor(b, last, c, ALU.subtract))
            st.link(v_.tensor_tensor(b, b, ok, ALU.mult))
            st.link(v_.tensor_tensor(b, b, c, ALU.add))
            st.link(v_.tensor_copy(r["fix_put"][:, :], b))


def gat_edges(nc, t, d, r, tag, g_name, ed_name):
    with Phase(nc, tag) as ph:
        idx_in = ph.sems("idx_in")
        rows_in = ph.sems("rows_in")
        step = ph.sem("dve_step")
        start = ph.sem("start")
        arg_ready = ph.sems("arg_ready")
        exp_done = ph.sems("exp_done")
        row_ready = ph.sems("row_ready")
        stored = ph.sems("stored")

        srci = ph.sbs("srci", [128, A], I32)
        dsti = ph.sbs("dsti", [128, A], I32)
        rows = ph.sbs("rows", [128, A, GW])
        edst = ph.sbs("edst", [128, A, H])
        e = ph.sbs("e", [128, A, H])
        base = ph.sbs("base", [128, A, H])
        arg = ph.sbs("arg", [128, 2, A, H])
        wts = ph.sbs("wts", [128, 2, A, H])
        gw = ph.sbs("gw", [128, A, C])
        tmp = ph.sb("tmp", [128, C])
        out = ph.sbs("out", [128, A, PW])
        block = ph.block()
        K = SL * 18

        @block.sync
        def _(sp):
            def load(i, s, js=None):
                sp.dma_start(srci[s][:, :], edge_columns(d["src"], i, s)).then_inc(idx_in[s], 16)
                sp.dma_start(dsti[s][:, :], edge_columns(d["dst"], i, s)).then_inc(idx_in[s], 16)

            def store(i, s):
                sp.dma_start(edge_rows(t["pg"], i, s), out[s][:, :, :]).then_inc(stored[s], 16)

            for s in range(SL):
                load(0, s)
            with sp.Fori(0, IT - 1) as i:
                ready = sp.snap(i + 1)
                for s in range(SL):
                    sp.wait_ge(row_ready[s], ready)
                    load(i + 1, s)
                    store(i, s)
            for s in range(SL):
                sp.wait_ge(row_ready[s], IT)
                store(IT - 1, s)
            for s in range(SL):
                sp.wait_ge(stored[s], IT * 16)

        @block.gpsimd
        def _(pool):
            pace = Pace(pool, ph.sem("pool_pace"))

            def body(i):
                for s in range(SL):
                    if not isinstance(i, int):
                        pool.wait_ge(row_ready[s], i)
                    pool.wait_ge(idx_in[s], i * 32 + 32)
                    pace.tick()
                    for a in range(A):
                        nc.gpsimd.indirect_dma_start(out=rows[s][:, a, :], out_offset=None, in_=t[g_name],
                                                     in_offset=at(srci[s][:, a:a + 1])).then_inc(rows_in[s], 16)
                    for a in range(A):
                        nc.gpsimd.indirect_dma_start(out=edst[s][:, a, :], out_offset=None, in_=t[ed_name],
                                                     in_offset=at(dsti[s][:, a:a + 1])).then_inc(rows_in[s], 16)

            rounds(pool, body)

        @block.scalar
        def _(act):
            def body(i):
                for s in range(SL):
                    act.wait_ge(arg_ready[s], i + 1)
                    nc.scalar.activation(wts[s][:, :, :, :], arg[s][:, :, :, :], ACT.Exp).then_inc(exp_done[s], 1)

            rounds(act, body)

        @block.vector
        def _(dve):
            v_ = nc.vector
            before = out[SL - 1]
            v_.memset(before[:, A - 1, 0:C + H], 0.0).then_inc(start, 1)
            v_.memset(before[:, A - 1, C + H:PW], -BIG).then_inc(start, 1)
            dve.wait_ge(start, 2)

            def body(i):
                st = Steps(dve, step, i, K)
                for s in range(SL):
                    o, prev = out[s], out[(s - 1) % SL][:, A - 1, :]
                    m = o[:, :, C + H:PW]
                    fresh = edge_columns(r["fresh"], i, s)
                    dve.wait_ge(rows_in[s], i * 128 + 128)
                    if not isinstance(i, int):
                        dve.wait_ge(stored[s], i * 16)
                    st.link(v_.tensor_tensor(e[s][:, :, :], rows[s][:, :, C:C + H], edst[s][:, :, :], ALU.add))
                    st.link(v_.scalar_tensor_tensor(e[s][:, :, :], e[s][:, :, :], 0.2, e[s][:, :, :], ALU.mult, ALU.max))
                    for h in range(H):
                        last = v_.tensor_tensor_scan(m[:, :, h], fresh, e[s][:, :, h], prev[:, C + H + h:C + H + h + 1],
                                                     ALU.add, ALU.max)
                    st.link(last)
                    st.done(v_.tensor_tensor(base[s][:, 0:1, :], prev[:, C + H:PW].unsqueeze(1),
                                             fresh[:, 0:1].unsqueeze(2).broadcast_to([128, 1, H]), ALU.add))
                    st.link(v_.tensor_tensor(base[s][:, 1:A, :], m[:, 0:A - 1, :],
                                             fresh[:, 1:A].unsqueeze(2).broadcast_to([128, A - 1, H]), ALU.add))
                    st.done(v_.tensor_tensor(arg[s][:, 0, :, :], base[s][:, :, :], m, ALU.subtract))
                    v_.tensor_tensor(arg[s][:, 1, :, :], e[s][:, :, :], m, ALU.subtract).then_inc(arg_ready[s], 1)
                    dve.wait_ge(exp_done[s], i + 1)
                    keep, w = wts[s][:, 0, :, :], wts[s][:, 1, :, :]
                    for h in range(H):
                        st.done(v_.tensor_tensor_scan(o[:, :, C + h], keep[:, :, h], w[:, :, h], prev[:, C + h:C + h + 1],
                                                      ALU.mult, ALU.add))
                    st.link(v_.tensor_tensor(gw[s][:, :, :].rearrange("p a (h d) -> p a h d", h=H),
                                             rows[s][:, :, 0:C].rearrange("p a (h d) -> p a h d", h=H),
                                             over(w, D), ALU.mult))
                    for a in range(A):
                        was = prev[:, 0:C] if a == 0 else o[:, a - 1, 0:C]
                        st.link(v_.tensor_tensor(tmp[:, :].rearrange("p (h d) -> p h d", h=H),
                                                 was.rearrange("p (h d) -> p h d", h=H),
                                                 keep[:, a, :].unsqueeze(2).broadcast_to([128, H, D]), ALU.mult))
                        ins = v_.tensor_tensor(o[:, a, 0:C], tmp[:, :], gw[s][:, a, :], ALU.add)
                        if a < A - 1:
                            st.link(ins)
                        else:
                            ins.then_inc(row_ready[s], 1)
                            dve.wait_ge(row_ready[s], i + 1)
                assert st.n == K, st.n

            rounds(dve, body)
            st = Steps(dve, start, base=2)
            st.link(v_.tensor_copy(r["tail"][:, 0:PW], out[SL - 1][:, A - 1, :]))


def softmax_fix(nc, t, d, r, tag, name, heads, width):
    per = C // heads
    sums, tops = C, C + heads
    with Phase(nc, tag) as ph:
        step = ph.sem("dve_step")
        spread = ph.sem("spread")
        tops_done = ph.sem("tops_done")
        arg_ready = ph.sem("arg_ready")
        exp_done = ph.sem("exp_done")
        w_ready = ph.sem("w_ready")
        cin_done = ph.sem("cin_done")
        got = ph.sem("got")
        fixed = ph.sem("fixed")
        put = ph.sem("put")
        mb = ph.sb("mb", [128, heads, 128])
        masked = ph.sb("masked", [128, 128])
        mc = ph.sb("mc", [128, heads])
        arg = ph.sb("arg", [128, heads, 128])
        w = ph.sb("w", [128, heads, 128])
        old = ph.sb("old", [128, width])
        arg2 = ph.sb("arg2", [128, 2, heads])
        f = ph.sb("f", [128, 2, heads])
        t1 = ph.sb("t1", [128, C])
        t2 = ph.sb("t2", [128, C])
        pm = ph.ps("pm")
        pq = ph.ps("pq")
        pc = ph.ps("pc")
        block = ph.block()
        tail = r["tail"]

        @block.gpsimd
        def _(pool):
            nc.gpsimd.indirect_dma_start(out=old[:, :], out_offset=None, in_=t[name][0:EP + 1, :],
                                         in_offset=at(r["fix_get"][:, :])).then_inc(got, 16)
            pool.wait_ge(fixed, 1)
            nc.gpsimd.indirect_dma_start(out=t[name], out_offset=at(r["fix_put"][:, :]), in_=old[:, :],
                                         in_offset=None).then_inc(put, 16)
            pool.wait_ge(put, 16)

        @block.tensor
        def _(pe):
            for k, p in ((0, pm), (1, pq)):
                pe.wait_ge(spread, heads * (k + 1))
                for h in range(heads):
                    last = nc.tensor.matmul(p[:, h * 128:(h + 1) * 128], mb[:, h, :], r["ident"][:, :], start=True, stop=True)
                last.then_inc(tops_done, 1)
            pe.wait_ge(w_ready, heads)
            for h in range(heads):
                nc.tensor.matmul(pc[:, h * per:(h + 1) * per], w[:, h, :], tail[:, h * per:(h + 1) * per], start=True, stop=True)
                last = nc.tensor.matmul(pc[:, C + h:C + h + 1], w[:, h, :], tail[:, sums + h:sums + h + 1], start=True, stop=True)
            last.then_inc(cin_done, 1)

        @block.scalar
        def _(act):
            act.wait_ge(arg_ready, heads)
            nc.scalar.activation(w[:, :, :], arg[:, :, :], ACT.Exp).then_inc(exp_done, 1)
            act.wait_ge(arg_ready, heads + 2)
            nc.scalar.activation(f[:, :, :], arg2[:, :, :], ACT.Exp).then_inc(exp_done, 1)

        @block.vector
        def _(dve):
            st = Steps(dve, step)
            v_ = nc.vector
            for h in range(heads):
                v_.tensor_copy(mb[:, h, :], tail[:, tops + h:tops + h + 1].broadcast_to([128, 128])).then_inc(spread, 1)
            dve.wait_ge(tops_done, 1)
            for h in range(heads):
                st.link(v_.tensor_tensor(masked[:, :], pm[:, h * 128:(h + 1) * 128], r["carry_mask"][:, :], ALU.add))
                st.link(v_.reduce_max(mc[:, h:h + 1], masked[:, :], AX.X))
            for h in range(heads):
                v_.tensor_copy(mb[:, h, :], mc[:, h:h + 1].broadcast_to([128, 128])).then_inc(spread, 1)
            dve.wait_ge(tops_done, 2)
            for h in range(heads):
                st.link(v_.tensor_scalar(arg[:, h, :], pq[:, h * 128:(h + 1) * 128], tail[:, tops + h:tops + h + 1], -1.0,
                                         ALU.subtract, ALU.mult))
                v_.tensor_scalar(arg[:, h, :], arg[:, h, :], 0.0, None, ALU.min).then_inc(arg_ready, 1)
            dve.wait_ge(exp_done, 1)
            for h in range(heads):
                v_.tensor_tensor(w[:, h, :], w[:, h, :], r["carry"][:, :], ALU.mult).then_inc(w_ready, 1)
            dve.wait_ge(got, 16)
            om = old[:, tops:tops + heads]
            st.link(v_.tensor_tensor(t1[:, 0:heads], om, mc[:, :], ALU.max))
            v_.tensor_tensor(arg2[:, 0, :], om, t1[:, 0:heads], ALU.subtract).then_inc(arg_ready, 1)
            v_.tensor_tensor(arg2[:, 1, :], mc[:, :], t1[:, 0:heads], ALU.subtract).then_inc(arg_ready, 1)
            dve.wait_ge(arg_ready, heads + 2)
            st.link(v_.tensor_copy(om, t1[:, 0:heads]))
            dve.wait_ge(exp_done, 2)
            dve.wait_ge(cin_done, 1)
            for lo, n in ((0, C), (sums, heads)):
                k = n // heads
                f0, f1 = (f[:, q, :].unsqueeze(2).broadcast_to([128, heads, k]) for q in (0, 1))

                def cut(v):
                    return v.rearrange("p (h k) -> p h k", h=heads)

                st.link(v_.tensor_tensor(cut(t1[:, 0:n]), cut(old[:, lo:lo + n]), f0, ALU.mult))
                st.link(v_.tensor_tensor(cut(t2[:, 0:n]), cut(pc[:, lo:lo + n]), f1, ALU.mult))
                ins = v_.tensor_tensor(old[:, lo:lo + n], t1[:, 0:n], t2[:, 0:n], ALU.add)
                if lo == 0:
                    st.link(ins)
                else:
                    ins.then_inc(fixed, 1)


def gat_args(nc, st, near, own, sc, arg, arg_ready):
    v_ = nc.vector
    top = near[:, :, C + H:PW]
    st.link(v_.tensor_tensor(sc[:, 0, :, :], own[:, :, C:C + H], own[:, :, C + H:GW], ALU.add))
    st.link(v_.scalar_tensor_tensor(sc[:, 0, :, :], sc[:, 0, :, :], 0.2, sc[:, 0, :, :], ALU.mult, ALU.max))
    st.link(v_.tensor_tensor(sc[:, 1, :, :], top, sc[:, 0, :, :], ALU.max))
    st.done(v_.tensor_tensor(arg[:, 0, :, :], top, sc[:, 1, :, :], ALU.subtract))
    v_.tensor_tensor(arg[:, 1, :, :], sc[:, 0, :, :], sc[:, 1, :, :], ALU.subtract).then_inc(arg_ready, 1)


def gat_weights(nc, st, near, sc, f):
    v_ = nc.vector
    st.link(v_.tensor_tensor(sc[:, 2, :, :], near[:, :, C:C + H], f[:, 0, :, :], ALU.mult))
    st.link(v_.tensor_tensor(sc[:, 2, :, :], sc[:, 2, :, :], f[:, 1, :, :], ALU.add))
    st.link(v_.tensor_scalar(sc[:, 2, :, :], sc[:, 2, :, :], 1e-16, None, ALU.add))
    st.link(v_.reciprocal(sc[:, 3, :, :], sc[:, 2, :, :]))
    st.done(v_.tensor_tensor(sc[:, 4, :, :], f[:, 0, :, :], sc[:, 3, :, :], ALU.mult))
    st.link(v_.tensor_tensor(sc[:, 5, :, :], f[:, 1, :, :], sc[:, 3, :, :], ALU.mult))


def gat_mix(nc, st, near, own, sc, s, mixed):
    v_ = nc.vector
    rows = slice(s * A, s * A + A)

    def heads(v):
        return v[:, rows, 0:C].rearrange("p a (h d) -> p a h d", h=H)

    st.done(v_.tensor_tensor(heads(near), heads(near), over(sc[:, 4, rows, :], D), ALU.mult))
    st.link(v_.tensor_tensor(heads(own), heads(own), over(sc[:, 5, rows, :], D), ALU.mult))
    v_.tensor_tensor(own[:, rows, 0:C], own[:, rows, 0:C], near[:, rows, 0:C], ALU.add).then_inc(mixed, 1)


def gather_rows(nc, out, src, idx, arrived):
    for a in range(A):
        nc.gpsimd.indirect_dma_start(out=out[:, a, :], out_offset=None, in_=src, in_offset=at(idx[:, a:a + 1])).then_inc(arrived, 16)


def gat_nodes(nc, t, d, r, layer):
    own_rows, gain, shift = (("g", "g1", "be1"), ("g2", "g2", "be2"))[layer - 1]
    project_next = layer == 1
    with Phase(nc, f"gn{layer}") as ph:
        own_in = ph.sems("own_in")
        idx_in = [ph.sems(f"idx_in{b}_") for b in range(2)]
        near_in = [ph.sems(f"near_in{b}_") for b in range(2)]
        step = ph.sem("dve_step")
        arg_ready = ph.sem("arg_ready")
        exp_done = ph.sem("exp_done")
        shift_ready = ph.sem("shift_ready")
        mixed = ph.sems("mixed")
        gelu_done = ph.sems("gelu_done")
        xn_ready = ph.sems("xn_ready")
        turned = ph.sems("turned")
        ht_ready = ph.sems("ht_ready")
        g_done = ph.sems("g_done")
        g_ready = ph.sems("g_ready")
        stored = ph.sems("stored")
        dve_pace = ph.sem("dve_pace")
        pool_pace = ph.sem("pool_pace")

        own = ph.sb("own", [128, SL * A, GW])
        near = ph.sbs("near", [128, SL * A, PW], n=2)
        idx = [ph.sbs(f"idx{b}_", [128, A], I32) for b in range(2)]
        sc = ph.sb("sc", [128, 6, SL * A, H])
        arg = ph.sb("arg", [128, 2, SL * A, H])
        f = ph.sb("f", [128, 2, SL * A, H])
        y = ph.sbs("y", [128, A, C])
        norms = norm_tiles(ph)
        ht = ph.sbs("ht", [128, G])
        g = ph.sbs("g", [128, A, GW])
        ed = ph.sbs("ed", [128, A, H])
        pt = ph.pss("pt")
        pg = ph.pss("pg")
        block = ph.block()
        FIRST = NORM_STEPS + 10 + SL * 2
        K = FIRST + 2 * SL * project_next
        STORES = 32 if project_next else 16

        @block.sync
        def _(sp):
            def load_idx(i, b, s):
                sp.dma_start(idx[b][s][:, :], node_rows(t["last_edge"][0:NP, :], i, s)).then_inc(idx_in[b][s], 16)

            def load_own(i, s):
                sp.dma_start(own[:, s * A:s * A + A, :].rearrange("p a c -> p (a c)"), node_rows(t[own_rows], i, s)).then_inc(own_in[s], 16)

            def store(i, s):
                if project_next:
                    sp.dma_start(node_rows(t["g2"], i, s), g[s][:, :, :].rearrange("p a c -> p (a c)")).then_inc(stored[s], 16)
                    sp.dma_start(node_rows(t["ed2"], i, s), ed[s][:, :, :].rearrange("p a c -> p (a c)")).then_inc(stored[s], 16)
                else:
                    sp.dma_start(turned_rows(t["y0"], i, s), ht[s][:, :]).then_inc(stored[s], 16)

            result = g_ready if project_next else ht_ready

            def body(i, b):
                gathered, used, before, was = (value(sp, v) for v in (landed(i - 1, 1 - b, 64), i + 1, i, i - 1))
                for s in range(SL):
                    if later(i) and not final(i):
                        sp.wait_ge(near_in[1 - b][s], gathered)
                        load_idx(i + 1, 1 - b, s)
                for s in range(SL):
                    if later(i):
                        sp.wait_ge(result[s], before)
                        store(was, s)
                for s in range(SL):
                    if not final(i):
                        sp.wait_ge(gelu_done[s], used)
                        load_own(i + 1, s)

            for s in range(SL):
                load_idx(0, 0, s)
                load_idx(1, 1, s)
                load_own(0, s)
            double_rounds(sp, body)
            for s in range(SL):
                sp.wait_ge(result[s], IT)
                store(IT - 1, s)
            for s in range(SL):
                sp.wait_ge(stored[s], IT * STORES)

        @block.gpsimd
        def _(pool):
            pace = Pace(pool, pool_pace)

            def body(i, b):
                for s in range(SL):
                    pool.wait_ge(idx_in[b][s], landed(i, b, 16))
                    if later(i, 2):
                        pool.wait_ge(mixed[s], i - 1)
                    pace.tick()
                    gather_rows(nc, near[b][:, s * A:s * A + A, :], t["pg"][0:EP + 1, :], idx[b][s], near_in[b][s])

            double_rounds(pool, body)

        @block.vector
        def _(dve):
            pace = Pace(dve, dve_pace)

            def body(i, b):
                st = Steps(dve, step, i, K, FIRST - K if later(i) else 0)
                for s in range(SL):
                    dve.wait_ge(own_in[s], i * 16 + 16)
                for s in range(SL):
                    dve.wait_ge(near_in[b][s], landed(i, b, 64))
                gat_args(nc, st, near[b], own, sc, arg, arg_ready)
                dve.wait_ge(exp_done, i + 1)
                gat_weights(nc, st, near[b], sc, f)
                for s in range(SL):
                    gat_mix(nc, st, near[b], own, sc, s, mixed[s])
                if project_next and later(i):
                    for s in range(SL):
                        dve.wait_ge(g_done[s], i)
                        evacuate(nc, st, g[s], pg[s], pt[s], r["bias2_all"], ed[s], g_ready[s])
                for s in range(SL):
                    dve.wait_ge(gelu_done[s], i + 1)
                    row_stats(nc, st, norms, y[s], s)
                row_norms(nc, st, pace, norms, shift_ready)
                assert st.n == (K if later(i) else FIRST), st.n

            double_rounds(dve, body)
            if project_next:
                st = Steps(dve, step, IT, K, FIRST - K)
                for s in range(SL):
                    dve.wait_ge(g_done[s], IT)
                    evacuate(nc, st, g[s], pg[s], pt[s], r["bias2_all"], ed[s], g_ready[s])

        @block.tensor
        def _(pe):
            def body(i):
                for s in range(SL):
                    pe.wait_ge(xn_ready[s], i + 1)
                    if not isinstance(i, int):
                        pe.wait_ge((g_ready if project_next else ht_ready)[s], i)
                    for a in range(A):
                        last = nc.tensor.transpose(pt[s][:, a * 128:(a + 1) * 128], y[s][:, a, :], r["ident"][:, :])
                    last.then_inc(turned[s], 1)
                if not project_next:
                    return
                for s in range(SL):
                    pe.wait_ge(ht_ready[s], i + 1)
                    if not isinstance(i, int):
                        pe.wait_ge(stored[s], i * 32)
                    project(nc, pg[s], pt[s], ht[s], r["W2e"], g_done[s])

            rounds(pe, body)

        @block.scalar
        def _(act):
            def scaled(turns):
                act.wait_ge(shift_ready, turns)
                for s in range(SL):
                    normalize(nc, norms, y[s], y[s], s, ACT.Identity, xn_ready[s])
                for s in range(SL):
                    act.wait_ge(turned[s], turns)
                    nc.scalar.activation(ht[s][:, :], pt[s][:, :], ACT.Identity, bias=r[shift][:, 0:1],
                                         scale=r[gain][:, 0:1]).then_inc(ht_ready[s], 1)

            def body(i):
                act.wait_ge(arg_ready, i + 1)
                nc.scalar.activation(f[:, :, :, :], arg[:, :, :, :], ACT.Exp).then_inc(exp_done, 1)
                if later(i):
                    scaled(i)
                for s in range(SL):
                    act.wait_ge(mixed[s], i + 1)
                    if later(i) and not project_next:
                        act.wait_ge(stored[s], i * 16)
                    nc.scalar.activation(y[s][:, :, :], own[:, s * A:s * A + A, 0:C], ACT.Gelu_apprx_tanh).then_inc(gelu_done[s], 1)

            rounds(act, body)
            scaled(IT)


def ode_nodes(nc, t, d, r):
    with Phase(nc, "od") as ph:
        y0_in = ph.sems("y0_in", OSL)
        srci_in = ph.sems("srci_in", OSL)
        look_in = ph.sems("look_in", OSL)
        look_out = ph.sems("look_out", OSL)
        y0b_ready = ph.sems("y0b_ready", OSL)
        mm_done = ph.sems("mm_done", OSL)
        z0_ready = ph.sems("z0_ready", OSL)
        t_ready = ph.sems("t_ready", OSL)
        z_ready = ph.sems("z_ready", OSL)
        tt_ready = ph.sems("tt_ready", OSL)
        ut_ready = ph.sems("ut_ready", OSL)
        v_ready = ph.sems("v_ready", OSL)
        u_ready = ph.sems("u_ready", OSL)
        y_ready = ph.sems("y_ready", OSL)
        back = ph.sems("back", OSL)
        h_part = ph.sems("h_part", OSL)
        h_ready = ph.sems("h_ready", OSL)
        stored = ph.sems("stored", OSL)
        pool_pace = ph.sem("pool_pace")

        srci = ph.sbs("srci", [128, A], I32, OSL)
        look = ph.sbs("look", [128, A], I32, OSL)
        y0 = ph.sbs("y0", [128, G], n=OSL)
        y0b = ph.sbs("y0b", [128, G], n=OSL)
        z0 = ph.sbs("z0", [128, G], n=OSL)
        zs = ph.sbs("zs", [128, G], n=OSL)
        z = ph.sbs("z", [128, G], n=OSL)
        tk = [ph.sbs(f"t{k + 1}_", [128, G], n=OSL) for k in range(4)]
        tt = ph.sbs("tt", [128, G], n=OSL)
        ut = ph.sbs("ut", [128, G], n=OSL)
        v = ph.sbs("v", [128, G], n=OSL)
        u = ph.sbs("u", [128, G], n=OSL)
        yt = ph.sbs("yt", [128, G], n=OSL)
        h = ph.sbs("h", [128, A, HW], n=OSL)
        pz = ph.pss("pz", OSL)
        pt = ph.pss("pt", 2)
        pw = ph.pss("pw", 2)
        block = ph.block()
        MM = 4 * ODE_STEPS + 1
        TT = 4 * ODE_STEPS
        ZZ = 4 * ODE_STEPS - 1

        def place(i, beat, s):
            if beat >= s:
                return None if isinstance(i, int) and i == OIT else (i, beat - s)
            return None if isinstance(i, int) and i == 0 else (i - 1, beat - s + MM)

        def beats(eng, stage):
            def body(i):
                for beat in range(MM):
                    for s in range(OSL):
                        stage(i, beat, s)

            rounds(eng, body, OIT)
            for beat in range(OSL - 1):
                for s in range(OSL):
                    stage(OIT, beat, s)

        @block.sync
        def _(sp):
            def load_y0(i, s):
                sp.dma_start(y0[s][:, :], turned_rows(t["y0"], i, s, OSL)).then_inc(y0_in[s], 16)

            def load_srci(i, s):
                sp.dma_start(srci[s][:, :], edge_columns(d["src"], i, s, OSL)).then_inc(srci_in[s], 16)

            def store_look(i, s):
                sp.dma_start(edge_columns(t["src_edge"], i, s, OSL), look[s][:, :]).then_inc(look_out[s], 16)

            def store(i, s):
                sp.dma_start(node_rows(t["h"], i, s, OSL), h[s][:, :, :].rearrange("p a c -> p (a c)")).then_inc(stored[s], 16)

            def body(i):
                turn, product, looked = value(sp, i + 1), value(sp, i * MM + 1), value(sp, i * 64 + 64)
                for s in range(OSL):
                    sp.wait_ge(y0b_ready[s], turn)
                    sp.wait_ge(mm_done[s], product)
                    load_y0(i + 1, s)
                if not isinstance(i, int):
                    before, was = sp.snap(i), sp.snap(i - 1)
                    for s in range(OSL):
                        sp.wait_ge(h_ready[s], before)
                        store(was, s)
                for s in range(OSL):
                    sp.wait_ge(look_in[s], looked)
                    store_look(i, s)
                    load_srci(i + 1, s)

            for s in range(OSL):
                load_y0(0, s)
                load_srci(0, s)
            body(0)
            with sp.Fori(1, OIT - 1) as i:
                body(i)
            for s in range(OSL):
                sp.wait_ge(h_ready[s], OIT - 1)
                store(OIT - 2, s)
            for s in range(OSL):
                sp.wait_ge(look_in[s], OIT * 64)
                store_look(OIT - 1, s)
            for s in range(OSL):
                sp.wait_ge(h_ready[s], OIT)
                store(OIT - 1, s)
            for s in range(OSL):
                sp.wait_ge(look_out[s], OIT * 16)
                sp.wait_ge(stored[s], OIT * 16)

        @block.gpsimd
        def _(pool):
            pace = Pace(pool, pool_pace)

            def look_up(i, e):
                s, a = e // A, e % A
                if a == 0:
                    pool.wait_ge(srci_in[s], i * 16 + 16)
                    if not isinstance(i, int):
                        pool.wait_ge(look_out[s], i * 16)
                    pace.tick()
                nc.gpsimd.indirect_dma_start(out=look[s][:, a:a + 1], out_offset=None, in_=t["last_edge"][0:NP, :],
                                             in_offset=at(srci[s][:, a:a + 1])).then_inc(look_in[s], 16)

            def stage(i, beat, s):
                if place(i, beat, s):
                    turn, q = place(i, beat, s)
                    n, k = divmod(q, 4)
                    if k == 0 and 0 < n < ODE_STEPS:
                        pool.wait_ge(u_ready[s], turn * ODE_STEPS + n)
                        pool.wait_ge(t_ready[s], turn * TT + q + 1)
                        nc.gpsimd.tensor_tensor(out=ut[s][:, :], in0=u[s][:, :], in1=tk[0][s][:, :],
                                                op=ALU.add).then_inc(ut_ready[s], 1)
                    if k == 2:
                        pool.wait_ge(t_ready[s], turn * TT + q + 1)
                        nc.gpsimd.tensor_tensor(out=tt[s][:, :], in0=tk[1][s][:, :], in1=tk[2][s][:, :],
                                                op=ALU.add).then_inc(tt_ready[s], 1)
                if s == OSL - 1 and 1 <= beat <= OSL * A and not (isinstance(i, int) and i == OIT):
                    look_up(i, beat - 1)

            beats(pool, stage)

        @block.vector
        def _(dve):
            v_ = nc.vector

            def arg(turn, s, q):
                n, k = divmod(q, 4)
                dve.wait_ge(mm_done[s], turn * MM + q + 1)
                if q == 1:
                    dve.wait_ge(z0_ready[s], turn + 1)
                first = z0[s] if k == 0 or n == 0 else zs[s]
                v_.scalar_tensor_tensor((zs if k == 0 else z)[s][:, :], pz[s][:, :], (DT / 6, DT / 2, DT / 2, DT)[k],
                                        first[:, :], ALU.mult, ALU.add).then_inc(z_ready[s], 1)

            def middle(turn, s, n):
                dve.wait_ge(tt_ready[s], turn * ODE_STEPS + n + 1)
                if n > 0:
                    dve.wait_ge(ut_ready[s], turn * (ODE_STEPS - 1) + n)
                before = tk[0][s] if n == 0 else ut[s]
                v_.scalar_tensor_tensor(v[s][:, :], tt[s][:, :], 2.0, before[:, :], ALU.mult, ALU.add).then_inc(v_ready[s], 1)

            def total(turn, s, n):
                dve.wait_ge(t_ready[s], turn * TT + 4 * n + 4)
                dve.wait_ge(v_ready[s], turn * ODE_STEPS + n + 1)
                v_.tensor_tensor(u[s][:, :], v[s][:, :], tk[3][s][:, :], ALU.add).then_inc(u_ready[s], 1)

            def end(turn, s):
                dve.wait_ge(mm_done[s], turn * MM + MM)
                v_.scalar_tensor_tensor(yt[s][:, :], pz[s][:, :], DT / 6, y0b[s][:, :],
                                        ALU.mult, ALU.add).then_inc(y_ready[s], 1)

            def stage(i, beat, s):
                now = place(i, beat, s)
                if now and 0 < now[1] < TT:
                    arg(now[0], s, now[1])
                    if now[1] % 4 == 3:
                        middle(now[0], s, now[1] // 4)
                elif now and now[1] == TT:
                    end(now[0], s)
                p = (s - 1) % OSL
                then = place(i, beat if s > 0 else beat - 1, p)
                if then and then[1] % 4 == 3:
                    total(then[0], p, then[1] // 4)

            beats(dve, stage)

        @block.tensor
        def _(pe):
            def turn_back(s, turns):
                pe.wait_ge(y_ready[s], turns)
                if s > 1:
                    pe.wait_ge(h_ready[s - 2], turns)
                for a in range(A):
                    nc.tensor.transpose(pt[s % 2][:, a * 128:(a + 1) * 128], yt[s][:, a * 128:(a + 1) * 128], r["ident"][:, :])
                for a in range(A):
                    last = nc.tensor.matmul(pw[s % 2][:, a:a + 1], yt[s][:, a * 128:(a + 1) * 128], r["w_hop"][:, :],
                                            start=True, stop=True)
                last.then_inc(back[s], 1)

            def product(s, w, src):
                nc.tensor.matmul(pz[s][:, :], r[w][:, :], src[s][:, :], start=True, stop=True).then_inc(mm_done[s], 1)

            def stage(i, beat, s):
                if not place(i, beat, s):
                    return
                turn, q = place(i, beat, s)
                if q == 0:
                    pe.wait_ge(y0_in[s], i * 16 + 16)
                    if not isinstance(i, int):
                        pe.wait_ge(y_ready[s], i)
                    product(s, "Wa", y0)
                    if not isinstance(i, int):
                        turn_back(s, i)
                elif q == 1:
                    pe.wait_ge(t_ready[s], turn * TT + 1)
                    pe.wait_ge(z0_ready[s], turn + 1)
                    product(s, "WbWa", tk[0])
                else:
                    n, k = divmod(q, 4)
                    if k == 0:
                        pe.wait_ge(u_ready[s], turn * ODE_STEPS + n)
                    else:
                        pe.wait_ge(t_ready[s], turn * TT + q)
                    pe.wait_ge(z_ready[s], turn * ZZ + q - 1)
                    product(s, "WbWa" if q < TT else "Wb", u if k == 0 else tk[k - 1])

            beats(pe, stage)
            for s in range(OSL):
                turn_back(s, OIT)

        @block.scalar
        def _(act):
            def rows(s, turns):
                act.wait_ge(back[s], turns)
                nc.scalar.activation(h[s][:, :, 0:C], pt[s % 2][:, :].rearrange("p (a c) -> p a c", a=A),
                                     ACT.Copy).then_inc(h_part[s], 1)
                act.wait_ge(h_part[s], turns)
                nc.scalar.activation(h[s][:, :, C], pw[s % 2][:, 0:A], ACT.Copy).then_inc(h_ready[s], 1)

            def stage(i, beat, s):
                if not place(i, beat, s):
                    return
                turn, q = place(i, beat, s)
                if q == 0:
                    act.wait_ge(mm_done[s], i * MM + 1)
                    nc.scalar.activation(tk[0][s][:, :], pz[s][:, :], ACT.Tanh, bias=r["tanh_bias"][:, 0:1]).then_inc(t_ready[s], 1)
                    nc.scalar.activation(z0[s][:, :], pz[s][:, :], ACT.Copy).then_inc(z0_ready[s], 1)
                    nc.scalar.activation(y0b[s][:, :], y0[s][:, :], ACT.Identity, bias=r["bo2"][:, 0:1]).then_inc(y0b_ready[s], 1)
                    if not isinstance(i, int):
                        rows(s, i)
                elif q < TT:
                    if q == TT // 2 and not isinstance(i, int):
                        act.wait_ge(stored[s], i * 16)
                    act.wait_ge(z_ready[s], turn * ZZ + q)
                    n, k = divmod(q, 4)
                    b = 2 * n + (0, 1, 1, 2)[k]
                    nc.scalar.activation(tk[k][s][:, :], (zs if k == 0 else z)[s][:, :], ACT.Tanh,
                                         bias=r["tanh_bias"][:, b:b + 1]).then_inc(t_ready[s], 1)

            beats(act, stage)
            for s in range(OSL):
                rows(s, OIT)


def hop_edges(nc, t, d, r, k):
    source, index, width = ((t["h"], d["src"], HW), (t["p1"][0:EP + 1, :], t["src_edge"], HW + 1),
                            (t["p2"][0:EP + 1, :], t["src_edge"], HW + 1))[k - 1]
    stores = 1 if k == 3 else 2
    with Phase(nc, f"h{k}") as ph:
        idx_in = ph.sems("idx_in")
        rows_in = ph.sems("rows_in")
        step = ph.sem("dve_step")
        start = ph.sem("start")
        row_ready = ph.sems("row_ready")
        stored = ph.sems("stored")
        pool_pace = ph.sem("pool_pace")
        idx = ph.sbs("idx", [128, A], I32)
        rows = ph.sbs("rows", [128, A, width])
        rc = ph.sbs("rc", [128, A])
        mean = ph.sbs("mean", [128, A, HW])
        out = ph.sbs("out", [128, A, HW + 1])
        block = ph.block()
        K = SL * (4 + 3 * (k > 1))

        @block.sync
        def _(sp):
            def load(i, s):
                sp.dma_start(idx[s][:, :], edge_columns(index, i, s)).then_inc(idx_in[s], 16)

            def store(i, s):
                lo = (k - 1) * HW
                if k < 3:
                    sp.dma_start(edge_rows(t[f"p{k}"], i, s), out[s][:, :, :]).then_inc(stored[s], 16)
                    sp.dma_start(edge_rows(t["pc"], i, s, lo, lo + HW), out[s][:, :, 0:HW]).then_inc(stored[s], 16)
                else:
                    sp.dma_start(edge_rows(t["pc"], i, s, lo, CW), out[s][:, :, :]).then_inc(stored[s], 16)

            for s in range(SL):
                load(0, s)
            with sp.Fori(0, IT - 1) as i:
                ready = sp.snap(i + 1)
                for s in range(SL):
                    sp.wait_ge(row_ready[s], ready)
                    load(i + 1, s)
                    store(i, s)
            for s in range(SL):
                sp.wait_ge(row_ready[s], IT)
                store(IT - 1, s)
            for s in range(SL):
                sp.wait_ge(stored[s], IT * 16 * stores)

        @block.gpsimd
        def _(pool):
            pace = Pace(pool, pool_pace)

            def body(i):
                for s in range(SL):
                    if not isinstance(i, int):
                        pool.wait_ge(row_ready[s], i)
                    pool.wait_ge(idx_in[s], i * 16 + 16)
                    pace.tick()
                    gather_rows(nc, rows[s], source, idx[s], rows_in[s])

            rounds(pool, body)

        @block.vector
        def _(dve):
            v_ = nc.vector
            v_.memset(out[SL - 1][:, A - 1, :], 0.0).then_inc(start, 1)
            dve.wait_ge(start, 1)

            def body(i):
                st = Steps(dve, step, i, K)
                for s in range(SL):
                    o, prev = out[s], out[(s - 1) % SL][:, A - 1, :]
                    same = edge_columns(r["same"], i, s)
                    dve.wait_ge(rows_in[s], i * 64 + 64)
                    if not isinstance(i, int):
                        dve.wait_ge(stored[s], i * 16 * stores)
                    st.done(v_.tensor_copy(o[:, :, HW], edge_columns(r["cnt"], i, s)))
                    v = rows[s]
                    if k > 1:
                        v = mean[s]
                        st.link(v_.tensor_scalar(rc[s][:, :], rows[s][:, :, HW], 1.0, None, ALU.max))
                        st.link(v_.reciprocal(rc[s][:, :], rc[s][:, :]))
                        st.link(v_.tensor_tensor(v[:, :, :], rows[s][:, :, 0:HW],
                                                 rc[s][:, :].unsqueeze(2).broadcast_to([128, A, HW]), ALU.mult))
                    for a in range(A):
                        was = prev[:, 0:HW] if a == 0 else o[:, a - 1, 0:HW]
                        ins = v_.scalar_tensor_tensor(o[:, a, 0:HW], was, same[:, a:a + 1], v[:, a, 0:HW], ALU.mult, ALU.add)
                        if a < A - 1:
                            st.link(ins)
                        else:
                            ins.then_inc(row_ready[s], 1)
                            dve.wait_ge(row_ready[s], i + 1)
                assert st.n == K, st.n

            rounds(dve, body)
            Steps(dve, start, base=1).link(v_.tensor_copy(r["tail"][:, 0:HW + 1], out[SL - 1][:, A - 1, :]))


def hop_fix(nc, t, d, r, k):
    name, width = (("p1", HW + 1), ("p2", HW + 1), ("pc", CW))[k - 1]
    with Phase(nc, f"hf{k}") as ph:
        got = ph.sem("got")
        summed = ph.sem("summed")
        step = ph.sem("dve_step")
        fixed = ph.sem("fixed")
        put = ph.sem("put")
        old = ph.sb("old", [128, width])
        pc = ph.ps("pc")
        block = ph.block()

        @block.tensor
        def _(pe):
            nc.tensor.matmul(pc[:, 0:HW + 1], r["carry"][:, :], r["tail"][:, 0:HW + 1], start=True, stop=True).then_inc(summed, 1)

        @block.gpsimd
        def _(pool):
            nc.gpsimd.indirect_dma_start(out=old[:, :], out_offset=None, in_=t[name][0:EP + 1, :],
                                         in_offset=at(r["fix_get"][:, :])).then_inc(got, 16)
            pool.wait_ge(fixed, 1)
            nc.gpsimd.indirect_dma_start(out=t[name], out_offset=at(r["fix_put"][:, :]), in_=old[:, :],
                                         in_offset=None).then_inc(put, 16)
            pool.wait_ge(put, 16)

        @block.vector
        def _(dve):
            st = Steps(dve, step)
            v_ = nc.vector
            carried = r["carried"]
            dve.wait_ge(summed, 1)
            lo = (k - 1) * HW
            st.link(v_.tensor_copy(carried[:, lo:lo + HW + 1], pc[:, 0:HW + 1]))
            dve.wait_ge(got, 16)
            part = carried[:, lo:lo + HW + 1] if k < 3 else carried[:, :]
            v_.tensor_tensor(old[:, :], old[:, :], part, ALU.add).then_inc(fixed, 1)


def hop_nodes(nc, t, d, r):
    with Phase(nc, "hn") as ph:
        own_in = ph.sems("own_in")
        x_in = ph.sems("x_in")
        idx_in = [ph.sems(f"idx_in{b}_") for b in range(2)]
        near_in = [ph.sems(f"near_in{b}_") for b in range(2)]
        step = ph.sem("dve_step")
        arg_ready = ph.sems("arg_ready")
        exp_done = ph.sems("exp_done")
        weighted = ph.sems("weighted")
        agg_done = ph.sems("agg_done")
        agg_ready = ph.sems("agg_ready")
        o_done = ph.sems("o_done")
        x1_ready = ph.sems("x1_ready")
        shift_ready = ph.sem("shift_ready")
        h2_ready = ph.sems("h2_ready")
        x1_stored = ph.sems("x1_stored")
        h2_stored = ph.sems("h2_stored")
        dve_pace = ph.sem("dve_pace")
        pool_pace = ph.sem("pool_pace")
        own = ph.sbs("own", [128, A, HW])
        x = ph.sbs("x", [128, A, C])
        near = [ph.sbs(f"near{b}_", [128, A, CW]) for b in range(2)]
        idx = [ph.sbs(f"idx{b}_", [128, A], I32) for b in range(2)]
        rc = ph.sbs("rc", [128, A])
        sc = ph.sbs("sc", [128, A, 4])
        top = ph.sbs("top", [128, A])
        arg = ph.sbs("arg", [128, A, 4])
        w = ph.sbs("w", [128, A, 4])
        agt = ph.sbs("agt", [128, G])
        x1 = ph.sbs("x1", [128, A, C])
        norms = norm_tiles(ph)
        h2 = ph.sbs("h2", [128, A, C])
        part = ph.sbs("part", [128, A, 4, C])
        pt = ph.pss("pt")
        po = ph.pss("po")
        block = ph.block()
        FIRST = 10 * SL
        K = FIRST + NORM_STEPS

        @block.sync
        def _(sp):
            def load_idx(i, b, s):
                sp.dma_start(idx[b][s][:, :], node_rows(t["last_edge"][0:NP, :], i, s)).then_inc(idx_in[b][s], 16)

            def load_own(i, s):
                sp.dma_start(own[s][:, :, :].rearrange("p a c -> p (a c)"), node_rows(t["h"], i, s)).then_inc(own_in[s], 16)

            def load_x(i, s):
                sp.dma_start(x[s][:, :, :].rearrange("p a c -> p (a c)"), node_rows(d["x"], i, s)).then_inc(x_in[s], 16)

            def store_x1(i, s):
                sp.dma_start(node_rows(t["x1"], i, s), x1[s][:, :, :].rearrange("p a c -> p (a c)")).then_inc(x1_stored[s], 16)

            def store_h2(i, s):
                sp.dma_start(node_rows(t["h2"], i, s), h2[s][:, :, :].rearrange("p a c -> p (a c)")).then_inc(h2_stored[s], 16)

            def body(i, b):
                gathered, used, before, was, earlier = (value(sp, v) for v in (landed(i - 1, 1 - b, 64), i + 1, i, i - 1, i - 2))
                for s in range(SL):
                    if later(i) and not final(i):
                        sp.wait_ge(near_in[1 - b][s], gathered)
                        load_idx(i + 1, 1 - b, s)
                for s in range(SL):
                    if later(i, 2):
                        sp.wait_ge(h2_ready[s], was)
                        store_h2(earlier, s)
                    if not final(i):
                        sp.wait_ge(weighted[s], used)
                        load_own(i + 1, s)
                    if later(i):
                        sp.wait_ge(x1_ready[s], before)
                        store_x1(was, s)
                        load_x(i, s)

            for s in range(SL):
                load_idx(0, 0, s)
                load_idx(1, 1, s)
                load_own(0, s)
                load_x(0, s)
            double_rounds(sp, body)
            for s in range(SL):
                sp.wait_ge(x1_ready[s], IT)
                store_x1(IT - 1, s)
            for i in (IT - 2, IT - 1):
                for s in range(SL):
                    sp.wait_ge(h2_ready[s], i + 1)
                    store_h2(i, s)
            for s in range(SL):
                sp.wait_ge(x1_stored[s], IT * 16)
                sp.wait_ge(h2_stored[s], IT * 16)

        @block.gpsimd
        def _(pool):
            pace = Pace(pool, pool_pace)

            def body(i, b):
                for s in range(SL):
                    pool.wait_ge(idx_in[b][s], landed(i, b, 16))
                    if later(i, 2):
                        pool.wait_ge(weighted[s], i - 1)
                    pace.tick()
                    gather_rows(nc, near[b][s], t["pc"][0:EP + 1, :], idx[b][s], near_in[b][s])

            double_rounds(pool, body)

        @block.vector
        def _(dve):
            pace = Pace(dve, dve_pace)
            v_ = nc.vector

            def residual(st, i, s):
                dve.wait_ge(o_done[s], i)
                dve.wait_ge(x_in[s], i * 16)
                v_.tensor_tensor(x1[s][:, :, :], po[s][:, :].rearrange("p (a c) -> p a c", a=A), x[s][:, :, :],
                                 ALU.add).then_inc(x1_ready[s], 1)
                dve.wait_ge(x1_ready[s], i)
                row_stats(nc, st, norms, x1[s], s)

            def body(i, b):
                st = Steps(dve, step, i, K, FIRST - K if later(i) else 0)
                for s in range(SL):
                    dve.wait_ge(own_in[s], i * 16 + 16)
                    dve.wait_ge(near_in[b][s], landed(i, b, 64))
                    st.done(v_.tensor_copy(sc[s][:, :, 0], own[s][:, :, C]))
                    st.link(v_.tensor_scalar(rc[s][:, :], near[b][s][:, :, 3 * HW], 1.0, None, ALU.max))
                    st.link(v_.reciprocal(rc[s][:, :], rc[s][:, :]))
                    dots = near[b][s][:, :, 0:3 * HW].rearrange("p a (k c) -> p a k c", k=3)[:, :, :, C]
                    rc3 = rc[s][:, :].unsqueeze(2).broadcast_to([128, A, 3])
                    st.link(v_.tensor_tensor(sc[s][:, :, 1:4], dots, rc3, ALU.mult))
                    st.link(v_.tensor_reduce(top[s][:, :], sc[s][:, :, :], AX.X, ALU.max))
                    v_.tensor_tensor(arg[s][:, :, :], sc[s][:, :, :], top[s][:, :].unsqueeze(2).broadcast_to([128, A, 4]),
                                     ALU.subtract).then_inc(arg_ready[s], 1)
                    if later(i):
                        dve.wait_ge(agg_done[s], i)
                    dve.wait_ge(exp_done[s], i + 1)
                    st.link(v_.tensor_reduce(top[s][:, :], w[s][:, :, :], AX.X, ALU.add))
                    st.link(v_.reciprocal(top[s][:, :], top[s][:, :]))
                    st.link(v_.tensor_tensor(w[s][:, :, :], w[s][:, :, :], top[s][:, :].unsqueeze(2).broadcast_to([128, A, 4]), ALU.mult))
                    st.link(v_.tensor_tensor(w[s][:, :, 1:4], w[s][:, :, 1:4],
                                             rc[s][:, :].unsqueeze(2).broadcast_to([128, A, 3]), ALU.mult))
                    hops = near[b][s][:, :, 0:3 * HW].rearrange("p a (k c) -> p a k c", k=3)[:, :, :, 0:C]
                    st.done(v_.tensor_tensor(part[s][:, :, 0, :], own[s][:, :, 0:C],
                                             w[s][:, :, 0:1].broadcast_to([128, A, C]), ALU.mult))
                    v_.tensor_tensor(part[s][:, :, 1:4, :], hops, over(w[s][:, :, 1:4], C), ALU.mult).then_inc(weighted[s], 1)
                    if later(i):
                        if later(i, 2):
                            dve.wait_ge(h2_ready[s], i - 1)
                            dve.wait_ge(x1_stored[s], (i - 1) * 16)
                        residual(st, i, s)
                if later(i):
                    row_norms(nc, st, pace, norms, shift_ready)
                assert st.n == (K if later(i) else FIRST), st.n

            double_rounds(dve, body)
            st = Steps(dve, step, IT, K, FIRST - K)
            for s in range(SL):
                dve.wait_ge(h2_ready[s], IT - 1)
                dve.wait_ge(x1_stored[s], (IT - 1) * 16)
                residual(st, IT, s)
            row_norms(nc, st, pace, norms, shift_ready)

        @block.tensor
        def _(pe):
            def output(turns, s, free):
                pe.wait_ge(agg_ready[s], turns)
                if free:
                    pe.wait_ge(x1_ready[s], turns - 1)
                for a in range(A):
                    o = po[s][:, a * 128:(a + 1) * 128]
                    nc.tensor.matmul(o, agt[s][:, a * 128:(a + 1) * 128], r["W_out"][:, :], start=True, stop=False)
                    last = nc.tensor.matmul(o, r["ones_row"][:, :], r["b_out_row"][:, :], start=False, stop=True)
                last.then_inc(o_done[s], 1)

            def body(i):
                for s in range(SL):
                    pe.wait_ge(weighted[s], i + 1)
                    if later(i):
                        pe.wait_ge(agg_ready[s], i)
                    for a in range(A):
                        for k in range(4):
                            last = nc.tensor.matmul(pt[s][:, a * 128:(a + 1) * 128], part[s][:, a, k, :], r["ident"][:, :],
                                                    start=(k == 0), stop=(k == 3))
                    last.then_inc(agg_done[s], 1)
                    if s > 0:
                        output(i + 1, s - 1, later(i))
                    elif later(i):
                        output(i, SL - 1, later(i, 2))

            late_rounds(pe, body, 2)
            output(IT, SL - 1, True)

        @block.scalar
        def _(act):
            def hidden(turns, s):
                act.wait_ge(shift_ready, turns)
                normalize(nc, norms, h2[s], x1[s], s, ACT.Relu, h2_ready[s])

            def copy_out(turns, s):
                act.wait_ge(agg_done[s], turns)
                nc.scalar.activation(agt[s][:, :], pt[s][:, :], ACT.Copy).then_inc(agg_ready[s], 1)

            def body(i):
                for s in range(SL):
                    act.wait_ge(arg_ready[s], i + 1)
                    nc.scalar.activation(w[s][:, :, :], arg[s][:, :, :], ACT.Exp).then_inc(exp_done[s], 1)
                    if s > 0:
                        copy_out(i + 1, s - 1)
                    elif later(i):
                        copy_out(i, SL - 1)
                    if later(i, 2):
                        if later(i, 3):
                            act.wait_ge(h2_stored[s], (i - 2) * 16)
                        hidden(i - 1, s)

            late_rounds(act, body, 3)
            copy_out(IT, SL - 1)
            for turns in (IT - 1, IT):
                for s in range(SL):
                    act.wait_ge(h2_stored[s], (turns - 1) * 16)
                    hidden(turns, s)


def relation_edges(nc, t, d, r):
    with Phase(nc, "re") as ph:
        idx_in = ph.sems("idx_in")
        rel_in = ph.sems("rel_in")
        rows_in = ph.sems("rows_in")
        step = ph.sem("dve_step")
        start = ph.sem("start")
        hot_ready = ph.sems("hot_ready")
        rel_done = ph.sems("rel_done")
        arg_ready = ph.sems("arg_ready")
        exp_done = ph.sems("exp_done")
        row_ready = ph.sems("row_ready")
        stored = ph.sems("stored")
        pool_pace = ph.sem("pool_pace")
        srci = ph.sbs("srci", [128, A], I32)
        dsti = ph.sbs("dsti", [128, A], I32)
        rel = ph.sbs("rel", [128, G], I32)
        hot_a = ph.sbs("hot_a", [128, G])
        hot_b = ph.sbs("hot_b", [NR - 128, G])
        hs = ph.sbs("hs", [128, A, C])
        hd = ph.sbs("hd", [128, A, C])
        comp = ph.sbs("comp", [128, A, C])
        score = ph.sbs("score", [128, A])
        base = ph.sbs("base", [128, A])
        arg = ph.sbs("arg", [128, 2, A])
        wts = ph.sbs("wts", [128, 2, A])
        out = ph.sbs("out", [128, A, LW])
        pr = ph.pss("pr")
        block = ph.block()
        K = SL * 12

        @block.sync
        def _(sp):
            def load(i, s):
                sp.dma_start(srci[s][:, :], edge_columns(d["src"], i, s)).then_inc(idx_in[s], 16)
                sp.dma_start(dsti[s][:, :], edge_columns(d["dst"], i, s)).then_inc(idx_in[s], 16)
                j = (i * SL + s) * A
                flat = d["rel_t"].rearrange("(o j) p -> o (j p)", j=A)
                o = i * SL + s
                one = flat[o:o + 1, :] if isinstance(o, int) else flat[bass.ds(o, 1), :]
                sp.dma_start(rel[s][:, :], one.broadcast_to([128, G])).then_inc(rel_in[s], 16)

            def store(i, s):
                sp.dma_start(edge_rows(t["pl"], i, s), out[s][:, :, :]).then_inc(stored[s], 16)

            for s in range(SL):
                load(0, s)
            with sp.Fori(0, IT - 1) as i:
                ready = sp.snap(i + 1)
                for s in range(SL):
                    sp.wait_ge(row_ready[s], ready)
                    load(i + 1, s)
                    store(i, s)
            for s in range(SL):
                sp.wait_ge(row_ready[s], IT)
                store(IT - 1, s)
            for s in range(SL):
                sp.wait_ge(stored[s], IT * 16)

        @block.gpsimd
        def _(pool):
            pace = Pace(pool, pool_pace)

            def body(i):
                for s in range(SL):
                    if not isinstance(i, int):
                        pool.wait_ge(row_ready[s], i)
                    pool.wait_ge(idx_in[s], i * 32 + 32)
                    pace.tick()
                    gather_rows(nc, hs[s], t["h2"], srci[s], rows_in[s])
                    gather_rows(nc, hd[s], t["h2"], dsti[s], rows_in[s])

            rounds(pool, body)

        @block.tensor
        def _(pe):
            def body(i):
                for s in range(SL):
                    pe.wait_ge(hot_ready[s], i * 2 + 2)
                    for a in range(A):
                        o, c = pr[s][:, a * 128:(a + 1) * 128], slice(a * 128, (a + 1) * 128)
                        nc.tensor.matmul(o, hot_a[s][:, c], r["rel_a"][:, :], start=True, stop=False)
                        last = nc.tensor.matmul(o, hot_b[s][:, c], r["rel_b"][:, :], start=False, stop=True)
                    last.then_inc(rel_done[s], 1)

            rounds(pe, body)

        @block.scalar
        def _(act):
            def body(i):
                for s in range(SL):
                    act.wait_ge(arg_ready[s], i + 1)
                    nc.scalar.activation(wts[s][:, :, :], arg[s][:, :, :], ACT.Exp).then_inc(exp_done[s], 1)

            rounds(act, body)

        @block.vector
        def _(dve):
            v_ = nc.vector
            v_.memset(out[SL - 1][:, A - 1, 0:C + 1], 0.0).then_inc(start, 1)
            v_.memset(out[SL - 1][:, A - 1, C + 1:LW], -BIG).then_inc(start, 1)
            dve.wait_ge(start, 2)

            def body(i):
                st = Steps(dve, step, i, K)
                for s in range(SL):
                    dve.wait_ge(rel_in[s], i * 16 + 16)
                    v_.tensor_scalar(hot_a[s][:, :], rel[s][:, :], r["pidf"][:, 0:1], None, ALU.is_equal).then_inc(hot_ready[s], 1)
                    v_.tensor_scalar(hot_b[s][:, :], rel[s][0:NR - 128, :], r["pidf"][0:NR - 128, 1:2], None,
                                     ALU.is_equal).then_inc(hot_ready[s], 1)
                for s in range(SL):
                    o, prev = out[s], out[(s - 1) % SL][:, A - 1, :]
                    m = o[:, :, C + 1]
                    fresh = edge_columns(r["fresh"], i, s)
                    dve.wait_ge(rows_in[s], i * 128 + 128)
                    dve.wait_ge(rel_done[s], i + 1)
                    if not isinstance(i, int):
                        dve.wait_ge(stored[s], i * 16)
                    st.link(v_.tensor_tensor(comp[s][:, :, :], pr[s][:, :].rearrange("p (a c) -> p a c", a=A), hs[s][:, :, :], ALU.mult))
                    st.link(v_.tensor_tensor(hd[s][:, :, :], comp[s][:, :, :], hd[s][:, :, :], ALU.mult))
                    st.link(v_.tensor_reduce(score[s][:, :], hd[s][:, :, :], AX.X, ALU.add))
                    st.link(v_.tensor_tensor_scan(m, fresh, score[s][:, :], prev[:, C + 1:LW], ALU.add, ALU.max))
                    st.done(v_.tensor_tensor(base[s][:, 0:1], prev[:, C + 1:LW], fresh[:, 0:1], ALU.add))
                    st.link(v_.tensor_tensor(base[s][:, 1:A], m[:, 0:A - 1], fresh[:, 1:A], ALU.add))
                    st.done(v_.tensor_tensor(arg[s][:, 0, :], base[s][:, :], m, ALU.subtract))
                    v_.tensor_tensor(arg[s][:, 1, :], score[s][:, :], m, ALU.subtract).then_inc(arg_ready[s], 1)
                    dve.wait_ge(exp_done[s], i + 1)
                    keep, w = wts[s][:, 0, :], wts[s][:, 1, :]
                    st.done(v_.tensor_tensor_scan(o[:, :, C], keep, w, prev[:, C:C + 1], ALU.mult, ALU.add))
                    st.link(v_.tensor_tensor(comp[s][:, :, :], comp[s][:, :, :], w.unsqueeze(2).broadcast_to([128, A, C]), ALU.mult))
                    for a in range(A):
                        was = prev[:, 0:C] if a == 0 else o[:, a - 1, 0:C]
                        ins = v_.scalar_tensor_tensor(o[:, a, 0:C], was, keep[:, a:a + 1], comp[s][:, a, :], ALU.mult, ALU.add)
                        if a < A - 1:
                            st.link(ins)
                        else:
                            ins.then_inc(row_ready[s], 1)
                            dve.wait_ge(row_ready[s], i + 1)
                assert st.n == K, st.n

            rounds(dve, body)
            Steps(dve, start, base=2).link(v_.tensor_copy(r["tail"][:, 0:LW], out[SL - 1][:, A - 1, :]))


def norm_nodes(nc, t, d, r):
    with Phase(nc, "nn") as ph:
        idx_in = ph.sems("idx_in")
        near_in = ph.sems("near_in")
        step = ph.sem("dve_step")
        divided = ph.sems("divided")
        turned = ph.sems("turned")
        nt_ready = ph.sems("nt_ready")
        h_done = ph.sems("h_done")
        stats_done = ph.sems("stats_done")
        h_ready = ph.sems("h_ready")
        stored = ph.sems("stored")
        pool_pace = ph.sem("pool_pace")
        dve_pace = ph.sem("dve_pace")
        root_ready = ph.sem("root_ready")
        var_ready = ph.sem("var_ready")
        end = ph.sem("end")
        idx = ph.sbs("idx", [128, A], I32)
        near = ph.sbs("near", [128, A, LW])
        rs = ph.sbs("rs", [128, A])
        nt = ph.sbs("nt", [128, G])
        ht = ph.sbs("ht", [128, G])
        stats = ph.sb("stats", [128, IT * SL, 6])
        mv = ph.sb("mv", [128, 2])
        m2 = ph.sb("m2", [128, 1])
        var = ph.sb("var", [128, 1])
        rstd = ph.sb("rstd", [128, 1])
        pt = ph.pss("pt")
        po = ph.pss("po")
        block = ph.block()
        K = SL

        @block.sync
        def _(sp):
            def load(i, s):
                sp.dma_start(idx[s][:, :], node_rows(t["last_edge"][0:NP, :], i, s)).then_inc(idx_in[s], 16)

            def store(i, s):
                g = i * SL + s
                o = t["ht"][g] if isinstance(g, int) else t["ht"][bass.ds(g, 1)].rearrange("o p f -> (o p) f")
                sp.dma_start(o, ht[s][:, :]).then_inc(stored[s], 16)

            for s in range(SL):
                load(0, s)
            with sp.Fori(0, IT - 1) as i:
                done = sp.snap(i + 1)
                for s in range(SL):
                    sp.wait_ge(divided[s], done)
                    load(i + 1, s)
                for s in range(SL):
                    sp.wait_ge(h_ready[s], done)
                    store(i, s)
            for s in range(SL):
                sp.wait_ge(h_ready[s], IT)
                store(IT - 1, s)
            for s in range(SL):
                sp.wait_ge(stored[s], IT * 16)

        @block.gpsimd
        def _(pool):
            pace = Pace(pool, pool_pace)

            def body(i):
                for s in range(SL):
                    pool.wait_ge(idx_in[s], i * 16 + 16)
                    if not isinstance(i, int):
                        pool.wait_ge(turned[s], i)
                    pace.tick()
                    gather_rows(nc, near[s], t["pl"][0:EP + 1, :], idx[s], near_in[s])

            rounds(pool, body)
            pool.wait_ge(var_ready, 1)
            nc.gpsimd.tensor_tensor(out=rstd[:, :], in0=var[:, :], in1=r["mhalf"][:, 0:1], op=ALU.pow).then_inc(root_ready, 1)

        @block.vector
        def _(dve):
            pace = Pace(dve, dve_pace)
            v_ = nc.vector

            def body(i):
                st = Steps(dve, step, i, K)
                for s in range(SL):
                    dve.wait_ge(near_in[s], i * 64 + 64)
                    st.link(v_.reciprocal(rs[s][:, :], near[s][:, :, C]))
                    v_.tensor_tensor(near[s][:, :, 0:C], near[s][:, :, 0:C], rs[s][:, :].unsqueeze(2).broadcast_to([128, A, C]),
                                     ALU.mult).then_inc(divided[s], 1)
                for s in range(SL):
                    dve.wait_ge(h_ready[s], i + 1)
                    pace.tick()
                    g = i * SL + s
                    o = stats[:, g, :] if isinstance(g, int) else stats[:, bass.ds(g, 1), :].rearrange("p o k -> p (o k)")
                    v_.bn_stats(o, ht[s][:, :]).then_inc(stats_done[s], 1)
                assert st.n == K, st.n

            rounds(dve, body)
            grow = NP / N
            st = Steps(dve, end)
            for s in range(SL):
                dve.wait_ge(stats_done[s], IT)
            st.link(v_.bn_aggr(mv[:, :], stats[:, :, :].rearrange("p g k -> p (g k)")))
            st.link(v_.tensor_tensor(m2[:, :], mv[:, 0:1], mv[:, 0:1], ALU.mult))
            st.link(v_.scalar_tensor_tensor(var[:, :], m2[:, :], 1.0 - grow, mv[:, 1:2], ALU.mult, ALU.add))
            v_.tensor_scalar(var[:, :], var[:, :], grow, EPS, ALU.mult, ALU.add).then_inc(var_ready, 1)
            dve.wait_ge(root_ready, 1)
            st.link(v_.tensor_tensor(r["bn_scale"][:, :], rstd[:, :], r["gamma"][:, :], ALU.mult))
            st.link(v_.scalar_tensor_tensor(m2[:, :], mv[:, 0:1], -grow, r["bn_scale"][:, :], ALU.mult, ALU.mult))
            st.link(v_.tensor_tensor(r["bn_shift"][:, :], m2[:, :], r["beta"][:, :], ALU.add))

        @block.tensor
        def _(pe):
            def body(i):
                for s in range(SL):
                    pe.wait_ge(divided[s], i + 1)
                    if not isinstance(i, int):
                        pe.wait_ge(nt_ready[s], i)
                    for a in range(A):
                        last = nc.tensor.transpose(pt[s][:, a * 128:(a + 1) * 128], near[s][:, a, 0:C], r["ident"][:, :])
                    last.then_inc(turned[s], 1)
                for s in range(SL):
                    pe.wait_ge(nt_ready[s], i + 1)
                    if not isinstance(i, int):
                        pe.wait_ge(h_ready[s], i)
                    nc.tensor.matmul(po[s][:, :], r["neigh_w"][:, :], nt[s][:, :], start=True, stop=True).then_inc(h_done[s], 1)

            rounds(pe, body)

        @block.scalar
        def _(act):
            def body(i):
                for s in range(SL):
                    act.wait_ge(turned[s], i + 1)
                    nc.scalar.activation(nt[s][:, :], pt[s][:, :], ACT.Copy).then_inc(nt_ready[s], 1)
                for s in range(SL):
                    act.wait_ge(h_done[s], i + 1)
                    if not isinstance(i, int):
                        act.wait_ge(stored[s], i * 16)
                        act.wait_ge(stats_done[s], i)
                    nc.scalar.activation(ht[s][:, :], po[s][:, :], ACT.Copy).then_inc(h_ready[s], 1)

            rounds(act, body)


def out_nodes(nc, t, d, r, out):
    with Phase(nc, "on") as ph:
        h_in = ph.sems("h_in")
        x_in = ph.sems("x_in")
        tanh_done = ph.sems("tanh_done")
        turned = ph.sems("turned")
        o_ready = ph.sems("o_ready")
        stored = ph.sems("stored")
        ht = ph.sbs("ht", [128, G])
        x1 = ph.sbs("x1", [128, G])
        th = ph.sbs("th", [128, G])
        o = ph.sbs("o", [128, G])
        pt = ph.pss("pt")
        block = ph.block()

        @block.sync
        def _(sp):
            def load(i, s):
                g = i * SL + s
                h = t["ht"][g] if isinstance(g, int) else t["ht"][bass.ds(g, 1)].rearrange("o p f -> (o p) f")
                sp.dma_start(ht[s][:, :], h).then_inc(h_in[s], 16)

            def load_x(i, s):
                sp.dma_start(x1[s][:, :], node_rows(t["x1"], i, s)).then_inc(x_in[s], 16)

            for s in range(SL):
                load(0, s)
                load_x(0, s)
            with sp.Fori(0, IT - 1) as i:
                done = sp.snap(i + 1)
                for s in range(SL):
                    sp.wait_ge(tanh_done[s], done)
                    load(i + 1, s)
                    sp.wait_ge(o_ready[s], done)
                    load_x(i + 1, s)

        @block.scalar
        def _(act):
            def body(i):
                for s in range(SL):
                    act.wait_ge(h_in[s], i * 16 + 16)
                    if not isinstance(i, int):
                        act.wait_ge(turned[s], i)
                    nc.scalar.activation(th[s][:, :], ht[s][:, :], ACT.Tanh, bias=r["bn_shift"][:, 0:1],
                                         scale=r["bn_scale"][:, 0:1]).then_inc(tanh_done[s], 1)
                for s in range(SL):
                    act.wait_ge(o_ready[s], i + 1)
                    act.dma_start(node_rows(out, i, s), o[s][:, :]).then_inc(stored[s], 16)

            rounds(act, body)
            for s in range(SL):
                act.wait_ge(stored[s], IT * 16)

        @block.tensor
        def _(pe):
            def body(i):
                for s in range(SL):
                    pe.wait_ge(tanh_done[s], i + 1)
                    if not isinstance(i, int):
                        pe.wait_ge(o_ready[s], i)
                    for a in range(A):
                        last = nc.tensor.transpose(pt[s][:, a * 128:(a + 1) * 128], th[s][:, a * 128:(a + 1) * 128], r["ident"][:, :])
                    last.then_inc(turned[s], 1)

            rounds(pe, body)

        @block.vector
        def _(dve):
            def body(i):
                for s in range(SL):
                    dve.wait_ge(turned[s], i + 1)
                    dve.wait_ge(x_in[s], i * 16 + 16)
                    if not isinstance(i, int):
                        dve.wait_ge(stored[s], i * 16)
                    nc.vector.tensor_tensor(o[s][:, :], pt[s][:, :], x1[s][:, :], ALU.add).then_inc(o_ready[s], 1)

            rounds(dve, body)


def build(nc, d, out, upto=99):
    t = {}

    def dram(name, shape, dt=F32):
        t[name] = nc.dram_tensor(f"w_{name}", shape, dt, kind="Internal").ap()

    dram("g", (NP, GW))
    dram("ed", (NP, H))
    dram("g2", (NP, GW))
    dram("ed2", (NP, H))
    dram("pg", (EP + 129, PW))
    dram("p1", (EP + 129, HW + 1))
    dram("p2", (EP + 129, HW + 1))
    dram("pc", (EP + 129, CW))
    dram("pl", (EP + 129, LW))
    dram("h", (OIT * OSL * G, HW))
    dram("x1", (NP, C))
    dram("h2", (NP, C))
    dram("ht", (IT * SL, 128, G))
    dram("y0", (OIT * OSL, 128, G))
    dram("last_edge", (NP + EP, 1), I32)
    dram("src_edge", (128, OIT * OSL * A), I32)
    dram("sidx", (128, EC), I32)
    dram("eidx", (128, EC), I32)
    with ExitStack() as stack, nc.allow_non_contiguous_dma(reason="one word for each partition"):
        r = {}

        def keep(name, shape, dt=F32):
            r[name] = stack.enter_context(nc.sbuf_tensor(f"r_{name}", shape, dt))

        for k in ("ident", "W_in", "Wa", "Wb", "WbWa", "W_out", "neigh_w", "rel_a", "carry", "carry_mask"):
            keep(k, [128, 128])
        for k in VECTORS + ("chained",):
            keep(k, [128, 1])
        for k in ("pid", "low", "spare", "dfirst", "fix_get", "fix_put"):
            keep(k, [128, 1], I32)
        keep("tail", [128, PW])
        keep("carried", [128, CW])
        keep("pidf", [128, 2])
        keep("bn_scale", [128, 1])
        keep("bn_shift", [128, 1])
        keep("W1e", [128, GW])
        keep("W2e", [128, GW])
        keep("rel_b", [NR - 128, 128])
        keep("b_out_row", [1, 128])
        keep("ones_row", [1, 128])
        keep("mhalf", [128, 1])
        keep("bias1_all", [128, GW])
        keep("bias2_all", [128, GW])
        keep("tanh_bias", [128, 2 * ODE_STEPS + 1])
        for k in ("same", "fresh", "cnt"):
            keep(k, [128, EC])
        phases(nc, t, d, r, out, upto)


def phases(nc, t, d, r, out, upto):
    setup(nc, t, d, r)
    if upto < 1:
        return
    node_in(nc, t, d, r)
    fix_index(nc, t, d, r)
    if upto < 2:
        return
    gat_edges(nc, t, d, r, "ge1", "g", "ed")
    softmax_fix(nc, t, d, r, "gf1", "pg", H, PW)
    if upto < 3:
        return
    gat_nodes(nc, t, d, r, 1)
    gat_edges(nc, t, d, r, "ge2", "g2", "ed2")
    softmax_fix(nc, t, d, r, "gf2", "pg", H, PW)
    if upto < 4:
        return
    gat_nodes(nc, t, d, r, 2)
    ode_nodes(nc, t, d, r)
    if upto < 5:
        return
    for k in (1, 2, 3):
        hop_edges(nc, t, d, r, k)
        hop_fix(nc, t, d, r, k)
    if upto < 6:
        return
    hop_nodes(nc, t, d, r)
    if upto < 7:
        return
    relation_edges(nc, t, d, r)
    softmax_fix(nc, t, d, r, "rf", "pl", 1, LW)
    if upto < 8:
        return
    norm_nodes(nc, t, d, r)
    out_nodes(nc, t, d, r, out)


NAMES = {"L0_gnn_W_in": "W_in", "L0_gnn_b_in": "b_in", "L0_gnn_W1": "W1", "L0_gnn_att1_src": "att1_src",
         "L0_gnn_att1_dst": "att1_dst", "L0_gnn_bias1": "bias1", "L0_gnn_W2": "W2", "L0_gnn_att2_src": "att2_src",
         "L0_gnn_att2_dst": "att2_dst", "L0_gnn_bias2": "bias2", "L0_gnn_g1": "g1", "L0_gnn_be1": "be1",
         "L0_gnn_g2": "g2", "L0_gnn_be2": "be2", "L0_gnn_Wo1": "Wo1", "L0_gnn_bo1": "bo1", "L0_gnn_Wo2": "Wo2",
         "L0_gnn_bo2": "bo2", "L0_gnn_w_hop": "w_hop", "L0_gnn_W_out": "W_out", "L0_gnn_b_out": "b_out",
         "L1_gnn_rel_emb": "rel_emb", "L1_gnn_neigh_w": "neigh_w", "L1_gnn_gamma": "gamma", "L1_gnn_beta": "beta"}


def lay_out(inputs):
    def edges(name, fill):
        return np.concatenate([np.asarray(inputs[name]), np.full(EP - N, fill, np.int32)]).reshape(128, EC)

    x = np.asarray(inputs["x"])
    more = np.full((128, OIT * OSL * A - EC), N, np.int32)
    arrays = {"x": np.concatenate([x, np.zeros((NP - N, C), x.dtype)]),
              "src": np.concatenate([edges("src", N), more], axis=1), "dst": edges("dst", N)}
    arrays["rel_t"] = np.ascontiguousarray(edges("edge_type_130", 0).T)
    for name, short in NAMES.items():
        arrays[short] = np.ascontiguousarray(inputs[name])
    return arrays


def kernel(**inputs):
    import concourse.bacc as _bacc
    from concourse.bass_utils import run_bass_kernel_spmd as _run

    nc = _bacc.Bacc("TRN2", target_bir_lowering=False, num_devices=1)
    arrays = {f"in_{k}": a for k, a in lay_out(inputs).items()}
    d = {k[3:]: nc.dram_tensor(k, a.shape, mybir.dt.from_np(a.dtype), kind="ExternalInput").ap()
         for k, a in arrays.items()}
    out = nc.dram_tensor("out_0", (NP, C), F32, kind="ExternalOutput").ap()
    build(nc, d, out)
    r = _run(nc, [arrays], core_ids=[0])
    return r.results[0]["out_0"][:N]
```
